# Optimizing a Trainium2 kernel written in Bass

```python
import numpy as np
import jax
import jax.numpy as jnp

def _softmax(x, axis=-1):
    return jax.nn.softmax(x, axis=axis)

def _gelu(x):
    return jax.nn.gelu(x, approximate=True)

def _silu(x):
    return jax.nn.silu(x)

def _sigmoid(x):
    return jax.nn.sigmoid(x)

def _layernorm(x, axis=-1, eps=1e-05):
    m = jnp.mean(x, axis=axis, keepdims=True)
    v = jnp.var(x, axis=axis, keepdims=True)
    return (x - m) / jnp.sqrt(v + eps)

def _scatter_add(tgt, idx, src, axis=0):
    return tgt.at[idx].add(src)

def _segment_sum(src, seg, n):
    return jax.ops.segment_sum(src, seg, n)
kernel_name = 'mk_hybrid_d1_jaxref_r4_e774d6'

def setup_inputs(seed: int=0):
    np.random.seed(seed)
    _w = jnp.asarray

    def _L0_attn_a_setup():
        import jax, jax.numpy as jnp
        import numpy as np
        EPS = 1e-06

        def rmsnorm(y, w):
            return y * jax.lax.rsqrt(jnp.mean(y * y, axis=-1, keepdims=True) + EPS) * w

        def apply_rope_cumangle(z, cum_angle):
            B, T, H, N = z.shape
            zp = z.reshape(B, T, H, N // 2, 2)
            cos = jnp.cos(cum_angle)[..., None]
            sin = jnp.sin(cum_angle)[..., None]
            z0, z1 = (zp[..., 0], zp[..., 1])
            out = jnp.stack([z0 * cos - z1 * sin, z0 * sin + z1 * cos], axis=-1)
            return out.reshape(B, T, H, N)
        key = jax.random.key(seed)
        ks = jax.random.split(key, 6)
        B, T, D = (2, 256, 256)
        H, P, N = (8, 64, 128)
        d_inner = H * P
        x = jax.random.normal(ks[0], (B, T, D), dtype=jnp.float32)
        in_proj_w = jax.random.normal(ks[1], (d_inner, D), dtype=jnp.float32) * (1.0 / np.sqrt(D))
        sel_proj_w = jax.random.normal(ks[2], (2 * H * N + 3 * H, D), dtype=jnp.float32) * (1.0 / np.sqrt(D))
        out_proj_w = jax.random.normal(ks[3], (D, d_inner), dtype=jnp.float32) * (1.0 / np.sqrt(d_inner))
        A_log = jnp.log(jnp.arange(1, H + 1, dtype=jnp.float32))
        dt_bias = jax.random.normal(ks[4], (H,), dtype=jnp.float32) * 0.5
        rms_weight = jnp.ones((d_inner,), dtype=jnp.float32)
        return {'x': x, 'in_proj_w': in_proj_w, 'sel_proj_w': sel_proj_w, 'out_proj_w': out_proj_w, 'A_log': A_log, 'dt_bias': dt_bias, 'rms_weight': rms_weight}
    _L0_attn_a_in = _L0_attn_a_setup()

    def _L0_attn_b_setup():
        import jax, jax.numpy as jnp
        import numpy as np
        from jax import lax
        D = 256
        ORDER = 2
        FILT = 64
        EMB = 3
        INNER = D * (ORDER + 1)
        DF = D * (ORDER - 1)
        L_MAX = 512

        def _pos_emb(L):
            t = jnp.linspace(0.0, 1.0, L)[:, None]
            tr = jnp.linspace(0.0, L - 1.0, L)[:, None]
            w = 2.0 * np.pi * tr / L
            f = jnp.array([0.0001], jnp.float32)[None, :]
            z = jnp.concatenate([t, jnp.cos(f * w), -jnp.sin(f * w)], axis=-1)
            return (z, t)

        def _decay(t):
            max_d = np.log(0.01) / 0.3
            min_d = np.log(0.01) / 1.5
            deltas = jnp.linspace(min_d, max_d, DF)[None, :]
            return jnp.exp(-t * jnp.abs(deltas))
        key = jax.random.key(seed)
        ks = jax.random.split(key, 16)
        s = 0.02
        return {'u': jax.random.normal(ks[0], (4, L_MAX, D), jnp.float32), 'in_w': jax.random.normal(ks[1], (D, INNER), jnp.float32) * s, 'in_b': jnp.zeros((INNER,), jnp.float32), 'short_w': jax.random.normal(ks[2], (INNER, 3), jnp.float32) * 0.3, 'short_b': jnp.zeros((INNER,), jnp.float32), 'mlp_w1': jax.random.normal(ks[3], (EMB, FILT), jnp.float32) * 0.3, 'mlp_b1': jnp.zeros((FILT,), jnp.float32), 'mlp_w2': jax.random.normal(ks[4], (FILT, FILT), jnp.float32) * 0.1, 'mlp_b2': jnp.zeros((FILT,), jnp.float32), 'mlp_w3': jax.random.normal(ks[5], (FILT, FILT), jnp.float32) * 0.1, 'mlp_b3': jnp.zeros((FILT,), jnp.float32), 'mlp_wo': jax.random.normal(ks[6], (FILT, DF), jnp.float32) * 0.1, 'freq': jnp.ones((1, FILT), jnp.float32), 'filt_bias': jax.random.normal(ks[7], (DF,), jnp.float32), 'out_w': jax.random.normal(ks[8], (D, D), jnp.float32) * s, 'out_b': jnp.zeros((D,), jnp.float32)}
    _L0_attn_b_in = _L0_attn_b_setup()

    def _L0_ffn_setup():
        import jax, jax.numpy as jnp
        import numpy as np
        DIM = 256

        def _reference_tuple_inner(x, W_r, W_k, W_v, mu_r, mu_k):
            B, T, C = x.shape
            x_prev = jnp.concatenate([jnp.zeros((B, 1, C), x.dtype), x[:, :-1, :]], axis=1)
            xr = mu_r * x + (1.0 - mu_r) * x_prev
            xk = mu_k * x + (1.0 - mu_k) * x_prev
            r = jax.nn.sigmoid(jnp.einsum('btc,dc->btd', xr, W_r))
            k = jnp.einsum('btc,dc->btd', xk, W_k)
            k_act = jnp.square(jax.nn.relu(k))
            out = r * jnp.einsum('btc,dc->btd', k_act, W_v)
            new_state = x[:, -1, :]
            return (out, new_state)
        key = jax.random.key(seed)
        ks = jax.random.split(key, 6)
        B, T, C = (8, 512, DIM)
        x = jax.random.normal(ks[0], (B, T, C), dtype=jnp.float32)
        s = 1.0 / np.sqrt(C)
        W_r = jax.random.uniform(ks[1], (C, C), jnp.float32, -s, s)
        W_k = jax.random.uniform(ks[2], (C, C), jnp.float32, -s, s)
        W_v = jax.random.uniform(ks[3], (C, C), jnp.float32, -s, s)
        mu_r = jax.random.uniform(ks[4], (C,), jnp.float32)
        mu_k = jax.random.uniform(ks[5], (C,), jnp.float32)
        return {'x': x, 'W_r': W_r, 'W_k': W_k, 'W_v': W_v, 'mu_r': mu_r, 'mu_k': mu_k}
    _L0_ffn_in = _L0_ffn_setup()
    _d = {'L0_attn_a_x': _L0_attn_a_in['x'], 'L0_attn_a_in_proj_w': _L0_attn_a_in['in_proj_w'], 'L0_attn_a_sel_proj_w': _L0_attn_a_in['sel_proj_w'], 'L0_attn_a_out_proj_w': _L0_attn_a_in['out_proj_w'], 'L0_attn_a_A_log': _L0_attn_a_in['A_log'], 'L0_attn_a_dt_bias': _L0_attn_a_in['dt_bias'], 'L0_attn_a_rms_weight': _L0_attn_a_in['rms_weight'], 'L0_attn_b_in_w': _L0_attn_b_in['in_w'], 'L0_attn_b_in_b': _L0_attn_b_in['in_b'], 'L0_attn_b_short_w': _L0_attn_b_in['short_w'], 'L0_attn_b_short_b': _L0_attn_b_in['short_b'], 'L0_attn_b_mlp_w1': _L0_attn_b_in['mlp_w1'], 'L0_attn_b_mlp_b1': _L0_attn_b_in['mlp_b1'], 'L0_attn_b_mlp_w2': _L0_attn_b_in['mlp_w2'], 'L0_attn_b_mlp_b2': _L0_attn_b_in['mlp_b2'], 'L0_attn_b_mlp_w3': _L0_attn_b_in['mlp_w3'], 'L0_attn_b_mlp_b3': _L0_attn_b_in['mlp_b3'], 'L0_attn_b_mlp_wo': _L0_attn_b_in['mlp_wo'], 'L0_attn_b_freq': _L0_attn_b_in['freq'], 'L0_attn_b_filt_bias': _L0_attn_b_in['filt_bias'], 'L0_attn_b_out_w': _L0_attn_b_in['out_w'], 'L0_attn_b_out_b': _L0_attn_b_in['out_b'], 'L0_ffn_W_r': _L0_ffn_in['W_r'], 'L0_ffn_W_k': _L0_ffn_in['W_k'], 'L0_ffn_W_v': _L0_ffn_in['W_v'], 'L0_ffn_mu_r': _L0_ffn_in['mu_r'], 'L0_ffn_mu_k': _L0_ffn_in['mu_k']}
    _x0 = _d['L0_attn_a_x']
    _d['L0_attn_a_x'] = jax.random.normal(jax.random.fold_in(jax.random.key(seed), 1), (8, 2048, 256), dtype=_x0.dtype)
    del _x0
    return _d

def reference(L0_attn_a_x, L0_attn_a_in_proj_w, L0_attn_a_sel_proj_w, L0_attn_a_out_proj_w, L0_attn_a_A_log, L0_attn_a_dt_bias, L0_attn_a_rms_weight, L0_attn_b_in_w, L0_attn_b_in_b, L0_attn_b_short_w, L0_attn_b_short_b, L0_attn_b_mlp_w1, L0_attn_b_mlp_b1, L0_attn_b_mlp_w2, L0_attn_b_mlp_b2, L0_attn_b_mlp_w3, L0_attn_b_mlp_b3, L0_attn_b_mlp_wo, L0_attn_b_freq, L0_attn_b_filt_bias, L0_attn_b_out_w, L0_attn_b_out_b, L0_ffn_W_r, L0_ffn_W_k, L0_ffn_W_v, L0_ffn_mu_r, L0_ffn_mu_k):

    def _L0_attn_a_ref(x, in_proj_w, sel_proj_w, out_proj_w, A_log, dt_bias, rms_weight):
        import jax, jax.numpy as jnp
        import numpy as np
        EPS = 1e-06

        def rmsnorm(y, w):
            return y * jax.lax.rsqrt(jnp.mean(y * y, axis=-1, keepdims=True) + EPS) * w

        def apply_rope_cumangle(z, cum_angle):
            B, T, H, N = z.shape
            zp = z.reshape(B, T, H, N // 2, 2)
            cos = jnp.cos(cum_angle)[..., None]
            sin = jnp.sin(cum_angle)[..., None]
            z0, z1 = (zp[..., 0], zp[..., 1])
            out = jnp.stack([z0 * cos - z1 * sin, z0 * sin + z1 * cos], axis=-1)
            return out.reshape(B, T, H, N)
        B, T, D = x.shape
        H = A_log.shape[0]
        d_inner = in_proj_w.shape[0]
        P = d_inner // H
        N = (sel_proj_w.shape[0] - 3 * H) // (2 * H)
        u = (x @ in_proj_w.T).reshape(B, T, H, P)
        sel = x @ sel_proj_w.T
        B_proj = sel[..., :H * N].reshape(B, T, H, N)
        C_proj = sel[..., H * N:2 * H * N].reshape(B, T, H, N)
        scal = sel[..., 2 * H * N:].reshape(B, T, 3, H)
        dt = jax.nn.softplus(scal[:, :, 0] + dt_bias)
        lam = jax.nn.sigmoid(scal[:, :, 1])
        theta = scal[:, :, 2]
        cum_angle = jnp.cumsum(dt * theta, axis=1)
        B_proj = apply_rope_cumangle(B_proj, cum_angle)
        C_proj = apply_rope_cumangle(C_proj, cum_angle)
        A_neg = -jnp.exp(A_log)

        def step(carry, inp):
            h, Bx_prev = carry
            u_t, dt_t, lam_t, Bp_t, Cp_t = inp
            alpha = jnp.exp(dt_t * A_neg)
            beta = (1.0 - lam_t) * dt_t * alpha
            gamma = lam_t * dt_t
            Bx_t = u_t[:, :, :, None] * Bp_t[:, :, None, :]
            h = alpha[:, :, None, None] * h + beta[:, :, None, None] * Bx_prev + gamma[:, :, None, None] * Bx_t
            y_t = jnp.einsum('bhpn,bhn->bhp', h, Cp_t)
            return ((h, Bx_t), y_t)
        h0 = jnp.zeros((B, H, P, N), x.dtype)
        xs = (jnp.moveaxis(u, 1, 0), jnp.moveaxis(dt, 1, 0), jnp.moveaxis(lam, 1, 0), jnp.moveaxis(B_proj, 1, 0), jnp.moveaxis(C_proj, 1, 0))
        _, ys = jax.lax.scan(step, (h0, jnp.zeros_like(h0)), xs)
        y = jnp.moveaxis(ys, 0, 1).reshape(B, T, H * P)
        y = rmsnorm(y, rms_weight)
        return y @ out_proj_w.T

    def _L0_attn_b_ref(u, in_w, in_b, short_w, short_b, mlp_w1, mlp_b1, mlp_w2, mlp_b2, mlp_w3, mlp_b3, mlp_wo, freq, filt_bias, out_w, out_b):
        import jax, jax.numpy as jnp
        import numpy as np
        from jax import lax
        D = 256
        ORDER = 2
        FILT = 64
        EMB = 3
        INNER = D * (ORDER + 1)
        DF = D * (ORDER - 1)
        L_MAX = 512

        def _pos_emb(L):
            t = jnp.linspace(0.0, 1.0, L)[:, None]
            tr = jnp.linspace(0.0, L - 1.0, L)[:, None]
            w = 2.0 * np.pi * tr / L
            f = jnp.array([0.0001], jnp.float32)[None, :]
            z = jnp.concatenate([t, jnp.cos(f * w), -jnp.sin(f * w)], axis=-1)
            return (z, t)

        def _decay(t):
            max_d = np.log(0.01) / 0.3
            min_d = np.log(0.01) / 1.5
            deltas = jnp.linspace(min_d, max_d, DF)[None, :]
            return jnp.exp(-t * jnp.abs(deltas))
        B, L, _ = u.shape
        up = jnp.einsum('bld,de->ble', u, in_w) + in_b
        up = up.transpose(0, 2, 1)
        uc = lax.conv_general_dilated(up, short_w[:, None, :], (1,), [(2, 2)], feature_group_count=INNER, dimension_numbers=('NCH', 'OIH', 'NCH'))
        uc = uc[..., :L] + short_b[None, :, None]
        x0, x1, v = (uc[:, :D], uc[:, D:2 * D], uc[:, 2 * D:])
        z, t = _pos_emb(L)
        h = jnp.sin(freq * (z @ mlp_w1 + mlp_b1))
        h = jnp.sin(freq * (h @ mlp_w2 + mlp_b2))
        h = jnp.sin(freq * (h @ mlp_w3 + mlp_b3))
        h = h @ mlp_wo
        k = (h * _decay(t)).T
        vx = v * x1
        n = 2 * L
        y = jnp.fft.irfft(jnp.fft.rfft(vx, n=n) * jnp.fft.rfft(k, n=n), n=n)[..., :L]
        v = y + vx * filt_bias[None, :, None]
        yv = (v * x0).transpose(0, 2, 1)
        return jnp.einsum('bld,de->ble', yv, out_w) + out_b

    def _L0_ffn_ref(x, W_r, W_k, W_v, mu_r, mu_k):
        import jax, jax.numpy as jnp
        import numpy as np
        DIM = 256

        def _reference_tuple_inner(x, W_r, W_k, W_v, mu_r, mu_k):
            B, T, C = x.shape
            x_prev = jnp.concatenate([jnp.zeros((B, 1, C), x.dtype), x[:, :-1, :]], axis=1)
            xr = mu_r * x + (1.0 - mu_r) * x_prev
            xk = mu_k * x + (1.0 - mu_k) * x_prev
            r = jax.nn.sigmoid(jnp.einsum('btc,dc->btd', xr, W_r))
            k = jnp.einsum('btc,dc->btd', xk, W_k)
            k_act = jnp.square(jax.nn.relu(k))
            out = r * jnp.einsum('btc,dc->btd', k_act, W_v)
            new_state = x[:, -1, :]
            return (out, new_state)
        return _reference_tuple_inner(x, W_r, W_k, W_v, mu_r, mu_k)[0]
    x = L0_attn_a_x
    x = x + _L0_attn_a_ref(_layernorm(x, axis=-1), L0_attn_a_in_proj_w, L0_attn_a_sel_proj_w, L0_attn_a_out_proj_w, L0_attn_a_A_log, L0_attn_a_dt_bias, L0_attn_a_rms_weight)
    x = x + _L0_ffn_ref(_layernorm(x, axis=-1), L0_ffn_W_r, L0_ffn_W_k, L0_ffn_W_v, L0_ffn_mu_r, L0_ffn_mu_k)
    x = x + _L0_attn_b_ref(_layernorm(x, axis=-1), L0_attn_b_in_w, L0_attn_b_in_b, L0_attn_b_short_w, L0_attn_b_short_b, L0_attn_b_mlp_w1, L0_attn_b_mlp_b1, L0_attn_b_mlp_w2, L0_attn_b_mlp_b2, L0_attn_b_mlp_w3, L0_attn_b_mlp_b3, L0_attn_b_mlp_wo, L0_attn_b_freq, L0_attn_b_filt_bias, L0_attn_b_out_w, L0_attn_b_out_b)
    x = x + _L0_ffn_ref(_layernorm(x, axis=-1), L0_ffn_W_r, L0_ffn_W_k, L0_ffn_W_v, L0_ffn_mu_r, L0_ffn_mu_k)
    return x

_drawn_inputs = setup_inputs


def setup_inputs(seed=0):
    import zlib

    import numpy as np

    out = dict(_drawn_inputs(seed))
    spreads = {'L0_attn_a_rms_weight': (1.0, 0.2),
     'L0_attn_b_in_b': (0.0, 0.427),
     'L0_attn_b_short_b': (0.0, 0.363),
     'L0_attn_b_mlp_b1': (0.0, 0.8),
     'L0_attn_b_mlp_b2': (0.0, 0.8),
     'L0_attn_b_mlp_b3': (0.0, 0.764),
     'L0_attn_b_freq': (1.0, 0.6),
     'L0_attn_b_out_b': (0.0, 2.0)}
    factors = {'L0_attn_b_in_w': 2.902,
     'L0_attn_b_short_w': 2.706,
     'L0_attn_b_mlp_w1': 3.327,
     'L0_attn_b_mlp_w2': 2.871,
     'L0_attn_b_mlp_w3': 3.106,
     'L0_attn_b_filt_bias': 8.0,
     'L0_ffn_mu_r': 15.283}
    for name, (base, spread) in spreads.items():
        noise = np.random.default_rng([zlib.crc32(name.encode()), seed]).standard_normal(out[name].shape)
        drawn = base * np.exp(spread * noise) if base else spread * noise
        out[name] = jnp.asarray(drawn.astype(out[name].dtype))
    for name, factor in factors.items():
        out[name] = (out[name] * factor).astype(out[name].dtype)
    return out
```

```python
import numpy as np
import concourse.bass as bass
from concourse import mybir
from contextlib import ExitStack

F32 = mybir.dt.float32
BF16 = mybir.dt.bfloat16
ALU = mybir.AluOpType
ACT = mybir.ActivationFunctionType

BATCH, SEQ, DIM = 8, 2048, 256
HEADS, HEAD_U, STATE = 8, 64, 128
TOK = 128
CHUNKS = SEQ // TOK
TILES = BATCH * CHUNKS
COLS = TILES * HEADS
KT = DIM // 128
GROUP = 4
INNER = 3 * DIM
FILT = 64
LN_EPS, RMS_EPS = 1e-5, 1e-6
P_COS, P_SIN, P_A, P_G, P_RHO, P_W, P_EL, P_ET, P_ALL = 0, 8, 24, 32, 40, 48, 56, 64, 72
P_EARLY = P_G
MASKED = -30000.0
ROUND = 12582912.0
TWO_PI_HI = 6.28125
TWO_PI_LO = float(2.0 * np.pi - 6.28125)
SIN_LIMIT = 3.1415925


def wait(eng, sem, value):
    if isinstance(value, int) and value <= 0:
        return
    eng.wait_ge(sem, value)


def over(ap, n):
    return ap.unsqueeze(len(ap.shape)).broadcast_to(list(ap.shape) + [n])


def normalise_tokens(nc, ctx, t):
    sb = lambda name, shape, dt=F32: ctx.enter_context(nc.sbuf_tensor(name, shape, dt))
    ps = lambda name, shape, dt=F32: ctx.enter_context(nc.psum_tensor(name, shape, dt))
    sem = lambda name: ctx.enter_context(nc.semaphore(name))
    w_scal = sb("w_scal", [128, KT, 24])
    xg = sb("xg", [128, 2, 4, DIM])
    xn = sb("xn_g", [128, 4, DIM])
    stats = sb("stats_g", [128, 4, 6])
    mean_var = sb("mean_var_g", [128, 4, 2])
    var_eps = sb("var_eps_g", [128, 4])
    rstd = sb("rstd_g", [128, 4])
    xt = sb("xt_g", [128, 4, KT, TOK])
    p_tr = [ps(f"p_tr{k}", [128, 4 * TOK]) for k in range(KT)]
    p_sc = ps("p_sc", [128, 4, 24])
    x_in = [sem(f"x_in{k}") for k in range(2)]
    w_in, consts = sem("w_in"), sem("consts")
    var_ready, rstd_ready, xn_ready = sem("var_ready"), sem("rstd_ready"), sem("xn_ready")
    transposed, xt_ready, scal_ready, scal_taken, xt_out = (
        sem("transposed"), sem("xt_ready"), sem("scal_ready"), sem("scal_taken"), sem("xt_out"))
    PAIRS = TILES // 8
    with nc.Block() as block:
        @block.sync
        def _(sp):
            sp.dma_start(w_scal[:, :, :], t["w_scal"].rearrange("(k p) n -> p k n", p=128)).then_inc(w_in, 16)

            def load(g, par):
                wait(sp, xn_ready, 2 * g + par - 1)
                sp.dma_start(xg[:, par, :, :], t["x"][bass.ds((2 * g + par) * 4 * TOK, 4 * TOK), :]
                             .rearrange("(q p) c -> p q c", p=128)).then_inc(x_in[par], 16)
            load(0, 0)
            load(0, 1)
            with sp.Fori(1, PAIRS) as g:
                load(g, 0)
                load(g, 1)

        @block.gpsimd
        def _(pool):
            g_ = nc.gpsimd
            g_.memset(t["ident"][:, :], 0.0)
            g_.memset(t["upto"][:, :], 1.0)
            g_.memset(t["after"][:, :], 1.0)
            g_.memset(t["ones"][:, :], 1.0)
            g_.memset(t["nxt"][:, :], 0.0)
            g_.memset(t["wrap"][:, :], 0.0)
            g_.memset(t["mask"][:, :], MASKED)
            g_.memset(t["minus_half"][:, :], -0.5)
            pool.drain()
            g_.affine_select(out=t["ident"][:, :], in_=t["ident"][:, :], compare_op=ALU.not_equal, fill=1.0,
                             base=0, pattern=[[-1, 128]], channel_multiplier=1)
            g_.affine_select(out=t["upto"][:, :], in_=t["upto"][:, :], compare_op=ALU.is_ge, fill=0.0,
                             base=0, pattern=[[1, 128]], channel_multiplier=-1)
            g_.affine_select(out=t["after"][:, :], in_=t["after"][:, :], compare_op=ALU.is_gt, fill=0.0,
                             base=0, pattern=[[-1, 128]], channel_multiplier=1)
            g_.affine_select(out=t["nxt"][:, :], in_=t["nxt"][:, :], compare_op=ALU.not_equal, fill=1.0,
                             base=-1, pattern=[[-1, 128]], channel_multiplier=1)
            g_.affine_select(out=t["wrap"][:, :], in_=t["wrap"][:, :], compare_op=ALU.not_equal, fill=1.0,
                             base=-127, pattern=[[1, 128]], channel_multiplier=256)
            g_.affine_select(out=t["mask"][:, :], in_=t["mask"][:, :], compare_op=ALU.is_ge, fill=0.0,
                             base=0, pattern=[[-1, 128]], channel_multiplier=1)
            pool.drain()
            g_.tensor_copy(t["ident_b"][:, :], t["ident"][:, :])
            pool.drain().then_inc(consts, 1)

            def group(g, par):
                pool.wait_ge(var_ready, 2 * g + par + 1)
                g_.tensor_tensor(rstd[:, :], var_eps[:, :], t["minus_half"][:, 0:4], ALU.pow).then_inc(rstd_ready, 1)
            with pool.Fori(0, PAIRS) as g:
                group(g, 0)
                group(g, 1)

        @block.vector
        def _(dve):
            v_ = nc.vector

            def group(g, par):
                n = 2 * g + par
                dve.wait_ge(x_in[par], 16 * g + 16)
                for q in range(4):
                    v_.bn_stats(stats[:, q, :], xg[:, par, q, :])
                dve.drain()
                for q in range(4):
                    v_.bn_aggr(mean_var[:, q, :], stats[:, q, :])
                dve.drain()
                v_.tensor_scalar(var_eps[:, :], mean_var[:, :, 1], LN_EPS, None, ALU.add).then_inc(var_ready, 1)
                dve.wait_ge(rstd_ready, n + 1)
                wait(dve, transposed, n)
                for q in range(4):
                    last = v_.tensor_scalar(xn[:, q, :], xg[:, par, q, :], mean_var[:, q, 0:1], rstd[:, q:q + 1],
                                            ALU.subtract, ALU.mult)
                last.then_inc(xn_ready, 1)
                dve.wait_ge(scal_ready, n + 1)
                v_.tensor_copy(t["scal"][:, bass.ds(n * 4, 4), :], p_sc[:, :, :]).then_inc(scal_taken, 1)
            group(0, 0)
            group(0, 1)
            with dve.Fori(1, PAIRS) as g:
                group(g, 0)
                group(g, 1)

        @block.tensor
        def _(pe):
            pe.wait_ge(consts, 1)
            pe.wait_ge(w_in, 16)

            def group(g, par):
                n = 2 * g + par
                pe.wait_ge(xn_ready, n + 1)
                wait(pe, xt_ready, n)
                for k in range(KT):
                    for q in range(4):
                        last = nc.tensor.transpose(p_tr[k][:, q * TOK:(q + 1) * TOK],
                                                   xn[:, q, k * 128:(k + 1) * 128], t["ident"][:, :])
                last.then_inc(transposed, 1)
                pe.wait_ge(xt_ready, n + 1)
                wait(pe, scal_taken, n)
                for q in range(4):
                    for k in range(KT):
                        last = nc.tensor.matmul(p_sc[:, q, :], xt[:, q, k, :], w_scal[:, k, :],
                                                start=(k == 0), stop=(k == KT - 1))
                last.then_inc(scal_ready, 1)
            group(0, 0)
            group(0, 1)
            with pe.Fori(1, PAIRS) as g:
                group(g, 0)
                group(g, 1)

        @block.scalar
        def _(act):
            def group(g, par):
                n = 2 * g + par
                act.wait_ge(transposed, n + 1)
                wait(act, scal_ready, n)
                wait(act, xt_out, 16 * n)
                for k in range(KT):
                    last = nc.scalar.copy(xt[:, :, k, :], p_tr[k][:, :].rearrange("p (q t) -> p q t", q=4))
                last.then_inc(xt_ready, 1)
                act.wait_ge(xt_ready, n + 1)
                act.dma_start(t["xnT_dram"][bass.ds(n * 4, 4)].rearrange("q p k t -> p q k t"),
                              xt[:, :, :, :]).then_inc(xt_out, 16)
            group(0, 0)
            group(0, 1)
            with act.Fori(1, PAIRS) as g:
                group(g, 0)
                group(g, 1)
            act.wait_ge(xt_out, 16 * TILES // 4)


def scan_parameters(nc, ctx, t):
    sb = lambda name, shape, dt=F32: ctx.enter_context(nc.sbuf_tensor(name, shape, dt))
    sem = lambda name: ctx.enter_context(nc.semaphore(name))
    params = sb("params_all", [128, TILES, P_ALL])
    arr = {n: sb("sp_" + n, [128, COLS]) for n in ("e1", "e2", "dt", "dth", "gam", "a", "off", "ang", "m", "m2", "r")}
    omd = sb("sp_omd", [128, COLS + HEADS])
    dt_bias = sb("dt_bias", [128, HEADS])
    a_neg = sb("a_neg", [128, HEADS])
    pp = [ctx.enter_context(nc.psum_tensor(f"p_sp{k}", [128, COLS])) for k in range(4)]
    small_in, act_done, dve_done, pe_done, out_done = (
        sem("small_in"), sem("sp_act"), sem("sp_dve"), sem("sp_pe"), sem("sp_out"))
    as3 = lambda ap: ap.rearrange("p (t h) -> p t h", h=HEADS)
    col = lambda at: params[:, :, at:at + HEADS]
    with nc.Block() as block:
        @block.sync
        def _(sp):
            sp.dma_start(dt_bias[:, :], t["dt_bias"].partition_broadcast(128)).then_inc(small_in, 16)
            sp.dma_start(a_neg[:, :], t["A_log"].partition_broadcast(128)).then_inc(small_in, 16)
            sp.wait_ge(dve_done, 6)
            sp.dma_start(t["params_dram"], params[:, :, :]).then_inc(out_done, 16)
            sp.wait_ge(out_done, 16)

        @block.vector
        def _(dve):
            v_ = nc.vector
            scal = t["scal"]
            dve.wait_ge(small_in, 32)
            v_.tensor_tensor(as3(arr["dt"][:, :]), scal[:, :, 0:8],
                             dt_bias[:, :].unsqueeze(1).broadcast_to([128, TILES, HEADS]), ALU.add)
            v_.memset(omd[:, COLS:COLS + HEADS], 0.0)
            dve.drain()
            v_.scalar_tensor_tensor(out=arr["m"][:, :], in0=arr["dt"][:, :], scalar=-1.0, in1=arr["dt"][:, :],
                                    op0=ALU.mult, op1=ALU.max).then_inc(dve_done, 1)
            dve.wait_ge(act_done, 1)
            v_.scalar_tensor_tensor(out=arr["dt"][:, :], in0=arr["dt"][:, :], scalar=0.0, in1=arr["e1"][:, :],
                                    op0=ALU.max, op1=ALU.add)
            v_.tensor_scalar(arr["e2"][:, :], arr["e2"][:, :], 1.0, None, ALU.add)
            v_.tensor_scalar(a_neg[:, :], a_neg[:, :], -1.0, None, ALU.mult)
            dve.drain()
            v_.reciprocal(arr["m2"][:, :], arr["e2"][:, :])
            v_.tensor_tensor(as3(arr["dth"][:, :]), as3(arr["dt"][:, :]), scal[:, :, 16:24], ALU.mult)
            v_.tensor_tensor(as3(arr["a"][:, :]), as3(arr["dt"][:, :]),
                             a_neg[:, :].unsqueeze(1).broadcast_to([128, TILES, HEADS]), ALU.mult)
            dve.drain()
            v_.tensor_tensor(arr["gam"][:, :], arr["m2"][:, :], arr["dt"][:, :], ALU.mult)
            v_.tensor_scalar(arr["m2"][:, :], arr["m2"][:, :], -1.0, 1.0, ALU.mult, ALU.add)
            v_.tensor_copy(col(P_A), as3(arr["a"][:, :]))
            dve.drain()
            v_.tensor_tensor(omd[:, 0:COLS], arr["m2"][:, :], arr["dt"][:, :], ALU.mult)
            dve.drain().then_inc(dve_done, 1)
            dve.wait_ge(pe_done, 1)
            off4 = arr["off"][:, :].rearrange("p (b c h) -> p b c h", b=BATCH, c=CHUNKS)
            tot4 = arr["r"][:, :].rearrange("p (b c h) -> p b c h", b=BATCH, c=CHUNKS)
            v_.memset(off4[:, :, 0, :], 0.0)
            v_.tensor_copy(arr["r"][:, :], pp[1][:, :])
            for c in range(1, CHUNKS):
                dve.drain()
                v_.tensor_tensor(off4[:, :, c, :], off4[:, :, c - 1, :], tot4[:, :, c - 1, :], ALU.add)
            dve.drain()
            v_.tensor_tensor(arr["ang"][:, :], arr["off"][:, :], pp[0][:, :], ALU.add)
            v_.tensor_tensor(arr["e1"][:, :], arr["gam"][:, :], pp[2][:, :], ALU.add)
            dve.drain().then_inc(dve_done, 1)
            v_.tensor_scalar(arr["e2"][:, :], arr["e1"][:, :], 1e-30, None, ALU.max)
            v_.tensor_copy(col(P_G), as3(arr["e1"][:, :]))
            dve.drain()
            v_.reciprocal(arr["e1"][:, :], arr["e2"][:, :])
            dve.drain()
            v_.tensor_tensor(col(P_RHO), as3(arr["gam"][:, :]), as3(arr["e1"][:, :]), ALU.mult)
            for shift, r in ((0.0, "r"), (0.25, "m")):
                m = arr["m2"]
                v_.tensor_scalar(m[:, :], arr["ang"][:, :], 1.0 / (2.0 * np.pi), shift, ALU.mult, ALU.add)
                dve.drain()
                v_.tensor_scalar(m[:, :], m[:, :], ROUND, None, ALU.add)
                dve.drain()
                v_.tensor_scalar(m[:, :], m[:, :], ROUND, None, ALU.subtract)
                dve.drain()
                v_.scalar_tensor_tensor(out=arr[r][:, :], in0=m[:, :], scalar=-TWO_PI_HI, in1=arr["ang"][:, :],
                                        op0=ALU.mult, op1=ALU.add)
                dve.drain()
                v_.scalar_tensor_tensor(out=arr[r][:, :], in0=m[:, :], scalar=-TWO_PI_LO, in1=arr[r][:, :],
                                        op0=ALU.mult, op1=ALU.add)
                dve.drain()
                if shift:
                    v_.tensor_scalar(arr[r][:, :], arr[r][:, :], 2.0 * np.pi * shift, None, ALU.add)
                    dve.drain()
                v_.tensor_scalar(arr[r][:, :], arr[r][:, :], SIN_LIMIT, -SIN_LIMIT, ALU.min, ALU.max)
                dve.drain()
            dve.drain().then_inc(dve_done, 1)
            dve.wait_ge(act_done, 2)
            pair = params[:, :, P_SIN:P_SIN + 16].rearrange("p t (h s) -> p t h s", s=2)
            v_.tensor_copy(col(P_COS), as3(arr["gam"][:, :]))
            v_.tensor_copy(pair[:, :, :, 1], as3(arr["off"][:, :]))
            v_.tensor_scalar(pair[:, :, :, 0], as3(arr["off"][:, :]), -1.0, None, ALU.mult)
            dve.drain().then_inc(dve_done, 1)
            dve.wait_ge(act_done, 3)
            by_seq = params[:, :, :].rearrange("p (b c) n -> p b c n", b=BATCH)
            v_.memset(by_seq[:, :, 0, P_EL:P_ALL], 0.0).then_inc(dve_done, 1)

        @block.scalar
        def _(act):
            s_ = nc.scalar
            act.wait_ge(dve_done, 1)
            s_.activation(arr["e1"][:, :], arr["m"][:, :], ACT.Exp, scale=-1.0)
            s_.activation(as3(arr["e2"][:, :]), t["scal"][:, :, 8:16], ACT.Exp, scale=-1.0)
            s_.activation(a_neg[:, :], a_neg[:, :], ACT.Exp)
            act.drain()
            s_.activation(arr["e1"][:, :], arr["e1"][:, :], ACT.Ln, bias=1.0)
            act.drain().then_inc(act_done, 1)
            act.wait_ge(dve_done, 4)
            s_.activation(arr["off"][:, :], arr["r"][:, :], ACT.Sin)
            s_.activation(arr["gam"][:, :], arr["m"][:, :], ACT.Sin)
            act.drain().then_inc(act_done, 1)
            act.wait_ge(pe_done, 2)
            s_.activation(col(P_EL), as3(pp[0][:, :]), ACT.Exp)
            s_.activation(col(P_W), as3(pp[1][:, :]), ACT.Exp)
            s_.activation(col(P_ET), as3(pp[3][:, :]), ACT.Exp)
            act.drain().then_inc(act_done, 1)

        @block.tensor
        def _(pe):
            pe.wait_ge(dve_done, 2)
            for half in range(2):
                c = slice(half * 512, half * 512 + 512)
                c1 = slice(half * 512 + HEADS, half * 512 + 512 + HEADS)
                nc.tensor.matmul(pp[0][:, c], t["upto"][:, :], arr["dth"][:, c], start=True, stop=True)
                nc.tensor.matmul(pp[1][:, c], t["ones"][:, :], arr["dth"][:, c], start=True, stop=True)
                nc.tensor.matmul(pp[2][:, c], t["nxt"][:, :], omd[:, c], start=True, stop=False)
                last = nc.tensor.matmul(pp[2][:, c], t["wrap"][:, :], omd[:, c1], start=False, stop=True)
            last.then_inc(pe_done, 1)
            pe.wait_ge(dve_done, 3)
            for half in range(2):
                c = slice(half * 512, half * 512 + 512)
                nc.tensor.matmul(pp[0][:, c], t["upto"][:, :], arr["a"][:, c], start=True, stop=True)
                nc.tensor.matmul(pp[1][:, c], t["after"][:, :], arr["a"][:, c], start=True, stop=True)
                last = nc.tensor.matmul(pp[3][:, c], t["ones"][:, :], arr["a"][:, c], start=True, stop=True)
            last.then_inc(pe_done, 1)


def long_filter(nc, ctx, t):
    sb = lambda name, shape, dt=F32: ctx.enter_context(nc.sbuf_tensor(name, shape, dt))
    sem = lambda name: ctx.enter_context(nc.semaphore(name))
    pos = sb("pos", [3, SEQ])
    w1, w2, w3 = sb("mlp_w1", [3, FILT]), sb("mlp_w2", [FILT, FILT]), sb("mlp_w3", [FILT, FILT])
    wo = sb("mlp_wo", [FILT, DIM])
    freq_b = sb("freq_b", [FILT, 4])
    decay = sb("decay", [128, KT, SEQ])
    h, r, m = sb("mlp_h", [FILT, SEQ]), sb("mlp_r", [FILT, SEQ]), sb("mlp_m", [FILT, SEQ])
    taps = sb("taps", [128, KT, TOK - 1 + SEQ])
    ph = ctx.enter_context(nc.psum_tensor("p_mlp", [128, SEQ]))
    f_in, f_pe, f_dve, f_act, f_out = sem("f_in"), sem("f_pe"), sem("f_dve"), sem("f_act"), sem("f_out")
    with nc.Block() as block:
        @block.sync
        def _(sp):
            loads = [(pos[:, :], t["pos"]), (w1[:, :], t["mlp_w1"]), (w2[:, :], t["mlp_w2"]), (w3[:, :], t["mlp_w3"]),
                     (wo[:, :], t["mlp_wo"]), (freq_b[:, :], t["freq_b"]),
                     (decay[:, :, :], t["decay"].rearrange("(k p) n -> p k n", p=128))]
            for dst, src in loads:
                sp.dma_start(dst, src).then_inc(f_in, 16)
            sp.wait_ge(f_dve, 5)
            sp.dma_start(t["taps_dram"].rearrange("(k p) n -> p k n", p=128), taps[:, :, :]).then_inc(f_out, 16)
            sp.wait_ge(f_out, 16)

        @block.tensor
        def _(pe):
            pe.wait_ge(f_in, 16 * 7)
            for layer, (w, src) in enumerate(((w1, pos), (w2, h), (w3, h))):
                if layer:
                    pe.wait_ge(f_act, layer)
                for q in range(4):
                    last = nc.tensor.matmul(ph[0:FILT, q * 512:(q + 1) * 512], w[:, :], src[:, q * 512:(q + 1) * 512],
                                            start=True, stop=True)
                last.then_inc(f_pe, 1)
            for k in range(KT):
                if k == 0:
                    pe.wait_ge(f_act, 3)
                else:
                    pe.wait_ge(f_dve, 4)
                for q in range(4):
                    last = nc.tensor.matmul(ph[:, q * 512:(q + 1) * 512], wo[:, k * 128:(k + 1) * 128],
                                            h[:, q * 512:(q + 1) * 512], start=True, stop=True)
                last.then_inc(f_pe, 1)

        @block.vector
        def _(dve):
            v_ = nc.vector
            v_.memset(taps[:, :, 0:TOK - 1], 0.0)
            dve.wait_ge(f_in, 16 * 7)
            for layer in range(3):
                dve.wait_ge(f_pe, layer + 1)
                v_.tensor_scalar(r[:, :], ph[0:FILT, :], freq_b[:, layer + 1:layer + 2], freq_b[:, 0:1], ALU.add, ALU.mult)
                dve.drain()
                v_.tensor_scalar(m[:, :], r[:, :], 1.0 / (2.0 * np.pi), None, ALU.mult)
                dve.drain()
                v_.tensor_scalar(m[:, :], m[:, :], ROUND, None, ALU.add)
                dve.drain()
                v_.tensor_scalar(m[:, :], m[:, :], ROUND, None, ALU.subtract)
                dve.drain()
                v_.scalar_tensor_tensor(out=r[:, :], in0=m[:, :], scalar=-TWO_PI_HI, in1=r[:, :], op0=ALU.mult, op1=ALU.add)
                dve.drain()
                v_.scalar_tensor_tensor(out=r[:, :], in0=m[:, :], scalar=-TWO_PI_LO, in1=r[:, :], op0=ALU.mult, op1=ALU.add)
                dve.drain()
                v_.tensor_scalar(r[:, :], r[:, :], SIN_LIMIT, -SIN_LIMIT, ALU.min, ALU.max)
                dve.drain().then_inc(f_dve, 1)
                dve.wait_ge(f_act, layer + 1)
            for k in range(KT):
                dve.wait_ge(f_pe, 4 + k)
                v_.tensor_tensor(taps[:, k, TOK - 1:], decay[:, k, :], ph[:, :], ALU.mult)
                dve.drain().then_inc(f_dve, 1)

        @block.scalar
        def _(act):
            for layer in range(3):
                act.wait_ge(f_dve, layer + 1)
                nc.scalar.activation(h[:, :], r[:, :], ACT.Sin).then_inc(f_act, 1)


def mixer_and_first_ffn(nc, ctx, t):
    sb = lambda name, shape, dt=F32: ctx.enter_context(nc.sbuf_tensor(name, shape, dt))
    sem = lambda name: ctx.enter_context(nc.semaphore(name))
    W4 = GROUP * STATE
    H64 = GROUP * HEAD_U
    ident, ident_b, upto, after, mask = t["ident"], t["ident_b"], t["upto"], t["after"], t["mask"]
    w_u, w_bc, w_out = sb("w_u", [128, KT, 512]), sb("w_bc", [128, KT, 2048]), sb("w_out", [128, 4, DIM])
    rms_w = sb("rms_w", [128, 4])
    in_w, in_b, short = sb("in_w", [128, KT, INNER]), sb("in_b", [128, 6]), sb("short", [128, 6, 4])
    w_r, w_k, w_v, mu = t["w_r_sb"], t["w_k_sb"], t["w_v_sb"], t["mu_sb"]
    keep = sb("keep", [128, TILES + 1])
    xnT = sb("xnT", [128, KT, TOK])
    early = sb("par_early", [128, P_EARLY])
    late = sb("par_late", [128, P_ALL - P_EARLY])
    rot1 = [sb(f"rot1_{k}", [128, W4]) for k in range(2)]
    rot2 = [sb(f"rot2_{k}", [128, W4]) for k in range(2)]
    turned = [[sb(f"turned_{g}{k}", [128, W4]) for k in range(2)] for g in range(2)]
    turned_t = [[sb(f"turned_t{g}{k}", [128, W4]) for k in range(2)] for g in range(2)]
    steps = sb("steps", [128, W4])
    decay = [sb(f"decay{g}", [128, W4]) for g in range(2)]
    mix = [sb(f"mix{g}", [128, W4]) for g in range(2)]
    u_g, u_w = sb("u_g", [128, 512]), sb("u_w", [128, 512])
    state = sb("state", [128, 512])
    y_from = sb("y_from", [128, H64])
    y = sb("y", [128, 512])
    y_sq, mean_sq, ms_eps, y_rstd = sb("y_sq", [128, 512]), sb("mean_sq", [128, 1]), sb("ms_eps", [128, 1]), sb("y_rstd", [128, 1])
    yT = sb("yT", [128, 512])
    rms_eps = sb("rms_eps", [128, 1])
    x_in, x1, xn, x2 = sb("x_in", [128, DIM]), sb("x1", [128, DIM]), sb("xn", [128, DIM]), sb("x2", [128, DIM])
    stats, mean_var, var_eps, rstd = sb("stats", [128, 6]), sb("mean_var", [128, 2]), sb("var_eps", [128, 1]), sb("rstd", [128, 1])
    xT = sb("xT", [128, KT, TOK + 1])
    dx, x_r, x_k = sb("dx", [128, KT, TOK]), sb("x_r", [128, KT, TOK]), sb("x_k", [128, KT, TOK])
    e_r, k_pos, k_sq, gate = sb("e_r", [128, DIM]), sb("k_pos", [128, 256]), sb("k_sq", [128, KT, TOK]), sb("gate", [128, DIM])
    x2T = sb("x2T", [128, KT, TOK])
    up = sb("up", [128, 6, TOK + 2])
    conv = sb("conv", [128, 6, TOK])
    vx = sb("vx", [128, KT, TOK])
    bank = [ctx.enter_context(nc.psum_tensor(f"bank{k}", [128, 512], F32)) for k in range(8)]
    p_bc, p_tr, p_arg, p_gram, p_y, p_post, p_state = bank[0:2], bank[2:4], bank[4], bank[5], bank[6], bank[7], bank[0]

    names = ("weights_in xnT_in early_in late_in x_res_in setup w_scaled bc_ready arg_ready u_ready tr_ready gram_ready y_ready "
             "state_ready rot_ready u_g_ready mix_ready y_done state_done turned_ready steps_ready u_w_ready exp_done "
             "trT_done yT_ready out_ready xnT_ready rk_ready v_ready x2nT_ready up_ready "
             "yT_done ss_done yrstd_ready var1_ready rstd1_ready xn1_done xT_done mixed exp_r_done k_done x2_done "
             "var2_ready rstd2_ready xn2_done x2T_done up_done conv_done x2_out x0_out vx_out").split()
    s = {n: sem(n) for n in names}
    heads = lambda ap: ap.rearrange("p (h n) -> p h n", h=GROUP)
    e_col = lambda at: early[:, at:at + HEADS]
    l_col = lambda at: late[:, at - P_EARLY:at - P_EARLY + HEADS]

    with nc.Block() as block:
        @block.sync
        def _(sp):
            for dst, src in (
                    (w_u[:, :, :], t["w_u"].rearrange("(k p) n -> p k n", p=128)),
                    (w_bc[:, :, :], t["w_bc"].rearrange("(k p) n -> p k n", p=128)),
                    (w_out[:, :, :], t["w_out"].rearrange("(k p) n -> p k n", p=128)),
                    (rms_w[:, :], t["rms_w"]), (in_b[:, :], t["in_b"]), (short[:, :, :], t["short"]), (mu[:, :, :], t["mu"]),
                    (in_w[:, :, :], t["in_w"].rearrange("(k p) n -> p k n", p=128)),
                    (w_r[:, :, :], t["w_r"].rearrange("(k p) n -> p k n", p=128)),
                    (w_k[:, :, :], t["w_k"].rearrange("(k p) n -> p k n", p=128)),
                    (w_v[:, :, :], t["w_v"].rearrange("(k p) n -> p k n", p=128))):
                sp.dma_start(dst, src).then_inc(s["weights_in"], 16)

            at = lambda n: n if isinstance(n, int) else sp.snap(n)
            flat = {n: t[n].rearrange(how) for n, how in (
                ("x", "r c -> (r c)"), ("x2_dram", "r c -> (r c)"), ("xnT_dram", "t p k n -> (t p k n)"),
                ("params_dram", "p t n -> p (t n)"))}
            flat |= {n: t[n].rearrange("(k p) t n -> p k (t n)", p=128) for n in ("x0T_dram", "vxT_dram")}

            def tile(i):
                block_at, early_at, late_at = at(i * (TOK * DIM)), at(i * P_ALL), at(i * P_ALL + P_EARLY)
                four = at(4 * i)
                wait(sp, s["bc_ready"], four)
                wait(sp, s["u_ready"], i)
                sp.dma_start(xnT[:, :, :], flat["xnT_dram"][bass.ds(block_at, TOK * DIM)]
                             .rearrange("(p k n) -> p k n", p=128, k=KT)).then_inc(s["xnT_in"], 16)
                wait(sp, s["turned_ready"], four)
                sp.dma_start(early[:, :], flat["params_dram"][:, bass.ds(early_at, P_EARLY)]).then_inc(s["early_in"], 16)
                wait(sp, s["state_done"], i)
                sp.dma_start(late[:, :], flat["params_dram"][:, bass.ds(late_at, P_ALL - P_EARLY)]).then_inc(s["late_in"], 16)

            def post(j):
                block_at, tok_at, this, nxt = at(j * (TOK * DIM)), at(j * TOK), at(j), at(j + 1)
                wait(sp, s["xn1_done"], this)
                sp.dma_start(x_in[:, :], flat["x"][bass.ds(block_at, TOK * DIM)].rearrange("(p c) -> p c", p=TOK)).then_inc(s["x_res_in"], 16)
                sp.wait_ge(s["x2_done"], nxt)
                sp.dma_start(flat["x2_dram"][bass.ds(block_at, TOK * DIM)].rearrange("(p c) -> p c", p=TOK), x2[:, :]).then_inc(s["x2_out"], 16)
                sp.wait_ge(s["conv_done"], nxt)
                sp.dma_start(flat["x0T_dram"][:, :, bass.ds(tok_at, TOK)], conv[:, 0:KT, :]).then_inc(s["x0_out"], 16)
                sp.dma_start(flat["vxT_dram"][:, :, bass.ds(tok_at, TOK)], vx[:, :, :]).then_inc(s["vx_out"], 16)

            tile(0)
            tile(1)
            post(0)
            with sp.Fori(2, TILES) as i:
                tile(i)
                post(i - 1)
            post(TILES - 1)
            sp.wait_ge(s["x2_out"], 16 * TILES)
            sp.wait_ge(s["x0_out"], 16 * TILES)
            sp.wait_ge(s["vx_out"], 16 * TILES)

        @block.tensor
        def _(pe):
            mm, tp = nc.tensor.matmul, nc.tensor.transpose
            pe.wait_ge(s["weights_in"], 16 * 11)
            pe.wait_ge(s["setup"], 1)
            pe.wait_ge(s["w_scaled"], 1)

            def project_bc(i, g):
                if g == 0:
                    pe.wait_ge(s["xnT_in"], 16 * i + 16)
                    wait(pe, s["state_done"], i)
                else:
                    pe.wait_ge(s["rot_ready"], 4 * i + 2)
                for c in range(2):
                    for k in range(KT):
                        last = mm(p_bc[c][:, :], xnT[:, k, :], w_bc[:, k, c * 1024 + g * W4:c * 1024 + (g + 1) * W4],
                                  start=(k == 0), stop=(k == KT - 1))
                    last.then_inc(s["bc_ready"], 1)

            def decay_logs(i, g):
                pe.wait_ge(s["steps_ready"], 2 * i + g + 1)
                wait(pe, s["exp_done"], 2 * i + g)
                mm(p_arg[:, :], after[:, :], steps[:, :], start=True, stop=False)
                mm(p_arg[:, :], ident_b[:, :], mask[:, :].unsqueeze(1).broadcast_to([128, GROUP, TOK]),
                   start=False, stop=True).then_inc(s["arg_ready"], 1)

            def project_u(i):
                wait(pe, s["mix_ready"], 2 * i)
                for k in range(KT):
                    last = mm(p_gram[:, :], xnT[:, k, :], w_u[:, k, :], start=(k == 0), stop=(k == KT - 1))
                last.then_inc(s["u_ready"], 1)

            def turn_over(i, g):
                for c in range(2):
                    pe.wait_ge(s["turned_ready"], 4 * i + 2 * g + c + 1)
                    wait(pe, s["trT_done"], 4 * i + 2 * g + c - 1)
                    for h in range(GROUP):
                        last = tp(p_tr[c][:, h * TOK:(h + 1) * TOK], turned[g][c][:, h * STATE:(h + 1) * STATE], ident[:, :])
                    last.then_inc(s["tr_ready"], 1)

            def gram(i, g):
                pe.wait_ge(s["trT_done"], 4 * i + 2 * g + 2)
                if g == 0:
                    pe.wait_ge(s["u_g_ready"], i + 1)
                else:
                    pe.wait_ge(s["mix_ready"], 2 * i + 1)
                for h in range(GROUP):
                    c = slice(h * TOK, (h + 1) * TOK)
                    last = mm(p_gram[:, c], turned_t[g][0][:, c], turned_t[g][1][:, c], start=True, stop=True)
                last.then_inc(s["gram_ready"], 1)

            def outputs(i, g):
                pe.wait_ge(s["mix_ready"], 2 * i + g + 1)
                wait(pe, s["y_done"], 2 * i + g)
                wait(pe, s["state_done"], i)
                for h in range(GROUP):
                    v, r = slice((g * GROUP + h) * HEAD_U, (g * GROUP + h + 1) * HEAD_U), slice(h * TOK, (h + 1) * TOK)
                    mm(p_y[:, h * HEAD_U:(h + 1) * HEAD_U], mix[g][:, r], u_g[:, v], start=True, stop=True)
                    last = mm(p_y[:, H64 + h * HEAD_U:H64 + (h + 1) * HEAD_U], turned_t[g][1][:, r], state[:, v],
                              start=True, stop=True)
                last.then_inc(s["y_ready"], 1)

            def new_state(i):
                pe.wait_ge(s["u_w_ready"], i + 1)
                pe.wait_ge(s["rot_ready"], 4 * i + 4)
                for h in range(HEADS):
                    v = slice(h * HEAD_U, (h + 1) * HEAD_U)
                    last = mm(p_state[:, v], turned[h // GROUP][0][:, (h % GROUP) * STATE:(h % GROUP + 1) * STATE], u_w[:, v],
                              start=True, stop=True)
                last.then_inc(s["state_ready"], 1)

            def y_over(j):
                pe.wait_ge(s["y_done"], 2 * j + 2)
                wait(pe, s["up_done"], 2 * j)
                for k in range(4):
                    last = tp(p_post[:, k * TOK:(k + 1) * TOK], y[:, k * 128:(k + 1) * 128], ident[:, :])
                last.then_inc(s["yT_ready"], 1)

            def project_out(j):
                pe.wait_ge(s["yT_done"], j + 1)
                for k in range(4):
                    last = mm(p_post[:, 0:DIM], yT[:, k * TOK:(k + 1) * TOK], w_out[:, k, :], start=(k == 0), stop=(k == 3))
                last.then_inc(s["out_ready"], 1)

            def xn_over(j):
                pe.wait_ge(s["xn1_done"], j + 1)
                for k in range(KT):
                    last = tp(p_post[:, k * TOK:(k + 1) * TOK], xn[:, k * 128:(k + 1) * 128], ident[:, :])
                last.then_inc(s["xnT_ready"], 1)

            def receptance_key(j):
                pe.wait_ge(s["mixed"], j + 1)
                for k in range(KT):
                    mm(p_post[:, 0:DIM], x_r[:, k, :], w_r[:, k, :], start=(k == 0), stop=(k == KT - 1))
                for e in range(KT):
                    for k in range(KT):
                        last = mm(p_post[:, DIM + e * TOK:DIM + (e + 1) * TOK], w_k[:, k, e * 128:(e + 1) * 128], x_k[:, k, :],
                                  start=(k == 0), stop=(k == KT - 1))
                last.then_inc(s["rk_ready"], 1)

            def value(j):
                pe.wait_ge(s["k_done"], j + 1)
                for k in range(KT):
                    last = mm(p_post[:, 0:DIM], k_sq[:, k, :], w_v[:, k, :], start=(k == 0), stop=(k == KT - 1))
                last.then_inc(s["v_ready"], 1)

            def x2n_over(j):
                pe.wait_ge(s["xn2_done"], j + 1)
                for k in range(KT):
                    last = tp(p_post[:, k * TOK:(k + 1) * TOK], xn[:, k * 128:(k + 1) * 128], ident[:, :])
                last.then_inc(s["x2nT_ready"], 1)

            def widen(j, part):
                if part == 0:
                    pe.wait_ge(s["x2T_done"], j + 1)
                else:
                    pe.wait_ge(s["up_done"], 2 * j + 1)
                for e in range(4 * part, min(4 * part + 4, 6)):
                    for k in range(KT):
                        last = mm(p_post[:, (e % 4) * TOK:(e % 4 + 1) * TOK], in_w[:, k, e * 128:(e + 1) * 128], x2T[:, k, :],
                                  start=(k == 0), stop=(k == KT - 1))
                last.then_inc(s["up_ready"], 1)

            def body(i, tile=True, before=True):
                j = i - 1
                if tile: project_bc(i, 0)
                if tile: decay_logs(i, 0)
                if before: y_over(j)
                if tile: project_u(i)
                if before: project_out(j)
                if tile:
                    project_bc(i, 1)
                    turn_over(i, 0)
                    decay_logs(i, 1)
                if before: xn_over(j)
                if tile: gram(i, 0)
                if before: receptance_key(j)
                if tile: turn_over(i, 1)
                if before: value(j)
                if tile:
                    outputs(i, 0)
                    gram(i, 1)
                if before: x2n_over(j)
                if tile: new_state(i)
                if before: widen(j, 0)
                if tile: outputs(i, 1)
                if before: widen(j, 1)
            body(0, before=False)
            body(1)
            with pe.Fori(2, TILES) as i:
                body(i)
            body(TILES, tile=False)

        @block.scalar
        def _(act):
            s_ = nc.scalar

            def exponentials(i, g):
                act.wait_ge(s["arg_ready"], 2 * i + g + 1)
                wait(act, s["mix_ready"], 2 * i + g - 1)
                s_.activation(decay[g][:, :], p_arg[:, :], ACT.Exp).then_inc(s["exp_done"], 1)

            def copy_turned(i, g):
                for c in range(2):
                    act.wait_ge(s["tr_ready"], 4 * i + 2 * g + c + 1)
                    if c == 0:
                        wait(act, s["gram_ready"], 2 * i + g - 1)
                    else:
                        wait(act, s["y_ready"], 2 * i + g - 1)
                    s_.copy(turned_t[g][c][:, :], p_tr[c][:, :]).then_inc(s["trT_done"], 1)

            def square_y(j):
                act.wait_ge(s["y_done"], 2 * j + 2)
                wait(act, s["yrstd_ready"], j)
                s_.activation(y_sq[:, :], y[:, :], ACT.Square, scale=float((HEADS * HEAD_U) ** -0.5),
                              accum_out=mean_sq[:, :]).then_inc(s["ss_done"], 1)

            def copy_yT(j):
                act.wait_ge(s["yT_ready"], j + 1)
                wait(act, s["out_ready"], j)
                s_.copy(yT[:, :], p_post[:, :]).then_inc(s["yT_done"], 1)

            def copy_xT(j):
                act.wait_ge(s["xnT_ready"], j + 1)
                s_.copy(xT[:, :, 1:TOK + 1], p_post[:, 0:DIM].rearrange("p (k n) -> p k n", k=KT)).then_inc(s["xT_done"], 1)

            def r_and_k(j):
                act.wait_ge(s["rk_ready"], j + 1)
                wait(act, s["x2_done"], j)
                s_.activation(e_r[:, :], p_post[:, 0:DIM], ACT.Exp, scale=-1.0).then_inc(s["exp_r_done"], 1)
                wait(act, s["v_ready"], j)
                s_.activation(k_pos[:, :], p_post[:, DIM:512], ACT.Relu)
                act.drain()
                s_.activation(k_sq[:, :, :], k_pos[:, :].rearrange("p (k n) -> p k n", k=KT), ACT.Square).then_inc(s["k_done"], 1)

            def copy_x2T(j):
                act.wait_ge(s["x2nT_ready"], j + 1)
                wait(act, s["up_ready"], 2 * j)
                s_.copy(x2T[:, :, :], p_post[:, 0:DIM].rearrange("p (k n) -> p k n", k=KT)).then_inc(s["x2T_done"], 1)

            def add_up_bias(j, part):
                act.wait_ge(s["up_ready"], 2 * j + part + 1)
                for e in range(4 * part, min(4 * part + 4, 6)):
                    last = s_.activation(up[:, e, 2:TOK + 2], p_post[:, (e % 4) * TOK:(e % 4 + 1) * TOK], ACT.Identity,
                                         bias=in_b[:, e:e + 1])
                last.then_inc(s["up_done"], 1)

            act.wait_ge(s["weights_in"], 16 * 11)

            def body(i, tile=True, before=True):
                j = i - 1
                if before: square_y(j)
                if tile: exponentials(i, 0)
                if before: copy_yT(j)
                if tile:
                    copy_turned(i, 0)
                    exponentials(i, 1)
                if before:
                    copy_xT(j)
                    r_and_k(j)
                if tile: copy_turned(i, 1)
                if before:
                    copy_x2T(j)
                    add_up_bias(j, 0)
                    add_up_bias(j, 1)
            body(0, before=False)
            body(1)
            with act.Fori(2, TILES) as i:
                body(i)
            body(TILES, tile=False)

        @block.gpsimd
        def _(pool):
            g_ = nc.gpsimd
            g_.memset(state[:, :], 0.0)
            g_.memset(xT[:, :, :], 0.0)
            g_.memset(up[:, :, :], 0.0)
            g_.memset(keep[:, :], 1.0)
            g_.memset(rms_eps[:, :], RMS_EPS)
            pool.drain()
            g_.memset(keep[:, 0:TILES].rearrange("p (b c) -> p b c", b=BATCH)[:, :, 0], 0.0)
            pool.drain().then_inc(s["setup"], 1)
            pool.wait_ge(s["weights_in"], 16 * 11)
            for k in range(4):
                last = g_.tensor_scalar(w_out[:, k, :], w_out[:, k, :], rms_w[:, k:k + 1], None, ALU.mult)
            last.then_inc(s["w_scaled"], 1)

            def masked_steps(i, g):
                if g == 0:
                    pool.wait_ge(s["early_in"], 16 * i + 16)
                wait(pool, s["arg_ready"], 2 * i + g)
                g_.tensor_tensor(heads(steps[:, :]), upto[:, :].unsqueeze(1).broadcast_to([128, GROUP, TOK]),
                                 over(e_col(P_A)[:, g * GROUP:(g + 1) * GROUP], TOK), ALU.mult).then_inc(s["steps_ready"], 1)

            def add_turned(i, g, c):
                pool.wait_ge(s["rot_ready"], 4 * i + 2 * g + c + 1)
                wait(pool, s["tr_ready"], 4 * i + 2 * g + c - 3)
                if c == 0:
                    wait(pool, s["state_ready"], i)
                g_.tensor_tensor(turned[g][c][:, :], rot1[c][:, :], rot2[c][:, :], ALU.add).then_inc(s["turned_ready"], 1)

            def decay_values(i):
                pool.wait_ge(s["u_g_ready"], i + 1)
                wait(pool, s["state_ready"], i)
                g_.tensor_tensor(u_w[:, :].rearrange("p (h n) -> p h n", h=HEADS), u_g[:, :].rearrange("p (h n) -> p h n", h=HEADS),
                                 over(l_col(P_W), HEAD_U), ALU.mult).then_inc(s["u_w_ready"], 1)

            def scan_rstd(j):
                pool.wait_ge(s["ss_done"], j + 1)
                wait(pool, s["xn1_done"], j)
                g_.tensor_tensor(ms_eps[:, :], mean_sq[:, :], rms_eps[:, :], ALU.add)
                pool.drain()
                g_.tensor_tensor(y_rstd[:, :], ms_eps[:, :], t["minus_half"][:, 0:1], ALU.pow).then_inc(s["yrstd_ready"], 1)

            def layer_rstd(j, n):
                pool.wait_ge(s[f"var{n}_ready"], j + 1)
                g_.tensor_tensor(rstd[:, :], var_eps[:, :], t["minus_half"][:, 0:1], ALU.pow).then_inc(s[f"rstd{n}_ready"], 1)

            def body(i, tile=True, before=True):
                j = i - 1
                if tile: masked_steps(i, 0)
                if before: scan_rstd(j)
                if tile:
                    add_turned(i, 0, 0)
                    add_turned(i, 0, 1)
                    masked_steps(i, 1)
                if before: layer_rstd(j, 1)
                if tile:
                    decay_values(i)
                    add_turned(i, 1, 0)
                    add_turned(i, 1, 1)
                if before: layer_rstd(j, 2)
            body(0, before=False)
            body(1)
            with pool.Fori(2, TILES) as i:
                body(i)
            body(TILES, tile=False)

        @block.vector
        def _(dve):
            v_ = nc.vector

            def rotate(i, g):
                if g == 0:
                    dve.wait_ge(s["early_in"], 16 * i + 16)
                cos = over(e_col(P_COS)[:, g * GROUP:(g + 1) * GROUP], STATE)
                sin = early[:, P_SIN + 2 * g * GROUP:P_SIN + 2 * (g + 1) * GROUP]
                for c in range(2):
                    dve.wait_ge(s["bc_ready"], 4 * i + 2 * g + c + 1)
                    wait(dve, s["turned_ready"], 4 * i + 2 * g + c - 1)
                    v_.tensor_tensor(heads(rot1[c][:, :]), heads(p_bc[c][:, :]), cos, ALU.mult)
                    parts = lambda ap: ap.rearrange("p (h s n) -> p h s n", h=GROUP, s=2)
                    v_.tensor_tensor(parts(rot2[c][:, :]), parts(p_bc[c][:, :])[:, :, ::-1, :],
                                     over(sin.rearrange("p (h s) -> p h s", s=2), STATE // 2), ALU.mult).then_inc(s["rot_ready"], 1)

            def gate_values(i):
                dve.wait_ge(s["u_ready"], i + 1)
                dve.wait_ge(s["late_in"], 16 * i + 16)
                wait(dve, s["u_w_ready"], i)
                wait(dve, s["y_ready"], 2 * i)
                v_.tensor_tensor(u_g[:, :].rearrange("p (h n) -> p h n", h=HEADS), p_gram[:, :].rearrange("p (h n) -> p h n", h=HEADS),
                                 over(l_col(P_G), HEAD_U), ALU.mult).then_inc(s["u_g_ready"], 1)

            def decay_diagonal(i, g):
                dve.wait_ge(s["exp_done"], 2 * i + g + 1)
                for h in range(GROUP):
                    c = slice(h * TOK, (h + 1) * TOK)
                    at = P_RHO - P_EARLY + g * GROUP + h
                    v_.scalar_tensor_tensor(out=decay[g][:, c], in0=ident[:, :], scalar=late[:, at:at + 1],
                                            in1=decay[g][:, c], op0=ALU.mult, op1=ALU.add)

            def weigh_gram(i, g):
                dve.wait_ge(s["gram_ready"], 2 * i + g + 1)
                v_.tensor_tensor(mix[g][:, :], p_gram[:, :], decay[g][:, :], ALU.mult).then_inc(s["mix_ready"], 1)

            def take_y(i, g):
                dve.wait_ge(s["y_ready"], 2 * i + g + 1)
                if g == 0:
                    wait(dve, s["yT_ready"], i)
                    wait(dve, s["ss_done"], i)
                v_.tensor_tensor(heads(y_from[:, :]), heads(p_y[:, H64:]), over(l_col(P_EL)[:, g * GROUP:(g + 1) * GROUP], HEAD_U), ALU.mult)
                dve.drain()
                v_.tensor_tensor(y[:, g * H64:(g + 1) * H64], p_y[:, 0:H64], y_from[:, :], ALU.add).then_inc(s["y_done"], 1)

            def carry_state(i):
                dve.wait_ge(s["y_ready"], 2 * i + 2)
                st = state[:, :].rearrange("p (h n) -> p h n", h=HEADS)
                v_.tensor_tensor(st, st, over(l_col(P_ET), HEAD_U), ALU.mult)
                dve.drain()
                dve.wait_ge(s["state_ready"], i + 1)
                v_.tensor_tensor(state[:, :], p_state[:, :], state[:, :], ALU.add).then_inc(s["state_done"], 1)

            def norm(j, src, n):
                v_.bn_stats(stats[:, :], src)
                dve.drain()
                v_.bn_aggr(mean_var[:, :], stats[:, :])
                dve.drain()
                v_.tensor_scalar(var_eps[:, :], mean_var[:, 1:2], LN_EPS, None, ALU.add).then_inc(s[f"var{n}_ready"], 1)

            def normalised(j, src, n):
                dve.wait_ge(s[f"rstd{n}_ready"], j + 1)
                v_.tensor_scalar(xn[:, :], src, mean_var[:, 0:1], rstd[:, :], ALU.subtract, ALU.mult).then_inc(s[f"xn{n}_done"], 1)

            def residual1(j):
                dve.wait_ge(s["out_ready"], j + 1)
                dve.wait_ge(s["yrstd_ready"], j + 1)
                dve.wait_ge(s["x_res_in"], 16 * j + 16)
                v_.scalar_tensor_tensor(out=x1[:, :], in0=p_post[:, 0:DIM], scalar=y_rstd[:, :], in1=x_in[:, :],
                                        op0=ALU.mult, op1=ALU.add)
                v_.tensor_scalar(xT[:, :, 0], xT[:, :, TOK], keep[:, bass.ds(j, 1)], None, ALU.mult)
                dve.drain()
                norm(j, x1[:, :], 1)

            def shift_mix(j):
                dve.wait_ge(s["xT_done"], j + 1)
                v_.tensor_tensor(dx[:, :, :], xT[:, :, 1:TOK + 1], xT[:, :, 0:TOK], ALU.subtract)
                dve.drain()
                for k in range(KT):
                    for which, dst in enumerate((x_r, x_k)):
                        last = v_.scalar_tensor_tensor(out=dst[:, k, :], in0=dx[:, k, :], scalar=mu[:, which, k:k + 1],
                                                       in1=xT[:, k, 0:TOK], op0=ALU.mult, op1=ALU.add)
                last.then_inc(s["mixed"], 1)

            def sigmoid(j):
                dve.wait_ge(s["exp_r_done"], j + 1)
                v_.tensor_scalar(gate[:, :], e_r[:, :], 1.0, None, ALU.add)
                dve.drain()
                v_.reciprocal(gate[:, :], gate[:, :])

            def residual2(j):
                dve.wait_ge(s["v_ready"], j + 1)
                wait(dve, s["x2_out"], 16 * j)
                v_.tensor_tensor(gate[:, :], gate[:, :], p_post[:, 0:DIM], ALU.mult)
                v_.tensor_scalar(up[:, :, 0:2], up[:, :, TOK:TOK + 2], keep[:, bass.ds(j, 1)], None, ALU.mult)
                dve.drain()
                v_.tensor_tensor(x2[:, :], gate[:, :], x1[:, :], ALU.add)
                dve.drain().then_inc(s["x2_done"], 1)
                norm(j, x2[:, :], 2)

            def short_filter(j):
                dve.wait_ge(s["up_done"], 2 * j + 2)
                wait(dve, s["x0_out"], 16 * j)
                wait(dve, s["vx_out"], 16 * j)
                for e in range(6):
                    v_.tensor_scalar(conv[:, e, :], up[:, e, 2:TOK + 2], short[:, e, 2:3], short[:, e, 3:4], ALU.mult, ALU.add)
                for tap in (1, 0):
                    dve.drain()
                    for e in range(6):
                        v_.scalar_tensor_tensor(out=conv[:, e, :], in0=up[:, e, tap:TOK + tap], scalar=short[:, e, tap:tap + 1],
                                                in1=conv[:, e, :], op0=ALU.mult, op1=ALU.add)
                dve.drain()
                v_.tensor_tensor(vx[:, :, ::-1], conv[:, 4:6, :], conv[:, 2:4, :], ALU.mult).then_inc(s["conv_done"], 1)

            dve.wait_ge(s["weights_in"], 16 * 11)
            dve.wait_ge(s["setup"], 1)

            def body(i, tile=True, before=True):
                j = i - 1
                if tile:
                    rotate(i, 0)
                    gate_values(i)
                if before:
                    residual1(j)
                if tile: rotate(i, 1)
                if before: normalised(j, x1[:, :], 1)
                if tile: decay_diagonal(i, 0)
                if before: shift_mix(j)
                if tile:
                    dve.drain()
                    weigh_gram(i, 0)
                    decay_diagonal(i, 1)
                if before:
                    sigmoid(j)
                    dve.drain()
                    residual2(j)
                    normalised(j, x2[:, :], 2)
                if tile:
                    take_y(i, 0)
                    weigh_gram(i, 1)
                    take_y(i, 1)
                    carry_state(i)
                if before: short_filter(j)
            body(0, before=False)
            body(1)
            with dve.Fori(2, TILES) as i:
                body(i)
            body(TILES, tile=False)


def long_convolution(nc, ctx, t):
    sb = lambda name, shape, dt=F32: ctx.enter_context(nc.sbuf_tensor(name, shape, dt))
    sem = lambda name: ctx.enter_context(nc.semaphore(name))
    U = 4
    ident = t["ident"]
    skip = sb("skip", [128, DIM])
    toep = [sb(f"toep{u}", [128, SEQ]) for u in range(U)]
    vt = [sb(f"vt{p}", [128, U, TOK]) for p in range(2)]
    x0t = [sb(f"x0t{p}", [128, U, TOK]) for p in range(2)]
    sig = [sb(f"sig{p}", [128, TILES]) for p in range(2)]
    skipped = [sb(f"skipped{p}", [128, TOK]) for p in range(2)]
    ys = [sb(f"ys{p}", [128, TILES]) for p in range(2)]
    yv = [sb(f"yv{p}", [128, U, TOK]) for p in range(2)]
    pst = lambda name: ctx.enter_context(nc.psum_tensor(name, [128, 512], F32))
    p_sig, p_y, p_back = [pst(f"p_sig{p}") for p in range(2)], [pst(f"p_yc{p}") for p in range(2)], [pst(f"p_back{p}") for p in range(2)]
    skip_in = sem("skip_in")
    toep_in = [sem(f"toep_in{u}") for u in range(U)]
    vt_in, x0t_in, yv_out = [sem(f"vt_in{p}") for p in range(2)], [sem(f"x0t_in{p}") for p in range(2)], [sem(f"yv_out{p}") for p in range(2)]
    sig_over, sig_ready, conv_ready, ys_ready, back_ready, yv_ready = (
        sem("sig_over"), sem("sig_ready"), sem("conv_ready"), sem("ys_ready"), sem("back_ready"), sem("yv_ready"))
    by_seq = lambda ap: ap.rearrange("p (b c) -> p b c", b=BATCH)
    ROW = TOK - 1 + SEQ
    ITERS = DIM // (2 * U)
    taps = t["taps_dram"].rearrange("d n -> (d n)")

    with nc.Block() as block:
        @block.sync
        def _(sp):
            at = lambda n: n if isinstance(n, int) else sp.snap(n)
            sp.dma_start(skip[:, :], t["filt_bias"].partition_broadcast(128)).then_inc(skip_in, 16)

            def quad(it, q):
                n0 = 2 * U * it + U * q
                offs = [at((n0 + u) * ROW) for u in range(U)]
                frees = [at(n0 + u - U + 1) for u in range(U)]
                for u in range(U):
                    wait(sp, conv_ready, frees[u])
                    src = taps[bass.ds(offs[u], ROW)]
                    rows = bass.AP(src.tensor, src.offset, [[1, 128], [1, SEQ]])
                    sp.dma_start(toep[u][:, :], rows).then_inc(toep_in[u], 16)
            quad(0, 0)
            quad(0, 1)
            with sp.Fori(1, ITERS) as it:
                quad(it, 0)
                quad(it, 1)

        @block.scalar
        def _(act):
            at = lambda n: n if isinstance(n, int) else act.snap(n)
            flat = {n: t[n].rearrange("c t n -> (c t n)") for n in ("vxT_dram", "x0T_dram", "yT_dram")}
            QUAD = U * TILES * TOK
            rows = lambda name, off: flat[name][bass.ds(off, QUAD)].rearrange("(u t n) -> t u n", u=U, t=TILES)

            def fetch(off, q, frees):
                wait(act, yv_ready, frees)
                act.dma_start(vt[q][:, :, :], rows("vxT_dram", off)).then_inc(vt_in[q], 16)
                act.dma_start(x0t[q][:, :, :], rows("x0T_dram", off)).then_inc(x0t_in[q], 16)

            def store(off, q, done):
                wait(act, yv_ready, done)
                act.dma_start(rows("yT_dram", off), yv[q][:, :, :]).then_inc(yv_out[q], 16)

            def copy_signal(n, p):
                act.wait_ge(sig_over, n + 1)
                wait(act, conv_ready, n - 1)
                nc.scalar.copy(sig[p][:, :], p_sig[p][:, 0:TILES]).then_inc(sig_ready, 1)

            def copy_sums(n, p):
                wait(act, conv_ready, n + 1)
                wait(act, back_ready, n - 1)
                nc.scalar.copy(ys[p][:, :], p_y[p][:, 0:TILES]).then_inc(ys_ready, 1)

            def body(it, first=False, last=False):
                for q in range(2):
                    for u in range(U):
                        n = 2 * U * it + U * q + u
                        copy_signal(n, u % 2)
                        if not (first and q == 0 and u == 0):
                            copy_sums(n - 1, (u - 1) % 2)
                        if u == 2 and not (first and q == 0):
                            off, off_next, done = at((2 * it + q - 1) * QUAD), at((2 * it + q + 1) * QUAD), at((2 * it + q) * U)
                            store(off, 1 - q, done)
                            if not (last and q == 1):
                                fetch(off_next, 1 - q, done)
            fetch(0, 0, 0)
            fetch(QUAD, 1, 0)
            body(0, first=True)
            with act.Fori(1, ITERS - 1) as it:
                body(it)
            body(ITERS - 1, last=True)
            copy_sums(DIM - 1, 1)
            store((2 * ITERS - 1) * QUAD, 1, DIM)
            for p in range(2):
                act.wait_ge(yv_out[p], 16 * ITERS)

        @block.tensor
        def _(pe):
            mm, tp = nc.tensor.matmul, nc.tensor.transpose

            def signal_over(it, q, u):
                n = 2 * U * it + U * q + u
                if u == 0:
                    pe.wait_ge(vt_in[q], 16 * it + 16)
                wait(pe, sig_ready, n - 1)
                tp(p_sig[u % 2][:, 0:TILES], vt[q][:, u, :], ident[:, :]).then_inc(sig_over, 1)

            def convolve(it, q, u):
                n = 2 * U * it + U * q + u
                pe.wait_ge(toep_in[u], 16 * (2 * it + q) + 16)
                pe.wait_ge(sig_ready, n + 1)
                wait(pe, ys_ready, n - 1)
                p = u % 2
                for lag in range(CHUNKS):
                    last = mm(by_seq(p_y[p][:, 0:TILES])[:, :, lag:], toep[u][:, lag * TOK:(lag + 1) * TOK],
                              by_seq(sig[p][:, :])[:, :, 0:CHUNKS - lag], start=(lag == 0), stop=(lag == CHUNKS - 1))
                last.then_inc(conv_ready, 1)

            def back_over(it, q, u):
                n = 2 * U * it + U * q + u
                pe.wait_ge(ys_ready, n + 1)
                wait(pe, yv_ready, n - 1)
                tp(p_back[u % 2][:, 0:TOK], ys[u % 2][:, :], ident[:, :]).then_inc(back_ready, 1)

            def body(it, first=False):
                for q in range(2):
                    for u in range(U):
                        nxt = (it, q, u + 1) if u + 1 < U else (it, 1, 0) if q == 0 else (it + 1, 0, 0)
                        prev = (it, q, u - 1) if u else (it, 0, U - 1) if q else (it - 1, 1, U - 1)
                        if not (first == "last" and q == 1 and u == U - 1):
                            signal_over(*nxt)
                        convolve(it, q, u)
                        if not (first is True and q == 0 and u == 0):
                            back_over(*prev)
            signal_over(0, 0, 0)
            body(0, first=True)
            with pe.Fori(1, ITERS - 1) as it:
                body(it)
            body(ITERS - 1, first="last")
            back_over(ITERS - 1, 1, U - 1)

        @block.vector
        def _(dve):
            v_ = nc.vector

            def skip_and_gate(it, q, u):
                n = 2 * U * it + U * q + u
                channel = at_n(n)
                if u == 0:
                    dve.wait_ge(x0t_in[q], 16 * it + 16)
                    wait(dve, yv_out[q], 16 * it)
                dve.wait_ge(back_ready, n + 1)
                v_.scalar_tensor_tensor(out=skipped[u % 2][:, :], in0=vt[q][:, u, ::-1], scalar=skip[:, bass.ds(channel, 1)],
                                        in1=p_back[u % 2][:, 0:TOK], op0=ALU.mult, op1=ALU.add)
                dve.drain()
                v_.tensor_tensor(yv[q][:, u, :], skipped[u % 2][:, :], x0t[q][:, u, :], ALU.mult).then_inc(yv_ready, 1)

            at_n = lambda n: n if isinstance(n, int) else dve.snap(n)
            dve.wait_ge(skip_in, 16)

            def body(it):
                for q in range(2):
                    for u in range(U):
                        skip_and_gate(it, q, u)
            body(0)
            with dve.Fori(1, ITERS) as it:
                body(it)


def project_and_second_ffn(nc, ctx, t):
    sb = lambda name, shape, dt=F32: ctx.enter_context(nc.sbuf_tensor(name, shape, dt))
    names = ("weights2_in proj_ready x3_ready rstd3_ready var3_ready xn3_ready xn3T_ready xT3_done mixed3 rk3_ready tanh_done "
             "k3_done v3_ready y_ready3 setup3 x2b_ready").split()
    s = {n: ctx.enter_context(nc.semaphore(n)) for n in names}
    R = 4
    load_in = [[ctx.enter_context(nc.semaphore(f"load_{n}{u}")) for u in range(R)] for n in "yx"]
    stored = [ctx.enter_context(nc.semaphore(f"stored{u}")) for u in range(R)]
    ident = t["ident"]
    w_r, w_k, w_v, mu = t["w_r_sb"], t["w_k_sb"], t["w_v_sb"], t["mu_sb"]
    out_w, out_b = sb("out_w", [128, KT, DIM]), sb("out_b", [128, DIM])
    keep = sb("keep3", [128, TILES + 1])
    yv = [sb(f"yvT{u}", [128, KT, TOK]) for u in range(R)]
    x3 = [sb(f"x3_{u}", [128, DIM]) for u in range(R)]
    mean_var = [sb(f"mean_var3_{u}", [128, 2]) for u in range(R)]
    stats, var_eps, rstd = sb("stats3", [128, 6]), [sb(f"var_eps3_{p}", [128, 1]) for p in range(2)], [sb(f"rstd3_{p}", [128, 1]) for p in range(2)]
    xn = sb("xn3", [128, DIM])
    xT = sb("xT3", [128, KT, TOK + 1])
    dx = sb("dx3", [128, KT, TOK])
    x_r, x_k = [sb(f"x_r3_{p}", [128, KT, TOK]) for p in range(2)], [sb(f"x_k3_{p}", [128, KT, TOK]) for p in range(2)]
    tanh, k_pos, k_sq = [sb(f"tanh3_{p}", [128, DIM]) for p in range(2)], sb("k_pos3", [128, 256]), [sb(f"k_sq3_{p}", [128, KT, TOK]) for p in range(2)]
    gated = sb("gated3", [128, DIM])
    bank = [ctx.enter_context(nc.psum_tensor(f"bank3_{k}", [128, 512], F32)) for k in range(8)]
    p_proj, p_tr, p_rk, p_v = bank[0:2], bank[2:4], bank[4:6], bank[6:8]

    def rounds(eng, body, stages):
        for i in range(R):
            body(i, i, range(min(i, 3) + 1))
        with eng.Fori(1, TILES // R) as g:
            for u in range(R):
                body(g * R + u, u, range(4))
        for i in range(TILES, TILES + 3):
            body(i, i % R, range(i - TILES + 1, 4))

    with nc.Block() as block:
        @block.sync
        def _(sp):
            at = lambda n: n if isinstance(n, int) else sp.snap(n)
            yflat, xflat, oflat = (t["yT_dram"].rearrange("(k p) t n -> p k (t n)", p=128), t["x2_dram"].rearrange("r c -> (r c)"),
                                   t["out"].rearrange("r c -> (r c)"))
            sp.dma_start(out_w[:, :, :], t["out_w"].rearrange("(k p) n -> p k n", p=128)).then_inc(s["weights2_in"], 16)
            sp.dma_start(out_b[:, :], t["out_b"].partition_broadcast(128)).then_inc(s["weights2_in"], 16)

            def body(i, u, stages):
                if 0 in stages:
                    tok_at, block_at, free_y, free_x = at(i * TOK), at(i * (TOK * DIM)), at(i - R + 1), at((i - u) * (16 // R))
                    wait(sp, s["proj_ready"], free_y)
                    sp.dma_start(yv[u][:, :, :], yflat[:, :, bass.ds(tok_at, TOK)]).then_inc(load_in[0][u], 16)
                    wait(sp, stored[u], free_x)
                    sp.dma_start(x3[u][:, :], xflat[bass.ds(block_at, TOK * DIM)].rearrange("(p c) -> p c", p=TOK)).then_inc(load_in[1][u], 16)
            rounds(sp, body, 4)

        @block.gpsimd
        def _(pool):
            g_ = nc.gpsimd
            g_.memset(xT[:, :, :], 0.0)
            g_.memset(keep[:, :], 1.0)
            pool.drain()
            g_.memset(keep[:, 0:TILES].rearrange("p (b c) -> p b c", b=BATCH)[:, :, 0], 0.0)
            pool.drain().then_inc(s["setup3"], 1)
            pool.wait_ge(s["weights2_in"], 32)

            def body(i, u, stages):
                if 0 in stages:
                    pool.wait_ge(load_in[1][u], (i - u) * (16 // R) + 16)
                    g_.tensor_tensor(x3[u][:, :], x3[u][:, :], out_b[:, :], ALU.add).then_inc(s["x2b_ready"], 1)
                    pool.wait_ge(s["var3_ready"], i + 1)
                    wait(pool, s["xn3_ready"], i - 1)
                    g_.tensor_tensor(rstd[u % 2][:, :], var_eps[u % 2][:, :], t["minus_half"][:, 0:1], ALU.pow).then_inc(s["rstd3_ready"], 1)
            rounds(pool, body, 4)

        @block.scalar
        def _(act):
            s_ = nc.scalar
            at = lambda n: n if isinstance(n, int) else act.snap(n)
            oflat = t["out"].rearrange("r c -> (r c)")

            def body(i, u, stages):
                if 1 in stages:
                    j = i - 1
                    act.wait_ge(s["xn3T_ready"], j + 1)
                    wait(act, s["mixed3"], j)
                    s_.copy(xT[:, :, 1:TOK + 1], p_tr[(u - 1) % 2][:, 0:DIM].rearrange("p (k n) -> p k n", k=KT)).then_inc(s["xT3_done"], 1)
                if 2 in stages:
                    j, p = i - 2, u % 2
                    act.wait_ge(s["rk3_ready"], j + 1)
                    wait(act, s["v3_ready"], j - 1)
                    s_.activation(k_pos[:, :], p_rk[p][:, DIM:512], ACT.Relu)
                    act.drain()
                    s_.activation(k_sq[p][:, :, :], k_pos[:, :].rearrange("p (k n) -> p k n", k=KT), ACT.Square).then_inc(s["k3_done"], 1)
                    wait(act, s["y_ready3"], j - 1)
                    s_.activation(tanh[p][:, :], p_rk[p][:, 0:DIM], ACT.Tanh, scale=0.5).then_inc(s["tanh_done"], 1)
                if 3 in stages:
                    j = i - 3
                    block_at, done = at(j * (TOK * DIM)), at(j + 1)
                    act.wait_ge(s["y_ready3"], done)
                    act.dma_start(oflat[bass.ds(block_at, TOK * DIM)].rearrange("(p c) -> p c", p=TOK), x3[(u - 3) % R][:, :]).then_inc(stored[(u - 3) % R], 16)
            rounds(act, body, 4)
            for u in range(R):
                act.wait_ge(stored[u], 16 * TILES // R)

        @block.tensor
        def _(pe):
            mm, tp = nc.tensor.matmul, nc.tensor.transpose
            pe.wait_ge(s["weights2_in"], 32)

            def body(i, u, stages):
                if 1 in stages:
                    j, p = i - 1, (u - 1) % 2
                    pe.wait_ge(s["xn3_ready"], j + 1)
                    wait(pe, s["xT3_done"], j - 1)
                    for k in range(KT):
                        last = tp(p_tr[p][:, k * TOK:(k + 1) * TOK], xn[:, k * 128:(k + 1) * 128], ident[:, :])
                    last.then_inc(s["xn3T_ready"], 1)
                if 3 in stages:
                    j, p = i - 3, (u - 3) % 2
                    pe.wait_ge(s["k3_done"], j + 1)
                    wait(pe, s["y_ready3"], j - 1)
                    for k in range(KT):
                        last = mm(p_v[p][:, 0:DIM], k_sq[p][:, k, :], w_v[:, k, :], start=(k == 0), stop=(k == KT - 1))
                    last.then_inc(s["v3_ready"], 1)
                if 2 in stages:
                    j, p = i - 2, u % 2
                    pe.wait_ge(s["mixed3"], j + 1)
                    wait(pe, s["tanh_done"], j - 1)
                    for e in range(KT):
                        for k in range(KT):
                            mm(p_rk[p][:, DIM + e * TOK:DIM + (e + 1) * TOK], w_k[:, k, e * 128:(e + 1) * 128], x_k[p][:, k, :],
                               start=(k == 0), stop=(k == KT - 1))
                    for k in range(KT):
                        last = mm(p_rk[p][:, 0:DIM], x_r[p][:, k, :], w_r[:, k, :], start=(k == 0), stop=(k == KT - 1))
                    last.then_inc(s["rk3_ready"], 1)
                if 0 in stages:
                    pe.wait_ge(load_in[0][u], (i - u) * (16 // R) + 16)
                    wait(pe, s["x3_ready"], i - 1)
                    for k in range(KT):
                        last = mm(p_proj[u % 2][:, 0:DIM], yv[u][:, k, :], out_w[:, k, :], start=(k == 0), stop=(k == KT - 1))
                    last.then_inc(s["proj_ready"], 1)
            rounds(pe, body, 4)

        @block.vector
        def _(dve):
            v_ = nc.vector
            dve.wait_ge(s["setup3"], 1)

            def body(i, u, stages):
                if 1 in stages:
                    j, q = i - 1, (u - 1) % R
                    wait(dve, s["xn3T_ready"], j)
                    dve.wait_ge(s["rstd3_ready"], j + 1)
                    v_.tensor_scalar(xn[:, :], x3[q][:, :], mean_var[q][:, 0:1], rstd[q % 2][:, :], ALU.subtract, ALU.mult).then_inc(s["xn3_ready"], 1)
                if 3 in stages:
                    j, q = i - 3, (u - 3) % R
                    dve.wait_ge(s["v3_ready"], j + 1)
                    dve.wait_ge(s["tanh_done"], j + 1)
                    if 0 not in stages:
                        dve.drain()
                    v_.scalar_tensor_tensor(out=gated[:, :], in0=tanh[q % 2][:, :], scalar=1.0, in1=p_v[q % 2][:, 0:DIM], op0=ALU.add, op1=ALU.mult)
                if 0 in stages:
                    dve.wait_ge(s["proj_ready"], i + 1)
                    dve.wait_ge(s["x2b_ready"], i + 1)
                    v_.tensor_tensor(x3[u][:, :], p_proj[u % 2][:, 0:DIM], x3[u][:, :], ALU.add).then_inc(s["x3_ready"], 1)
                dve.drain()
                if 3 in stages:
                    j, q = i - 3, (u - 3) % R
                    v_.scalar_tensor_tensor(out=x3[q][:, :], in0=gated[:, :], scalar=0.5, in1=x3[q][:, :], op0=ALU.mult, op1=ALU.add).then_inc(s["y_ready3"], 1)
                if 0 in stages:
                    v_.bn_stats(stats[:, :], x3[u][:, :])
                    dve.drain()
                    v_.bn_aggr(mean_var[u][:, :], stats[:, :])
                    dve.drain()
                    v_.tensor_scalar(var_eps[u % 2][:, :], mean_var[u][:, 1:2], LN_EPS, None, ALU.add).then_inc(s["var3_ready"], 1)
                if 1 in stages:
                    j, q = i - 1, (u - 1) % R
                    dve.wait_ge(s["xT3_done"], j + 1)
                    wait(dve, s["rk3_ready"], j - 1)
                    v_.tensor_tensor(dx[:, :, :], xT[:, :, 1:TOK + 1], xT[:, :, 0:TOK], ALU.subtract)
                    dve.drain()
                    for k in range(KT):
                        for which, dst in enumerate((x_r[q % 2], x_k[q % 2])):
                            v_.scalar_tensor_tensor(out=dst[:, k, :], in0=dx[:, k, :], scalar=mu[:, which, k:k + 1],
                                                    in1=xT[:, k, 0:TOK], op0=ALU.mult, op1=ALU.add)
                    dve.drain()
                    v_.tensor_scalar(xT[:, :, 0], xT[:, :, TOK], keep[:, bass.ds(i, 1)], None, ALU.mult).then_inc(s["mixed3"], 1)
            rounds(dve, body, 4)


def build(nc, t):
    with ExitStack() as ctx:
        const = lambda name, dt=F32: ctx.enter_context(nc.sbuf_tensor(name, [128, 128], dt))
        for n in ("ident", "upto", "after", "ones", "nxt", "wrap"):
            t[n] = const(n)
        t["mask"], t["ident_b"] = const("mask", BF16), const("ident_b", BF16)
        t["minus_half"] = ctx.enter_context(nc.sbuf_tensor("minus_half", [128, 4], F32))
        t["xnT_dram"] = nc.dram_tensor("xnT_dram", (TILES, 128, KT, TOK), F32, kind="Internal").ap()
        t["params_dram"] = nc.dram_tensor("params_dram", (128, TILES, P_ALL), F32, kind="Internal").ap()
        t["taps_dram"] = nc.dram_tensor("taps_dram", (DIM, TOK - 1 + SEQ), F32, kind="Internal").ap()
        with ExitStack() as early:
            t["scal"] = early.enter_context(nc.sbuf_tensor("scal", [128, TILES, 24], F32))
            with ExitStack() as c:
                normalise_tokens(nc, c, t)
            with ExitStack() as c:
                scan_parameters(nc, c, t)
        with ExitStack() as c:
            long_filter(nc, c, t)
        t["x2_dram"] = nc.dram_tensor("x2_dram", (TILES * TOK, DIM), F32, kind="Internal").ap()
        for n in ("x0T_dram", "vxT_dram", "yT_dram"):
            t[n] = nc.dram_tensor(n, (DIM, TILES, TOK), F32, kind="Internal").ap()
        keepers = lambda name, shape: ctx.enter_context(nc.sbuf_tensor(name, shape, F32))
        for n in ("w_r", "w_k", "w_v"):
            t[n + "_sb"] = keepers(n + "_sb", [128, KT, DIM])
        t["mu_sb"] = keepers("mu_sb", [128, 2, KT])
        with ExitStack() as c:
            mixer_and_first_ffn(nc, c, t)
        with ExitStack() as c:
            long_convolution(nc, c, t)
        with ExitStack() as c:
            project_and_second_ffn(nc, c, t)


_OWN = ("x", "w_scal", "dt_bias", "A_log", "pos", "mlp_w1", "mlp_w2", "mlp_w3", "mlp_wo", "freq_b", "decay",
        "w_u", "w_bc", "w_out", "rms_w", "w_r", "w_k", "w_v", "mu", "in_w", "in_b", "short", "filt_bias", "out_w", "out_b")


def kernel(**inputs):
    import numpy as _np
    import concourse.bacc as _bacc
    from concourse import mybir as _mybir
    from concourse.bass_utils import run_bass_kernel_spmd as _run
    nc = _bacc.Bacc("TRN2", target_bir_lowering=False, num_devices=1)
    a = {k.replace("L0_", "").replace("attn_", ""): _np.asarray(v) for k, v in inputs.items()}
    f32 = _np.float32
    order = (_np.arange(2 * HEADS)[:, None] * STATE
             + _np.concatenate([_np.arange(0, STATE, 2), _np.arange(1, STATE, 2)])[None]).reshape(-1)
    where = _np.linspace(0.0, 1.0, SEQ, dtype=f32)
    turn = (2.0 * _np.pi * _np.linspace(0.0, SEQ - 1.0, SEQ) / SEQ).astype(f32) * f32(1e-4)
    pos = _np.stack([where, _np.cos(turn), -_np.sin(turn)]).astype(f32)
    deltas = _np.linspace(_np.log(0.01) / 1.5, _np.log(0.01) / 0.3, DIM).astype(f32)
    decay = _np.exp(-where[None, :] * _np.abs(deltas)[:, None]).astype(f32)
    arrays = {
        "x": a["a_x"].reshape(TILES * TOK, DIM),
        "w_scal": a["a_sel_proj_w"][2 * HEADS * STATE:].T,
        "dt_bias": a["a_dt_bias"], "A_log": a["a_A_log"],
        "pos": pos, "mlp_w1": a["b_mlp_w1"], "mlp_w2": a["b_mlp_w2"], "mlp_w3": a["b_mlp_w3"], "mlp_wo": a["b_mlp_wo"],
        "freq_b": _np.stack([a["b_freq"][0], a["b_mlp_b1"], a["b_mlp_b2"], a["b_mlp_b3"]], axis=1),
        "decay": decay,
        "w_u": a["a_in_proj_w"].T,
        "w_bc": a["a_sel_proj_w"][order].T,
        "w_out": a["a_out_proj_w"].T, "rms_w": a["a_rms_weight"].reshape(-1, 128).T,
        "w_r": a["ffn_W_r"].T, "w_k": a["ffn_W_k"].T, "w_v": a["ffn_W_v"].T,
        "mu": _np.stack([a["ffn_mu_r"].reshape(KT, 128).T, a["ffn_mu_k"].reshape(KT, 128).T], axis=1),
        "in_w": a["b_in_w"], "in_b": a["b_in_b"].reshape(-1, 128).T,
        "short": _np.concatenate([a["b_short_w"].reshape(6, 128, 3), a["b_short_b"].reshape(6, 128, 1)], axis=2).transpose(1, 0, 2),
        "filt_bias": a["b_filt_bias"], "out_w": a["b_out_w"], "out_b": a["b_out_b"],
    }
    arrays = {n: _np.ascontiguousarray(arrays[n]) for n in _OWN}
    t = {n: nc.dram_tensor("arg_" + n, v.shape, _mybir.dt.from_np(v.dtype), kind="ExternalInput").ap() for n, v in arrays.items()}
    t["out"] = nc.dram_tensor("out", (TILES * TOK, DIM), F32, kind="ExternalOutput").ap()
    build(nc, t)
    r = _run(nc, [{"arg_" + n: v for n, v in arrays.items()}], core_ids=[0])
    return r.results[0]["out"].reshape(BATCH, SEQ, DIM)
```

```python
import numpy as np
import concourse.bass as bass
from concourse import mybir
from contextlib import ExitStack

F32 = mybir.dt.float32
BF16 = mybir.dt.bfloat16
F32R = mybir.dt.float32r
ALU = mybir.AluOpType
ACT = mybir.ActivationFunctionType

BATCH, SEQ, DIM = 8, 2048, 256
HEADS, HEAD_U, STATE = 8, 64, 128
TOK = 128
CHUNKS = SEQ // TOK
TILES = BATCH * CHUNKS
COLS = TILES * HEADS
KT = DIM // 128
GROUP = 4
INNER = 3 * DIM
FILT = 64
LN_EPS, RMS_EPS = 1e-5, 1e-6
P_COS, P_SIN, P_A, P_G, P_RHO, P_W, P_EL, P_ET, P_ALL = 0, 8, 24, 40, 48, 56, 64, 72, 80
P_EARLY = P_G
MASKED = -30000.0
ROUND = 12582912.0
TWO_PI_HI = 6.28125
TWO_PI_LO = float(2.0 * np.pi - 6.28125)
SIN_LIMIT = 3.1415925


def wait(eng, sem, value):
    if isinstance(value, int) and value <= 0:
        return
    eng.wait_ge(sem, value)


def over(ap, n):
    return ap.unsqueeze(len(ap.shape)).broadcast_to(list(ap.shape) + [n])


def normalise_tokens(nc, ctx, t):
    sb = lambda name, shape, dt=F32: ctx.enter_context(nc.sbuf_tensor(name, shape, dt))
    ps = lambda name, shape, dt=F32: ctx.enter_context(nc.psum_tensor(name, shape, dt))
    sem = lambda name: ctx.enter_context(nc.semaphore(name))
    w_scal = sb("w_scal", [128, KT, 24])
    xg = sb("xg", [128, 2, 4, DIM])
    xn = sb("xn_g", [128, 4, DIM])
    stats = sb("stats_g", [128, 4, 6])
    mean_var = sb("mean_var_g", [128, 4, 2])
    var_eps = sb("var_eps_g", [128, 4])
    rstd = sb("rstd_g", [128, 4])
    xt = sb("xt_g", [128, 4, KT, TOK])
    p_tr = [ps(f"p_tr{k}", [128, 4 * TOK]) for k in range(KT)]
    p_sc = ps("p_sc", [128, 4, 24])
    x_in = [sem(f"x_in{k}") for k in range(2)]
    w_in, consts = sem("w_in"), sem("consts")
    var_ready, rstd_ready, xn_ready = sem("var_ready"), sem("rstd_ready"), sem("xn_ready")
    transposed, xt_ready, scal_ready, scal_taken, xt_out = (
        sem("transposed"), sem("xt_ready"), sem("scal_ready"), sem("scal_taken"), sem("xt_out"))
    PAIRS = TILES // 8
    with nc.Block() as block:
        @block.sync
        def _(sp):
            sp.dma_start(w_scal[:, :, :], t["w_scal"].rearrange("(k p) n -> p k n", p=128)).then_inc(w_in, 16)

            def load(g, par):
                wait(sp, xn_ready, 2 * g + par - 1)
                sp.dma_start(xg[:, par, :, :], t["x"][bass.ds((2 * g + par) * 4 * TOK, 4 * TOK), :]
                             .rearrange("(q p) c -> p q c", p=128)).then_inc(x_in[par], 16)
            load(0, 0)
            load(0, 1)
            with sp.Fori(1, PAIRS) as g:
                load(g, 0)
                load(g, 1)

        @block.gpsimd
        def _(pool):
            g_ = nc.gpsimd
            g_.memset(t["ident"][:, :], 0.0)
            g_.memset(t["upto"][:, :], 1.0)
            g_.memset(t["after"][:, :], 1.0)
            g_.memset(t["ones"][:, :], 1.0)
            g_.memset(t["nxt"][:, :], 0.0)
            g_.memset(t["wrap"][:, :], 0.0)
            g_.memset(t["mask"][:, :], MASKED)
            g_.memset(t["minus_half"][:, :], -0.5)
            pool.drain()
            g_.affine_select(out=t["ident"][:, :], in_=t["ident"][:, :], compare_op=ALU.not_equal, fill=1.0,
                             base=0, pattern=[[-1, 128]], channel_multiplier=1)
            g_.affine_select(out=t["upto"][:, :], in_=t["upto"][:, :], compare_op=ALU.is_ge, fill=0.0,
                             base=0, pattern=[[1, 128]], channel_multiplier=-1)
            g_.affine_select(out=t["after"][:, :], in_=t["after"][:, :], compare_op=ALU.is_gt, fill=0.0,
                             base=0, pattern=[[-1, 128]], channel_multiplier=1)
            g_.affine_select(out=t["nxt"][:, :], in_=t["nxt"][:, :], compare_op=ALU.not_equal, fill=1.0,
                             base=-1, pattern=[[-1, 128]], channel_multiplier=1)
            g_.affine_select(out=t["wrap"][:, :], in_=t["wrap"][:, :], compare_op=ALU.not_equal, fill=1.0,
                             base=-127, pattern=[[1, 128]], channel_multiplier=256)
            g_.affine_select(out=t["mask"][:, :], in_=t["mask"][:, :], compare_op=ALU.is_ge, fill=0.0,
                             base=0, pattern=[[-1, 128]], channel_multiplier=1)
            pool.drain()
            g_.tensor_copy(t["ident_b"][:, :], t["ident"][:, :])
            pool.drain().then_inc(consts, 1)

            def group(g, par):
                pool.wait_ge(var_ready, 2 * g + par + 1)
                g_.tensor_tensor(rstd[:, :], var_eps[:, :], t["minus_half"][:, 0:4], ALU.pow).then_inc(rstd_ready, 1)
            with pool.Fori(0, PAIRS) as g:
                group(g, 0)
                group(g, 1)

        @block.vector
        def _(dve):
            v_ = nc.vector

            def group(g, par):
                n = 2 * g + par
                dve.wait_ge(x_in[par], 16 * g + 16)
                for q in range(4):
                    v_.bn_stats(stats[:, q, :], xg[:, par, q, :])
                dve.drain()
                for q in range(4):
                    v_.bn_aggr(mean_var[:, q, :], stats[:, q, :])
                dve.drain()
                v_.tensor_scalar(var_eps[:, :], mean_var[:, :, 1], LN_EPS, None, ALU.add).then_inc(var_ready, 1)
                dve.wait_ge(rstd_ready, n + 1)
                wait(dve, transposed, n)
                for q in range(4):
                    last = v_.tensor_scalar(xn[:, q, :], xg[:, par, q, :], mean_var[:, q, 0:1], rstd[:, q:q + 1],
                                            ALU.subtract, ALU.mult)
                last.then_inc(xn_ready, 1)
                dve.wait_ge(scal_ready, n + 1)
                v_.tensor_copy(t["scal"][:, bass.ds(n * 4, 4), :], p_sc[:, :, :]).then_inc(scal_taken, 1)
            group(0, 0)
            group(0, 1)
            with dve.Fori(1, PAIRS) as g:
                group(g, 0)
                group(g, 1)

        @block.tensor
        def _(pe):
            pe.wait_ge(consts, 1)
            pe.wait_ge(w_in, 16)

            def group(g, par):
                n = 2 * g + par
                pe.wait_ge(xn_ready, n + 1)
                wait(pe, xt_ready, n)
                for k in range(KT):
                    for q in range(4):
                        last = nc.tensor.transpose(p_tr[k][:, q * TOK:(q + 1) * TOK],
                                                   xn[:, q, k * 128:(k + 1) * 128], t["ident"][:, :])
                last.then_inc(transposed, 1)
                pe.wait_ge(xt_ready, n + 1)
                wait(pe, scal_taken, n)
                for q in range(4):
                    for k in range(KT):
                        last = nc.tensor.matmul(p_sc[:, q, :], xt[:, q, k, :], w_scal[:, k, :],
                                                start=(k == 0), stop=(k == KT - 1))
                last.then_inc(scal_ready, 1)
            group(0, 0)
            group(0, 1)
            with pe.Fori(1, PAIRS) as g:
                group(g, 0)
                group(g, 1)

        @block.scalar
        def _(act):
            def group(g, par):
                n = 2 * g + par
                act.wait_ge(transposed, n + 1)
                wait(act, scal_ready, n)
                wait(act, xt_out, 16 * n)
                for k in range(KT):
                    last = nc.scalar.copy(xt[:, :, k, :], p_tr[k][:, :].rearrange("p (q t) -> p q t", q=4))
                last.then_inc(xt_ready, 1)
                act.wait_ge(xt_ready, n + 1)
                act.dma_start(t["xnT_dram"][bass.ds(n * 4, 4)].rearrange("q p k t -> p q k t"),
                              xt[:, :, :, :]).then_inc(xt_out, 16)
            group(0, 0)
            group(0, 1)
            with act.Fori(1, PAIRS) as g:
                group(g, 0)
                group(g, 1)
            act.wait_ge(xt_out, 16 * TILES // 4)


def scan_parameters(nc, ctx, t):
    sb = lambda name, shape, dt=F32: ctx.enter_context(nc.sbuf_tensor(name, shape, dt))
    sem = lambda name: ctx.enter_context(nc.semaphore(name))
    params = sb("params_all", [128, TILES, P_ALL])
    arr = {n: sb("sp_" + n, [128, COLS]) for n in ("e1", "e2", "dt", "dth", "gam", "a", "off", "ang", "m", "m2", "r")}
    a_hi = sb("sp_a_hi", [128, COLS], F32R)
    omd = sb("sp_omd", [128, COLS + HEADS])
    dt_bias = sb("dt_bias", [128, HEADS])
    a_neg = sb("a_neg", [128, HEADS])
    pp = [ctx.enter_context(nc.psum_tensor(f"p_sp{k}", [128, COLS])) for k in range(4)]
    small_in, act_done, dve_done, pe_done, out_done = (
        sem("small_in"), sem("sp_act"), sem("sp_dve"), sem("sp_pe"), sem("sp_out"))
    as3 = lambda ap: ap.rearrange("p (t h) -> p t h", h=HEADS)
    col = lambda at: params[:, :, at:at + HEADS]
    with nc.Block() as block:
        @block.sync
        def _(sp):
            sp.dma_start(dt_bias[:, :], t["dt_bias"].partition_broadcast(128)).then_inc(small_in, 16)
            sp.dma_start(a_neg[:, :], t["A_log"].partition_broadcast(128)).then_inc(small_in, 16)
            sp.wait_ge(dve_done, 6)
            sp.dma_start(t["params_dram"], params[:, :, :]).then_inc(out_done, 16)
            sp.wait_ge(out_done, 16)

        @block.vector
        def _(dve):
            v_ = nc.vector
            scal = t["scal"]
            dve.wait_ge(small_in, 32)
            v_.tensor_tensor(as3(arr["dt"][:, :]), scal[:, :, 0:8],
                             dt_bias[:, :].unsqueeze(1).broadcast_to([128, TILES, HEADS]), ALU.add)
            v_.memset(omd[:, COLS:COLS + HEADS], 0.0)
            dve.drain()
            v_.scalar_tensor_tensor(out=arr["m"][:, :], in0=arr["dt"][:, :], scalar=-1.0, in1=arr["dt"][:, :],
                                    op0=ALU.mult, op1=ALU.max).then_inc(dve_done, 1)
            dve.wait_ge(act_done, 1)
            v_.scalar_tensor_tensor(out=arr["dt"][:, :], in0=arr["dt"][:, :], scalar=0.0, in1=arr["e1"][:, :],
                                    op0=ALU.max, op1=ALU.add)
            v_.tensor_scalar(arr["e2"][:, :], arr["e2"][:, :], 1.0, None, ALU.add)
            v_.tensor_scalar(a_neg[:, :], a_neg[:, :], -1.0, None, ALU.mult)
            dve.drain()
            v_.reciprocal(arr["m2"][:, :], arr["e2"][:, :])
            v_.tensor_tensor(as3(arr["dth"][:, :]), as3(arr["dt"][:, :]), scal[:, :, 16:24], ALU.mult)
            v_.tensor_tensor(as3(arr["a"][:, :]), as3(arr["dt"][:, :]),
                             a_neg[:, :].unsqueeze(1).broadcast_to([128, TILES, HEADS]), ALU.mult)
            dve.drain()
            v_.tensor_tensor(arr["gam"][:, :], arr["m2"][:, :], arr["dt"][:, :], ALU.mult)
            v_.tensor_scalar(arr["m2"][:, :], arr["m2"][:, :], -1.0, 1.0, ALU.mult, ALU.add)
            v_.tensor_copy(a_hi[:, :], arr["a"][:, :])
            dve.drain()
            v_.tensor_copy(col(P_A), as3(a_hi[:, :].bitcast(F32)))
            v_.tensor_tensor(col(P_A + HEADS), as3(arr["a"][:, :]), as3(a_hi[:, :].bitcast(F32)), ALU.subtract)
            v_.tensor_tensor(omd[:, 0:COLS], arr["m2"][:, :], arr["dt"][:, :], ALU.mult)
            dve.drain().then_inc(dve_done, 1)
            dve.wait_ge(pe_done, 1)
            off4 = arr["off"][:, :].rearrange("p (b c h) -> p b c h", b=BATCH, c=CHUNKS)
            tot4 = arr["r"][:, :].rearrange("p (b c h) -> p b c h", b=BATCH, c=CHUNKS)
            v_.memset(off4[:, :, 0, :], 0.0)
            v_.tensor_copy(arr["r"][:, :], pp[1][:, :])
            for c in range(1, CHUNKS):
                dve.drain()
                v_.tensor_tensor(off4[:, :, c, :], off4[:, :, c - 1, :], tot4[:, :, c - 1, :], ALU.add)
            dve.drain()
            v_.tensor_tensor(arr["ang"][:, :], arr["off"][:, :], pp[0][:, :], ALU.add)
            v_.tensor_tensor(arr["e1"][:, :], arr["gam"][:, :], pp[2][:, :], ALU.add)
            dve.drain().then_inc(dve_done, 1)
            v_.tensor_scalar(arr["e2"][:, :], arr["e1"][:, :], 1e-30, None, ALU.max)
            v_.tensor_copy(col(P_G), as3(arr["e1"][:, :]))
            dve.drain()
            v_.reciprocal(arr["e1"][:, :], arr["e2"][:, :])
            dve.drain()
            v_.tensor_tensor(col(P_RHO), as3(arr["gam"][:, :]), as3(arr["e1"][:, :]), ALU.mult)
            for shift, r in ((0.0, "r"), (0.25, "m")):
                m = arr["m2"]
                v_.tensor_scalar(m[:, :], arr["ang"][:, :], 1.0 / (2.0 * np.pi), shift, ALU.mult, ALU.add)
                dve.drain()
                v_.tensor_scalar(m[:, :], m[:, :], ROUND, None, ALU.add)
                dve.drain()
                v_.tensor_scalar(m[:, :], m[:, :], ROUND, None, ALU.subtract)
                dve.drain()
                v_.scalar_tensor_tensor(out=arr[r][:, :], in0=m[:, :], scalar=-TWO_PI_HI, in1=arr["ang"][:, :],
                                        op0=ALU.mult, op1=ALU.add)
                dve.drain()
                v_.scalar_tensor_tensor(out=arr[r][:, :], in0=m[:, :], scalar=-TWO_PI_LO, in1=arr[r][:, :],
                                        op0=ALU.mult, op1=ALU.add)
                dve.drain()
                if shift:
                    v_.tensor_scalar(arr[r][:, :], arr[r][:, :], 2.0 * np.pi * shift, None, ALU.add)
                    dve.drain()
                v_.tensor_scalar(arr[r][:, :], arr[r][:, :], SIN_LIMIT, -SIN_LIMIT, ALU.min, ALU.max)
                dve.drain()
            dve.drain().then_inc(dve_done, 1)
            dve.wait_ge(act_done, 2)
            pair = params[:, :, P_SIN:P_SIN + 16].rearrange("p t (h s) -> p t h s", s=2)
            v_.tensor_copy(col(P_COS), as3(arr["gam"][:, :]))
            v_.tensor_copy(pair[:, :, :, 1], as3(arr["off"][:, :]))
            v_.tensor_scalar(pair[:, :, :, 0], as3(arr["off"][:, :]), -1.0, None, ALU.mult)
            dve.drain().then_inc(dve_done, 1)
            dve.wait_ge(act_done, 3)
            by_seq = params[:, :, :].rearrange("p (b c) n -> p b c n", b=BATCH)
            v_.memset(by_seq[:, :, 0, P_EL:P_ALL], 0.0).then_inc(dve_done, 1)

        @block.scalar
        def _(act):
            s_ = nc.scalar
            act.wait_ge(dve_done, 1)
            s_.activation(arr["e1"][:, :], arr["m"][:, :], ACT.Exp, scale=-1.0)
            s_.activation(as3(arr["e2"][:, :]), t["scal"][:, :, 8:16], ACT.Exp, scale=-1.0)
            s_.activation(a_neg[:, :], a_neg[:, :], ACT.Exp)
            act.drain()
            s_.activation(arr["e1"][:, :], arr["e1"][:, :], ACT.Ln, bias=1.0)
            act.drain().then_inc(act_done, 1)
            act.wait_ge(dve_done, 4)
            s_.activation(arr["off"][:, :], arr["r"][:, :], ACT.Sin)
            s_.activation(arr["gam"][:, :], arr["m"][:, :], ACT.Sin)
            act.drain().then_inc(act_done, 1)
            act.wait_ge(pe_done, 2)
            s_.activation(col(P_EL), as3(pp[0][:, :]), ACT.Exp)
            s_.activation(col(P_W), as3(pp[1][:, :]), ACT.Exp)
            s_.activation(col(P_ET), as3(pp[3][:, :]), ACT.Exp)
            act.drain().then_inc(act_done, 1)

        @block.tensor
        def _(pe):
            pe.wait_ge(dve_done, 2)
            for half in range(2):
                c = slice(half * 512, half * 512 + 512)
                c1 = slice(half * 512 + HEADS, half * 512 + 512 + HEADS)
                nc.tensor.matmul(pp[0][:, c], t["upto"][:, :], arr["dth"][:, c], start=True, stop=True)
                nc.tensor.matmul(pp[1][:, c], t["ones"][:, :], arr["dth"][:, c], start=True, stop=True)
                nc.tensor.matmul(pp[2][:, c], t["nxt"][:, :], omd[:, c], start=True, stop=False)
                last = nc.tensor.matmul(pp[2][:, c], t["wrap"][:, :], omd[:, c1], start=False, stop=True)
            last.then_inc(pe_done, 1)
            pe.wait_ge(dve_done, 3)
            for half in range(2):
                c = slice(half * 512, half * 512 + 512)
                nc.tensor.matmul(pp[0][:, c], t["upto"][:, :], arr["a"][:, c], start=True, stop=True)
                nc.tensor.matmul(pp[1][:, c], t["after"][:, :], arr["a"][:, c], start=True, stop=True)
                last = nc.tensor.matmul(pp[3][:, c], t["ones"][:, :], arr["a"][:, c], start=True, stop=True)
            last.then_inc(pe_done, 1)


def long_filter(nc, ctx, t):
    sb = lambda name, shape, dt=F32: ctx.enter_context(nc.sbuf_tensor(name, shape, dt))
    sem = lambda name: ctx.enter_context(nc.semaphore(name))
    pos = sb("pos", [3, SEQ])
    w1, w2, w3 = sb("mlp_w1", [3, FILT]), sb("mlp_w2", [FILT, FILT]), sb("mlp_w3", [FILT, FILT])
    wo = sb("mlp_wo", [FILT, DIM])
    freq_b = sb("freq_b", [FILT, 4])
    decay = sb("decay", [128, KT, SEQ])
    h, r, m = sb("mlp_h", [FILT, SEQ]), sb("mlp_r", [FILT, SEQ]), sb("mlp_m", [FILT, SEQ])
    taps = sb("taps", [128, KT, TOK - 1 + SEQ])
    ph = ctx.enter_context(nc.psum_tensor("p_mlp", [128, SEQ]))
    f_in, f_pe, f_dve, f_act, f_out = sem("f_in"), sem("f_pe"), sem("f_dve"), sem("f_act"), sem("f_out")
    with nc.Block() as block:
        @block.sync
        def _(sp):
            loads = [(pos[:, :], t["pos"]), (w1[:, :], t["mlp_w1"]), (w2[:, :], t["mlp_w2"]), (w3[:, :], t["mlp_w3"]),
                     (wo[:, :], t["mlp_wo"]), (freq_b[:, :], t["freq_b"]),
                     (decay[:, :, :], t["decay"].rearrange("(k p) n -> p k n", p=128))]
            for dst, src in loads:
                sp.dma_start(dst, src).then_inc(f_in, 16)
            sp.wait_ge(f_dve, 5)
            sp.dma_start(t["taps_dram"].rearrange("(k p) n -> p k n", p=128), taps[:, :, :]).then_inc(f_out, 16)
            sp.wait_ge(f_out, 16)

        @block.tensor
        def _(pe):
            pe.wait_ge(f_in, 16 * 7)
            for layer, (w, src) in enumerate(((w1, pos), (w2, h), (w3, h))):
                if layer:
                    pe.wait_ge(f_act, layer)
                for q in range(4):
                    last = nc.tensor.matmul(ph[0:FILT, q * 512:(q + 1) * 512], w[:, :], src[:, q * 512:(q + 1) * 512],
                                            start=True, stop=True)
                last.then_inc(f_pe, 1)
            for k in range(KT):
                if k == 0:
                    pe.wait_ge(f_act, 3)
                else:
                    pe.wait_ge(f_dve, 4)
                for q in range(4):
                    last = nc.tensor.matmul(ph[:, q * 512:(q + 1) * 512], wo[:, k * 128:(k + 1) * 128],
                                            h[:, q * 512:(q + 1) * 512], start=True, stop=True)
                last.then_inc(f_pe, 1)

        @block.vector
        def _(dve):
            v_ = nc.vector
            v_.memset(taps[:, :, 0:TOK - 1], 0.0)
            dve.wait_ge(f_in, 16 * 7)
            for layer in range(3):
                dve.wait_ge(f_pe, layer + 1)
                v_.tensor_scalar(r[:, :], ph[0:FILT, :], freq_b[:, layer + 1:layer + 2], freq_b[:, 0:1], ALU.add, ALU.mult)
                dve.drain()
                v_.tensor_scalar(m[:, :], r[:, :], 1.0 / (2.0 * np.pi), None, ALU.mult)
                dve.drain()
                v_.tensor_scalar(m[:, :], m[:, :], ROUND, None, ALU.add)
                dve.drain()
                v_.tensor_scalar(m[:, :], m[:, :], ROUND, None, ALU.subtract)
                dve.drain()
                v_.scalar_tensor_tensor(out=r[:, :], in0=m[:, :], scalar=-TWO_PI_HI, in1=r[:, :], op0=ALU.mult, op1=ALU.add)
                dve.drain()
                v_.scalar_tensor_tensor(out=r[:, :], in0=m[:, :], scalar=-TWO_PI_LO, in1=r[:, :], op0=ALU.mult, op1=ALU.add)
                dve.drain()
                v_.tensor_scalar(r[:, :], r[:, :], SIN_LIMIT, -SIN_LIMIT, ALU.min, ALU.max)
                dve.drain().then_inc(f_dve, 1)
                dve.wait_ge(f_act, layer + 1)
            for k in range(KT):
                dve.wait_ge(f_pe, 4 + k)
                v_.tensor_tensor(taps[:, k, TOK - 1:], decay[:, k, :], ph[:, :], ALU.mult)
                dve.drain().then_inc(f_dve, 1)

        @block.scalar
        def _(act):
            for layer in range(3):
                act.wait_ge(f_dve, layer + 1)
                nc.scalar.activation(h[:, :], r[:, :], ACT.Sin).then_inc(f_act, 1)


def mixer_and_first_ffn(nc, ctx, t):
    sb = lambda name, shape, dt=F32: ctx.enter_context(nc.sbuf_tensor(name, shape, dt))
    W4 = GROUP * STATE
    H64 = GROUP * HEAD_U
    ident, ident_b, upto, after, mask = t["ident"], t["ident_b"], t["upto"], t["after"], t["mask"]
    w_u, w_bc = [sb(f"w_u{p}", [128, KT, 512], F32R) for p in range(2)], [sb(f"w_bc{p}", [128, KT, 2048], F32R) for p in range(2)]
    after_r = sb("after_r", [128, 128], F32R)
    w_out, rms_w = sb("w_out", [128, 4, DIM]), sb("rms_w", [128, 4])
    in_w, in_b, short = sb("in_w", [128, KT, INNER]), sb("in_b", [128, 6]), sb("short", [128, 6, 4])
    first_tap_b = sb("first_tap_b", [128, 6])
    w_r, w_k, w_v, mu = t["w_r_sb"], t["w_k_sb"], t["w_v_sb"], t["mu_sb"]
    stage = sb("stage", [128, KT, 2560])
    keep = sb("keep", [128, TILES + 1])
    rms_eps = sb("rms_eps", [128, 1])
    xnT_raw = sb("xnT_raw", [128, KT, TOK])
    xnT = [sb(f"xnT{p}", [128, KT, TOK], F32R) for p in range(2)]
    early = sb("par_early", [128, P_EARLY])
    late = sb("par_late", [128, P_ALL - P_EARLY])
    rot1 = [sb(f"rot1_{k}", [128, W4]) for k in range(2)]
    rot2 = [sb(f"rot2_{k}", [128, W4]) for k in range(2)]
    turned = [[sb(f"turned_{g}{k}", [128, W4]) for k in range(2)] for g in range(2)]
    turned_t = [[sb(f"turned_t{g}{k}", [128, W4]) for k in range(2)] for g in range(2)]
    steps = [sb(f"steps{p}", [128, W4], F32R) for p in range(2)]
    decay, own, mix = ([sb(f"{what}{g}", [128, W4]) for g in range(2)] for what in ("decay", "own", "mix"))
    u_g, u_w, state = sb("u_g", [128, 512]), sb("u_w", [128, 512]), sb("state", [128, 512])
    y_from, y = [sb(f"y_from{g}", [128, H64]) for g in range(2)], sb("y", [128, 512])
    y_sq, mean_sq, ms_eps, y_rstd = sb("y_sq", [128, 512]), sb("mean_sq", [128, 1]), sb("ms_eps", [128, 1]), sb("y_rstd", [128, 1])
    yT = sb("yT", [128, 512])
    x_in, x1, x2 = sb("x_in", [128, DIM]), sb("x1", [128, DIM]), sb("x2", [128, DIM])
    xn = [sb(f"xn_{n}", [128, DIM]) for n in "12"]
    stats, mean_var, var_eps, rstd = ([sb(f"{what}_{n}", [128, w]) for n in "12"] for what, w in
                                      (("stats", 6), ("mean_var", 2), ("var_eps", 1), ("rstd", 1)))
    xT = sb("xT", [128, KT, TOK + 1])
    dx, x_r, x_k = sb("dx", [128, KT, TOK]), sb("x_r", [128, KT, TOK]), sb("x_k", [128, KT, TOK])
    tanh_r, k_pos, k_sq, gated = sb("tanh_r", [128, DIM]), sb("k_pos", [128, 256]), sb("k_sq", [128, KT, TOK]), sb("gated", [128, DIM])
    x2T = sb("x2T", [128, KT, TOK])
    up = sb("up", [128, 6, TOK + 2])
    conv = sb("conv", [128, 6, TOK])
    vx = sb("vx", [128, KT, TOK])
    bank = [ctx.enter_context(nc.psum_tensor(f"bank{k}", [128, 512], F32)) for k in range(8)]
    p_bc, p_tr, p_arg, p_gram, p_y, p_post = bank[0:2], bank[2:4], bank[4], bank[5], bank[6], bank[7]
    p_state = p_arg

    names = ("project_b0 project_b1 project_c0 project_c1 rotate_b0 rotate_b1 rotate_c0 rotate_c1 turn_b0 turn_b1 turn_c0 turn_c1 "
             "over_b0 over_b1 over_c0 over_c1 copy_b0 copy_b1 copy_c0 copy_c1 steps0 steps1 logs0 logs1 exp0 exp1 own0 own1 "
             "values gate_values gram0 gram1 mix0 mix1 outputs0 outputs1 take_y0 take_y1 weigh_values new_state fade carry_state "
             "split_hi split_rest y_over copy_yT square_y scan_rstd project_out residual1 rstd1 norm1 xn_over copy_xT shift_mix "
             "receptance_key r_and_k value residual2 rstd2 norm2 x2n_over copy_x2T widen0 widen1 take_up0 take_up1 carry_up short_filter "
             "weights_in setup w_hi w_scaled load_xnT load_early load_late load_x store_x2 store_x0 store_vx").split()
    s = {n: ctx.enter_context(nc.semaphore(n)) for n in names}

    def wait_for(eng, step, i):
        each = 16 if step.startswith(("load", "store")) else 1
        wait(eng, s[step], min(i + 1, TILES) * each if isinstance(i, int) else (i + 1) * each)

    BANK_4 = (("logs0", 0, "exp0"), ("new_state", 1, "carry_state"), ("logs1", 0, "exp1"))
    BANK_5 = (("gram0", 1, "mix0"), ("gram1", 1, "mix1"), ("values", 0, "gate_values"))
    BANK_7 = (("widen1", 4, "take_up1"), ("xn_over", 3, "copy_xT"), ("receptance_key", 3, "r_and_k"), ("y_over", 2, "copy_yT"),
              ("value", 3, "residual2"), ("project_out", 2, "residual1"), ("x2n_over", 3, "copy_x2T"), ("widen0", 3, "take_up0"))

    def bank_read(eng, bank, step, i):
        at = [name for name, _, _ in bank].index(step)
        lag = bank[at][1]
        if isinstance(i, int):
            for n, (name, other, reader) in enumerate(bank):
                if name != step:
                    wait_for(eng, reader, i + lag - other - (1 if n > at else 0))
        else:
            _, other, reader = bank[at - 1]
            wait_for(eng, reader, i + (lag - other - (0 if at else 1)))
    BC = "bc"
    heads = lambda ap: ap.rearrange("p (h n) -> p h n", h=GROUP)
    all_heads = lambda ap: ap.rearrange("p (h n) -> p h n", h=HEADS)
    group_of = lambda ap, g: ap[:, g * GROUP:(g + 1) * GROUP]
    e_col = lambda at: early[:, at:at + HEADS]
    l_col = lambda at: late[:, at - P_EARLY:at - P_EARLY + HEADS]
    halves = lambda ap: ap.rearrange("p (k n) -> p k n", k=KT)
    SPLIT = [(p, q, k) for p, q in ((1, 0), (0, 1), (0, 0)) for k in range(KT)]

    LAGS = 4

    def rounds(eng, body):
        def some(it):
            def on(lag, step, *args):
                if 0 <= it - lag < TILES:
                    step(it - lag, *args)
            return on
        for it in range(LAGS + 1):
            body(some(it))
        with eng.Fori(LAGS + 1, TILES) as it:
            body(lambda lag, step, *args: step(it - lag if lag else it, *args))
        for it in range(TILES, TILES + LAGS):
            body(some(it))

    with nc.Block() as block:
        @block.sync
        def _(sp):
            by_k = lambda name: t[name].rearrange("(k p) n -> p k n", p=128)
            for dst, src in ((stage[:, :, 0:2048], by_k("w_bc")), (stage[:, :, 2048:2560], by_k("w_u")), (w_out[:, :, :], by_k("w_out")),
                             (rms_w[:, :], t["rms_w"]), (in_b[:, :], t["in_b"]), (short[:, :, :], t["short"]), (mu[:, :, :], t["mu"]),
                             (in_w[:, :, :], by_k("in_w")), (w_r[:, :, :], by_k("w_r")), (w_k[:, :, :], by_k("w_k")), (w_v[:, :, :], by_k("w_v"))):
                sp.dma_start(dst, src).then_inc(s["weights_in"], 16)
            at = lambda n: n if isinstance(n, int) else sp.snap(n)
            flat = {n: t[n].rearrange(how) for n, how in (
                ("x", "r c -> (r c)"), ("x2_dram", "r c -> (r c)"), ("xnT_dram", "t p k n -> (t p k n)"),
                ("params_dram", "p t n -> p (t n)"))}
            flat |= {n: t[n].rearrange("(k p) t n -> p k (t n)", p=128) for n in ("x0T_dram", "vxT_dram")}

            def load_xnT(i):
                block_at, this = at(i * (TOK * DIM)), at(i * 1)
                wait(sp, s["split_rest"], this)
                sp.dma_start(xnT_raw[:, :, :], flat["xnT_dram"][bass.ds(block_at, TOK * DIM)]
                             .rearrange("(p k n) -> p k n", p=128, k=KT)).then_inc(s["load_xnT"], 16)

            def load_early(i):
                early_at, this = at(i * P_ALL), at(i * 1)
                for user in ("turn_b0", "turn_c0", "turn_b1", "turn_c1", "steps0", "steps1"):
                    wait(sp, s[user], this)
                sp.dma_start(early[:, :], flat["params_dram"][:, bass.ds(early_at, P_EARLY)]).then_inc(s["load_early"], 16)

            def load_late(i):
                late_at, this = at(i * P_ALL + P_EARLY), at(i * 1)
                wait(sp, s["carry_state"], this)
                wait(sp, s["take_y1"], this)
                sp.dma_start(late[:, :], flat["params_dram"][:, bass.ds(late_at, P_ALL - P_EARLY)]).then_inc(s["load_late"], 16)

            def load_x(j):
                block_at, this = at(j * (TOK * DIM)), at(j * 1)
                wait(sp, s["residual1"], this)
                sp.dma_start(x_in[:, :], flat["x"][bass.ds(block_at, TOK * DIM)].rearrange("(p c) -> p c", p=TOK)).then_inc(s["load_x"], 16)

            def store_x2(j):
                block_at, nxt = at(j * (TOK * DIM)), at(j + 1)
                wait(sp, s["residual2"], nxt)
                sp.dma_start(flat["x2_dram"][bass.ds(block_at, TOK * DIM)].rearrange("(p c) -> p c", p=TOK), x2[:, :]).then_inc(s["store_x2"], 16)

            def store_conv(j):
                tok_at, nxt = at(j * TOK), at(j + 1)
                wait(sp, s["short_filter"], nxt)
                sp.dma_start(flat["x0T_dram"][:, :, bass.ds(tok_at, TOK)], conv[:, 0:KT, :]).then_inc(s["store_x0"], 16)
                sp.dma_start(flat["vxT_dram"][:, :, bass.ds(tok_at, TOK)], vx[:, :, :]).then_inc(s["store_vx"], 16)

            def body(on):
                on(0, load_xnT)
                on(1, load_late)
                on(0, load_early)
                on(4, store_conv)
                on(2, load_x)
                on(3, store_x2)
            rounds(sp, body)
            for step in ("store_x2", "store_x0", "store_vx"):
                wait_for(sp, step, TILES - 1)

        @block.tensor
        def _(pe):
            mm, tp = nc.tensor.matmul, nc.tensor.transpose
            pe.wait_ge(s["setup"], 1)
            pe.wait_ge(s["w_scaled"], 1)

            def project_bc(i, g, c):
                wait_for(pe, "split_rest", i)
                wait_for(pe, f"rotate_{BC[c]}{1 - g}", i - 1 + g)
                for n, (p, q, k) in enumerate(SPLIT):
                    last = mm(p_bc[c][:, :], xnT[p][:, k, :], w_bc[q][:, k, c * 1024 + g * W4:c * 1024 + (g + 1) * W4],
                              start=(n == 0), stop=(n == len(SPLIT) - 1))
                last.then_inc(s[f"project_{BC[c]}{g}"], 1)

            def decay_logs(i, g):
                wait_for(pe, f"steps{g}", i)
                bank_read(pe, BANK_4, f"logs{g}", i)
                mm(p_arg[:, :], after_r[:, :], steps[0][:, :], start=True, stop=False)
                mm(p_arg[:, :], after_r[:, :], steps[1][:, :], start=False, stop=False)
                mm(p_arg[:, :], ident_b[:, :], mask[:, :].unsqueeze(1).broadcast_to([128, GROUP, TOK]),
                   start=False, stop=True).then_inc(s[f"logs{g}"], 1)

            def project_u(i):
                wait_for(pe, "split_rest", i)
                bank_read(pe, BANK_5, "values", i)
                for n, (p, q, k) in enumerate(SPLIT):
                    last = mm(p_gram[:, :], xnT[p][:, k, :], w_u[q][:, k, :], start=(n == 0), stop=(n == len(SPLIT) - 1))
                last.then_inc(s["values"], 1)

            def turn_over(i, g, c):
                wait_for(pe, f"turn_{BC[c]}{g}", i)
                wait_for(pe, f"copy_{BC[c]}{1 - g}", i - 1 + g)
                for h in range(GROUP):
                    last = tp(p_tr[c][:, h * TOK:(h + 1) * TOK], turned[g][c][:, h * STATE:(h + 1) * STATE], ident[:, :])
                last.then_inc(s[f"over_{BC[c]}{g}"], 1)

            def gram(i, g):
                wait_for(pe, f"copy_b{g}", i)
                wait_for(pe, f"copy_c{g}", i)
                bank_read(pe, BANK_5, f"gram{g}", i)
                for h in range(GROUP):
                    c = slice(h * TOK, (h + 1) * TOK)
                    last = mm(p_gram[:, c], turned_t[g][0][:, c], turned_t[g][1][:, c], start=True, stop=True)
                last.then_inc(s[f"gram{g}"], 1)

            def outputs(i, g):
                wait_for(pe, f"mix{g}", i)
                wait_for(pe, f"take_y{1 - g}", i - 1 + g)
                wait_for(pe, "carry_state", i - 1)
                for h in range(GROUP):
                    v, r = slice((g * GROUP + h) * HEAD_U, (g * GROUP + h + 1) * HEAD_U), slice(h * TOK, (h + 1) * TOK)
                    mm(p_y[:, h * HEAD_U:(h + 1) * HEAD_U], mix[g][:, r], u_g[:, v], start=True, stop=True)
                    last = mm(p_y[:, H64 + h * HEAD_U:H64 + (h + 1) * HEAD_U], turned_t[g][1][:, r], state[:, v],
                              start=True, stop=True)
                last.then_inc(s[f"outputs{g}"], 1)

            def new_state(i):
                wait_for(pe, "weigh_values", i)
                bank_read(pe, BANK_4, "new_state", i)
                for h in range(HEADS):
                    v = slice(h * HEAD_U, (h + 1) * HEAD_U)
                    last = mm(p_state[:, v], turned[h // GROUP][0][:, (h % GROUP) * STATE:(h % GROUP + 1) * STATE], u_w[:, v],
                              start=True, stop=True)
                last.then_inc(s["new_state"], 1)

            def y_over(j):
                wait_for(pe, "take_y1", j)
                bank_read(pe, BANK_7, "y_over", j)
                for k in range(4):
                    last = tp(p_post[:, k * TOK:(k + 1) * TOK], y[:, k * 128:(k + 1) * 128], ident[:, :])
                last.then_inc(s["y_over"], 1)

            def x2n_over(j):
                wait_for(pe, "norm2", j)
                bank_read(pe, BANK_7, "x2n_over", j)
                for k in range(KT):
                    last = tp(p_post[:, k * TOK:(k + 1) * TOK], xn[1][:, k * 128:(k + 1) * 128], ident[:, :])
                last.then_inc(s["x2n_over"], 1)

            def widen(j, part):
                wait_for(pe, "copy_x2T", j)
                bank_read(pe, BANK_7, f"widen{part}", j)
                for e in range(4 * part, min(4 * part + 4, 6)):
                    for k in range(KT):
                        last = mm(p_post[:, (e % 4) * TOK:(e % 4 + 1) * TOK], in_w[:, k, e * 128:(e + 1) * 128], x2T[:, k, :],
                                  start=(k == 0), stop=(k == KT - 1))
                last.then_inc(s[f"widen{part}"], 1)

            def project_out(j):
                wait_for(pe, "copy_yT", j)
                bank_read(pe, BANK_7, "project_out", j)
                for k in range(4):
                    last = mm(p_post[:, 0:DIM], yT[:, k * TOK:(k + 1) * TOK], w_out[:, k, :], start=(k == 0), stop=(k == 3))
                last.then_inc(s["project_out"], 1)

            def xn_over(j):
                wait_for(pe, "norm1", j)
                bank_read(pe, BANK_7, "xn_over", j)
                for k in range(KT):
                    last = tp(p_post[:, k * TOK:(k + 1) * TOK], xn[0][:, k * 128:(k + 1) * 128], ident[:, :])
                last.then_inc(s["xn_over"], 1)

            def receptance_key(j):
                wait_for(pe, "shift_mix", j)
                bank_read(pe, BANK_7, "receptance_key", j)
                for e in range(KT):
                    for k in range(KT):
                        mm(p_post[:, DIM + e * TOK:DIM + (e + 1) * TOK], w_k[:, k, e * 128:(e + 1) * 128], x_k[:, k, :],
                           start=(k == 0), stop=(k == KT - 1))
                for k in range(KT):
                    last = mm(p_post[:, 0:DIM], x_r[:, k, :], w_r[:, k, :], start=(k == 0), stop=(k == KT - 1))
                last.then_inc(s["receptance_key"], 1)

            def value(j):
                wait_for(pe, "r_and_k", j)
                bank_read(pe, BANK_7, "value", j)
                for k in range(KT):
                    last = mm(p_post[:, 0:DIM], k_sq[:, k, :], w_v[:, k, :], start=(k == 0), stop=(k == KT - 1))
                last.then_inc(s["value"], 1)

            def body(on):
                on(0, project_bc, 0, 1)
                on(0, project_bc, 0, 0)
                on(4, widen, 1)
                on(1, gram, 0)
                on(1, turn_over, 1, 1)
                on(1, turn_over, 1, 0)
                on(3, xn_over)
                on(0, project_bc, 1, 1)
                on(0, decay_logs, 0)
                on(1, gram, 1)
                on(3, receptance_key)
                on(1, outputs, 0)
                on(2, y_over)
                on(0, project_bc, 1, 0)
                on(3, value)
                on(1, new_state)
                on(0, turn_over, 0, 1)
                on(2, project_out)
                on(1, outputs, 1)
                on(0, turn_over, 0, 0)
                on(3, x2n_over)
                on(0, project_u)
                on(3, widen, 0)
                on(0, decay_logs, 1)
            rounds(pe, body)

        @block.scalar
        def _(act):
            s_ = nc.scalar

            def split_xnT(i):
                wait_for(act, "load_xnT", i)
                for user in ("project_b0", "project_c0", "project_b1", "project_c1", "values"):
                    wait_for(act, user, i - 1)
                s_.copy(xnT[0][:, :, :], xnT_raw[:, :, :]).then_inc(s["split_hi"], 1)

            def exponentials(i, g):
                wait_for(act, f"logs{g}", i)
                wait_for(act, f"mix{g}", i - 1)
                s_.activation(decay[g][:, :], p_arg[:, :], ACT.Exp).then_inc(s[f"exp{g}"], 1)

            def copy_turned(i, g, c):
                wait_for(act, f"over_{BC[c]}{g}", i)
                wait_for(act, f"gram{g}", i - 1)
                if c == 1:
                    wait_for(act, f"outputs{g}", i - 1)
                s_.copy(turned_t[g][c][:, :], p_tr[c][:, :]).then_inc(s[f"copy_{BC[c]}{g}"], 1)

            def square_y(j):
                wait_for(act, "take_y1", j)
                wait_for(act, "scan_rstd", j - 1)
                s_.activation(y_sq[:, :], y[:, :], ACT.Square, scale=float((HEADS * HEAD_U) ** -0.5),
                              accum_out=mean_sq[:, :]).then_inc(s["square_y"], 1)

            def copy_yT(j):
                wait_for(act, "y_over", j)
                wait_for(act, "project_out", j - 1)
                s_.copy(yT[:, :], p_post[:, :]).then_inc(s["copy_yT"], 1)

            def copy_x2T(j):
                wait_for(act, "x2n_over", j)
                wait_for(act, "widen1", j - 1)
                s_.copy(x2T[:, :, :], halves(p_post[:, 0:DIM])).then_inc(s["copy_x2T"], 1)

            def take_up(j, part):
                wait_for(act, f"widen{part}", j)
                if part == 0:
                    wait_for(act, "carry_up", j)
                    wait_for(act, "store_x0", j - 1)
                for e in range(4 * part, min(4 * part + 4, 6)):
                    column = p_post[:, (e % 4) * TOK:(e % 4 + 1) * TOK]
                    s_.activation(conv[:, e, :], column, ACT.Identity, scale=short[:, e, 2:3], bias=first_tap_b[:, e:e + 1])
                    last = s_.activation(up[:, e, 2:TOK + 2], column, ACT.Identity, bias=in_b[:, e:e + 1])
                last.then_inc(s[f"take_up{part}"], 1)

            def copy_xT(j):
                wait_for(act, "xn_over", j)
                s_.copy(xT[:, :, 1:TOK + 1], halves(p_post[:, 0:DIM])).then_inc(s["copy_xT"], 1)

            def r_and_k(j):
                wait_for(act, "receptance_key", j)
                wait_for(act, "value", j - 1)
                wait_for(act, "residual2", j - 1)
                s_.activation(k_pos[:, :], p_post[:, DIM:512], ACT.Relu)
                act.drain()
                s_.activation(k_sq[:, :, :], halves(k_pos[:, :]), ACT.Square)
                s_.activation(tanh_r[:, :], p_post[:, 0:DIM], ACT.Tanh, scale=0.5).then_inc(s["r_and_k"], 1)

            act.wait_ge(s["weights_in"], 16 * 11)
            s_.copy(w_bc[0][:, :, :], stage[:, :, 0:2048])
            s_.copy(w_u[0][:, :, :], stage[:, :, 2048:2560])
            act.drain().then_inc(s["w_hi"], 1)

            def body(on):
                on(0, split_xnT)
                on(4, take_up, 0)
                on(4, take_up, 1)
                on(1, exponentials, 1)
                on(3, copy_xT)
                on(1, copy_turned, 1, 0)
                on(1, copy_turned, 1, 1)
                on(2, square_y)
                on(3, r_and_k)
                on(0, exponentials, 0)
                on(2, copy_yT)
                on(0, copy_turned, 0, 1)
                on(3, copy_x2T)
                on(0, copy_turned, 0, 0)
            rounds(act, body)

        @block.gpsimd
        def _(pool):
            g_ = nc.gpsimd
            g_.memset(state[:, :], 0.0)
            g_.memset(xT[:, :, :], 0.0)
            g_.memset(up[:, :, :], 0.0)
            g_.memset(keep[:, :], 1.0)
            g_.memset(rms_eps[:, :], RMS_EPS)
            pool.drain()
            g_.memset(keep[:, 0:TILES].rearrange("p (b c) -> p b c", b=BATCH)[:, :, 0], 0.0)
            pool.drain().then_inc(s["setup"], 1)
            pool.wait_ge(s["weights_in"], 16 * 11)
            for k in range(4):
                g_.tensor_scalar(w_out[:, k, :], w_out[:, k, :], rms_w[:, k:k + 1], None, ALU.mult)
            g_.tensor_copy(after_r[:, :], after[:, :])
            g_.tensor_tensor(first_tap_b[:, :], short[:, :, 2], in_b[:, :], ALU.mult)
            pool.drain()
            g_.tensor_tensor(first_tap_b[:, :], first_tap_b[:, :], short[:, :, 3], ALU.add)
            pool.wait_ge(s["w_hi"], 1)
            g_.tensor_tensor(w_bc[1][:, :, :], stage[:, :, 0:2048], w_bc[0][:, :, :].bitcast(F32), ALU.subtract)
            g_.tensor_tensor(w_u[1][:, :, :], stage[:, :, 2048:2560], w_u[0][:, :, :].bitcast(F32), ALU.subtract)
            pool.drain().then_inc(s["w_scaled"], 1)

            def split_xnT(i):
                wait_for(pool, "split_hi", i)
                g_.tensor_tensor(xnT[1][:, :, :], xnT_raw[:, :, :], xnT[0][:, :, :].bitcast(F32), ALU.subtract).then_inc(s["split_rest"], 1)

            def masked_steps(i, g):
                wait_for(pool, "load_early", i)
                wait_for(pool, f"logs{1 - g}", i - 1 + g)
                for p in range(2):
                    last = g_.tensor_tensor(heads(steps[p][:, :]), upto[:, :].unsqueeze(1).broadcast_to([128, GROUP, TOK]),
                                            over(group_of(e_col(P_A + p * HEADS), g), TOK), ALU.mult)
                last.then_inc(s[f"steps{g}"], 1)

            def add_turned(i, g, c):
                wait_for(pool, f"rotate_{BC[c]}{g}", i)
                wait_for(pool, f"over_{BC[c]}{g}", i - 1)
                if c == 0:
                    wait_for(pool, "new_state", i - 1)
                g_.tensor_tensor(turned[g][c][:, :], rot1[c][:, :], rot2[c][:, :], ALU.add).then_inc(s[f"turn_{BC[c]}{g}"], 1)

            def own_diagonal(i, g):
                wait_for(pool, "load_late", i)
                g_.tensor_tensor(heads(own[g][:, :]), ident[:, :].unsqueeze(1).broadcast_to([128, GROUP, TOK]),
                                 over(group_of(l_col(P_RHO), g), TOK), ALU.mult)

            def add_own(i, g):
                pool.drain()
                wait_for(pool, f"exp{g}", i)
                g_.tensor_tensor(decay[g][:, :], decay[g][:, :], own[g][:, :], ALU.add).then_inc(s[f"own{g}"], 1)

            def decay_values(i):
                wait_for(pool, "gate_values", i)
                wait_for(pool, "new_state", i - 1)
                g_.tensor_tensor(all_heads(u_w[:, :]), all_heads(u_g[:, :]), over(l_col(P_W), HEAD_U), ALU.mult).then_inc(s["weigh_values"], 1)

            def fade_state(i):
                wait_for(pool, "outputs1", i)
                g_.tensor_tensor(all_heads(state[:, :]), all_heads(state[:, :]), over(l_col(P_ET), HEAD_U), ALU.mult).then_inc(s["fade"], 1)

            def scan_rstd(j):
                wait_for(pool, "square_y", j)
                wait_for(pool, "residual1", j - 1)
                g_.tensor_tensor(ms_eps[:, :], mean_sq[:, :], rms_eps[:, :], ALU.add)
                pool.drain()
                g_.tensor_tensor(y_rstd[:, :], ms_eps[:, :], t["minus_half"][:, 0:1], ALU.pow).then_inc(s["scan_rstd"], 1)

            def layer_rstd(j, n):
                wait_for(pool, f"residual{n}", j)
                g_.tensor_tensor(rstd[n - 1][:, :], var_eps[n - 1][:, :], t["minus_half"][:, 0:1], ALU.pow).then_inc(s[f"rstd{n}"], 1)

            def body(on):
                on(0, split_xnT)
                on(1, own_diagonal, 0)
                on(1, add_own, 0)
                on(0, masked_steps, 0)
                on(1, own_diagonal, 1)
                on(0, add_turned, 0, 1)
                on(1, decay_values)
                on(2, scan_rstd)
                on(0, masked_steps, 1)
                on(1, add_own, 1)
                on(3, layer_rstd, 2)
                on(0, add_turned, 0, 0)
                on(0, add_turned, 1, 1)
                on(1, fade_state)
                on(2, layer_rstd, 1)
                on(0, add_turned, 1, 0)
            rounds(pool, body)

        @block.vector
        def _(dve):
            v_ = nc.vector

            def rotate(i, g, c):
                cos = over(group_of(e_col(P_COS), g), STATE)
                sin = early[:, P_SIN + 2 * g * GROUP:P_SIN + 2 * (g + 1) * GROUP]
                parts = lambda ap: ap.rearrange("p (h s n) -> p h s n", h=GROUP, s=2)
                wait_for(dve, "load_early", i)
                wait_for(dve, f"project_{BC[c]}{g}", i)
                wait_for(dve, f"turn_{BC[c]}{1 - g}", i - 1 + g)
                v_.tensor_tensor(heads(rot1[c][:, :]), heads(p_bc[c][:, :]), cos, ALU.mult)
                v_.tensor_tensor(parts(rot2[c][:, :]), parts(p_bc[c][:, :])[:, :, ::-1, :],
                                 over(sin.rearrange("p (h s) -> p h s", s=2), STATE // 2), ALU.mult).then_inc(s[f"rotate_{BC[c]}{g}"], 1)

            def gate_values(i):
                wait_for(dve, "values", i)
                wait_for(dve, "load_late", i)
                wait_for(dve, "weigh_values", i - 1)
                wait_for(dve, "outputs1", i - 1)
                v_.tensor_tensor(all_heads(u_g[:, :]), all_heads(p_gram[:, :]), over(l_col(P_G), HEAD_U), ALU.mult).then_inc(s["gate_values"], 1)

            def weigh_gram(i, g):
                wait_for(dve, f"gram{g}", i)
                wait_for(dve, f"own{g}", i)
                wait_for(dve, f"outputs{g}", i - 1)
                v_.tensor_tensor(mix[g][:, :], p_gram[:, :], decay[g][:, :], ALU.mult).then_inc(s[f"mix{g}"], 1)

            def take_y(i, g):
                wait_for(dve, f"outputs{g}", i)
                if g == 0:
                    wait_for(dve, "y_over", i - 1)
                    wait_for(dve, "square_y", i - 1)
                v_.tensor_tensor(heads(y_from[g][:, :]), heads(p_y[:, H64:]), over(group_of(l_col(P_EL), g), HEAD_U), ALU.mult)
                dve.drain()
                v_.tensor_tensor(y[:, g * H64:(g + 1) * H64], p_y[:, 0:H64], y_from[g][:, :], ALU.add).then_inc(s[f"take_y{g}"], 1)

            def carry_state(i):
                wait_for(dve, "fade", i)
                wait_for(dve, "new_state", i)
                v_.tensor_tensor(state[:, :], p_state[:, :], state[:, :], ALU.add).then_inc(s["carry_state"], 1)

            def norm(src, n):
                v_.bn_stats(stats[n - 1][:, :], src)
                dve.drain()
                v_.bn_aggr(mean_var[n - 1][:, :], stats[n - 1][:, :])
                dve.drain()
                v_.tensor_scalar(var_eps[n - 1][:, :], mean_var[n - 1][:, 1:2], LN_EPS, None, ALU.add).then_inc(s[f"residual{n}"], 1)

            def normalised(j, src, n):
                wait_for(dve, f"rstd{n}", j)
                wait_for(dve, "xn_over" if n == 1 else "x2n_over", j - 1)
                v_.tensor_scalar(xn[n - 1][:, :], src, mean_var[n - 1][:, 0:1], rstd[n - 1][:, :],
                                 ALU.subtract, ALU.mult).then_inc(s[f"norm{n}"], 1)

            def residual1(j):
                wait_for(dve, "project_out", j)
                wait_for(dve, "scan_rstd", j)
                wait_for(dve, "load_x", j)
                v_.scalar_tensor_tensor(out=x1[:, :], in0=p_post[:, 0:DIM], scalar=y_rstd[:, :], in1=x_in[:, :],
                                        op0=ALU.mult, op1=ALU.add)
                v_.tensor_scalar(xT[:, :, 0], xT[:, :, TOK], keep[:, bass.ds(j, 1)], None, ALU.mult)
                dve.drain()
                norm(x1[:, :], 1)

            def shift_mix(j):
                wait_for(dve, "copy_xT", j)
                wait_for(dve, "receptance_key", j - 1)
                v_.tensor_tensor(dx[:, :, :], xT[:, :, 1:TOK + 1], xT[:, :, 0:TOK], ALU.subtract)
                dve.drain()
                for k in range(KT):
                    for which, dst in enumerate((x_r, x_k)):
                        last = v_.scalar_tensor_tensor(out=dst[:, k, :], in0=dx[:, k, :], scalar=mu[:, which, k:k + 1],
                                                       in1=xT[:, k, 0:TOK], op0=ALU.mult, op1=ALU.add)
                last.then_inc(s["shift_mix"], 1)

            def residual2(j):
                wait_for(dve, "value", j)
                wait_for(dve, "r_and_k", j)
                v_.scalar_tensor_tensor(out=gated[:, :], in0=tanh_r[:, :], scalar=1.0, in1=p_post[:, 0:DIM], op0=ALU.add, op1=ALU.mult)
                dve.drain()
                wait_for(dve, "store_x2", j - 1)
                v_.scalar_tensor_tensor(out=x2[:, :], in0=gated[:, :], scalar=0.5, in1=x1[:, :], op0=ALU.mult, op1=ALU.add)
                dve.drain()
                norm(x2[:, :], 2)

            def short_filter(j):
                wait_for(dve, "take_up0", j)
                wait_for(dve, "take_up1", j)
                wait_for(dve, "store_vx", j - 1)
                for tap in (1, 0):
                    for e in range(6):
                        v_.scalar_tensor_tensor(out=conv[:, e, :], in0=up[:, e, tap:TOK + tap], scalar=short[:, e, tap:tap + 1],
                                                in1=conv[:, e, :], op0=ALU.mult, op1=ALU.add)
                    dve.drain()
                v_.tensor_tensor(vx[:, :, ::-1], conv[:, 4:6, :], conv[:, 2:4, :], ALU.mult).then_inc(s["short_filter"], 1)

            def carry_up(j):
                v_.tensor_scalar(up[:, :, 0:2], up[:, :, TOK:TOK + 2], keep[:, bass.ds(j, 1)], None, ALU.mult).then_inc(s["carry_up"], 1)

            dve.wait_ge(s["weights_in"], 16 * 11)
            dve.wait_ge(s["setup"], 1)

            def body(on):
                on(1, gate_values)
                on(0, rotate, 0, 1)
                on(0, rotate, 0, 0)
                on(1, weigh_gram, 0)
                on(3, shift_mix)
                on(4, short_filter)
                on(1, take_y, 0)
                on(0, rotate, 1, 1)
                on(3, residual2)
                on(1, weigh_gram, 1)
                on(3, carry_up)
                on(3, lambda j: normalised(j, x2[:, :], 2))
                on(2, residual1)
                on(0, rotate, 1, 0)
                on(1, carry_state)
                on(1, take_y, 1)
                on(2, lambda j: normalised(j, x1[:, :], 1))
            rounds(dve, body)


def long_convolution(nc, ctx, t):
    sb = lambda name, shape, dt=F32: ctx.enter_context(nc.sbuf_tensor(name, shape, dt))
    sem = lambda name: ctx.enter_context(nc.semaphore(name))
    U, Q, SLOTS = 4, 4, 8
    ident = t["ident"]
    skip = sb("skip", [128, DIM])
    HALF, AHEAD = TOK // 2, 2
    toep = [sb(f"toep{u}", [128, SEQ + HALF]) for u in range(SLOTS)]
    PARTS = {"dve": (0, 1152), "act": (1152, SEQ)}
    vt = [sb(f"vt{p}", [128, U, TOK]) for p in range(Q)]
    x0t = [sb(f"x0t{p}", [128, U, TOK]) for p in range(Q)]
    sig = [sb(f"sig{p}", [128, TILES]) for p in range(2)]
    skipped = [sb(f"skipped{p}", [128, TOK]) for p in range(2)]
    ys = [sb(f"ys{p}", [128, TILES]) for p in range(2)]
    yv = [sb(f"yv{p}", [128, U, TOK]) for p in range(Q)]
    pst = lambda name: ctx.enter_context(nc.psum_tensor(name, [128, 512], F32))
    p_sig, p_y, p_back = [pst(f"p_sig{p}") for p in range(2)], [pst(f"p_yc{p}") for p in range(2)], [pst(f"p_back{p}") for p in range(2)]
    skip_in = sem("skip_in")
    toep_in = [sem(f"toep_in{u}") for u in range(SLOTS)]
    quad_in, yv_out = [sem(f"quad_in{p}") for p in range(Q)], [sem(f"yv_out{p}") for p in range(Q)]
    sig_over, sig_ready, conv_ready, ys_ready, back_ready, yv_ready = (
        sem("sig_over"), sem("sig_ready"), sem("conv_ready"), sem("ys_ready"), sem("back_ready"), sem("yv_ready"))
    upper_by = {eng: sem(f"upper_by_{eng}") for eng in PARTS}

    def copy_upper(eng, name, copy, it, place):
        slot, (a, b) = place % SLOTS, PARTS[name]
        eng.wait_ge(toep_in[slot], 16 * (Q * U // SLOTS * it + place // SLOTS) + 16)
        copy(toep[slot][HALF:, a:b], toep[slot][0:HALF, a + HALF:b + HALF]).then_inc(upper_by[name], 1)

    by_seq = lambda ap: ap.rearrange("p (b c) -> p b c", b=BATCH)
    ROW = TOK - 1 + SEQ
    ITERS = DIM // (Q * U)
    taps = t["taps_dram"].rearrange("d n -> (d n)")

    with nc.Block() as block:
        @block.sync
        def _(sp):
            at = lambda n: n if isinstance(n, int) else sp.snap(n)
            sp.dma_start(skip[:, :], t["filt_bias"].partition_broadcast(128)).then_inc(skip_in, 16)

            def quad(it, q):
                n0 = Q * U * it + U * q
                offs = [at((n0 + u) * ROW) for u in range(U)]
                frees = [at(n0 + u - SLOTS + 1) for u in range(U)]
                for u in range(U):
                    wait(sp, conv_ready, frees[u])
                    src = taps[bass.ds(offs[u], ROW)]
                    rows = bass.AP(src.tensor, src.offset, [[1, HALF], [1, SEQ + HALF]])
                    slot = (U * q + u) % SLOTS
                    sp.dma_start(toep[slot][0:HALF, :], rows).then_inc(toep_in[slot], 16)
            for q in range(Q):
                quad(0, q)
            with sp.Fori(1, ITERS) as it:
                for q in range(Q):
                    quad(it, q)

        @block.scalar
        def _(act):
            at = lambda n: n if isinstance(n, int) else act.snap(n)
            flat = {n: t[n].rearrange("c t n -> (c t n)") for n in ("vxT_dram", "x0T_dram", "yT_dram")}
            QUAD = U * TILES * TOK
            rows = lambda name, off: flat[name][bass.ds(off, QUAD)].rearrange("(u t n) -> t u n", u=U, t=TILES)

            def fetch(off, q, frees):
                wait(act, yv_ready, frees)
                act.dma_start(vt[q][:, :, :], rows("vxT_dram", off)).then_inc(quad_in[q], 16)
                act.dma_start(x0t[q][:, :, :], rows("x0T_dram", off)).then_inc(quad_in[q], 16)

            def store(off, q, done):
                wait(act, yv_ready, done)
                act.dma_start(rows("yT_dram", off), yv[q][:, :, :]).then_inc(yv_out[q], 16)

            def copy_signal(n, p):
                act.wait_ge(sig_over, n + 1)
                wait(act, conv_ready, n - 1)
                nc.scalar.copy(sig[p][:, :], p_sig[p][:, 0:TILES]).then_inc(sig_ready, 1)

            def copy_sums(n, p):
                wait(act, conv_ready, n + 1)
                wait(act, back_ready, n - 1)
                nc.scalar.copy(ys[p][:, :], p_y[p][:, 0:TILES]).then_inc(ys_ready, 1)

            def body(it, first=False, last=False):
                for q in range(Q):
                    for u in range(U):
                        n = Q * U * it + U * q + u
                        copy_signal(n, u % 2)
                        place = U * q + u + AHEAD
                        if not (last and place >= Q * U):
                            copy_upper(act, "act", nc.scalar.copy, it, place)
                        if not (first and q == 0 and u == 0):
                            copy_sums(n - 1, (u - 1) % 2)
                        if u == 2 and not (first and q == 0):
                            off, off_next, done = at((Q * it + q - 1) * QUAD), at((Q * it + q + Q - 1) * QUAD), at((Q * it + q) * U)
                            slot = (q - 1) % Q
                            store(off, slot, done)
                            if not (last and q > 0):
                                fetch(off_next, slot, done)
            for q in range(Q):
                fetch(q * QUAD, q, 0)
            for place in range(AHEAD):
                copy_upper(act, "act", nc.scalar.copy, 0, place)
            body(0, first=True)
            with act.Fori(1, ITERS - 1) as it:
                body(it)
            body(ITERS - 1, last=True)
            copy_sums(DIM - 1, 1)
            store((Q * ITERS - 1) * QUAD, Q - 1, DIM)
            for p in range(Q):
                act.wait_ge(yv_out[p], 16 * ITERS)

        @block.tensor
        def _(pe):
            mm, tp = nc.tensor.matmul, nc.tensor.transpose

            def signal_over(it, q, u):
                n = Q * U * it + U * q + u
                if u == 0:
                    pe.wait_ge(quad_in[q], 32 * it + 32)
                wait(pe, sig_ready, n - 1)
                tp(p_sig[u % 2][:, 0:TILES], vt[q][:, u, :], ident[:, :]).then_inc(sig_over, 1)

            def convolve(it, q, u):
                n = Q * U * it + U * q + u
                for by in upper_by.values():
                    pe.wait_ge(by, n + 1)
                pe.wait_ge(sig_ready, n + 1)
                wait(pe, ys_ready, n - 1)
                p = u % 2
                for lag in range(CHUNKS):
                    last = mm(by_seq(p_y[p][:, 0:TILES])[:, :, lag:], toep[(U * q + u) % SLOTS][:, lag * TOK:(lag + 1) * TOK],
                              by_seq(sig[p][:, :])[:, :, 0:CHUNKS - lag], start=(lag == 0), stop=(lag == CHUNKS - 1))
                last.then_inc(conv_ready, 1)

            def back_over(it, q, u):
                n = Q * U * it + U * q + u
                pe.wait_ge(ys_ready, n + 1)
                wait(pe, yv_ready, n - 1)
                tp(p_back[u % 2][:, 0:TOK], ys[u % 2][:, :], ident[:, :]).then_inc(back_ready, 1)

            def body(it, first=False):
                for q in range(Q):
                    for u in range(U):
                        nxt = (it, q, u + 1) if u + 1 < U else (it, q + 1, 0) if q + 1 < Q else (it + 1, 0, 0)
                        prev = (it, q, u - 1) if u else (it, q - 1, U - 1) if q else (it - 1, Q - 1, U - 1)
                        if not (first == "last" and q == Q - 1 and u == U - 1):
                            signal_over(*nxt)
                        convolve(it, q, u)
                        if not (first is True and q == 0 and u == 0):
                            back_over(*prev)
            signal_over(0, 0, 0)
            body(0, first=True)
            with pe.Fori(1, ITERS - 1) as it:
                body(it)
            body(ITERS - 1, first="last")
            back_over(ITERS - 1, Q - 1, U - 1)

        @block.vector
        def _(dve):
            v_ = nc.vector

            def skip_and_gate(it, q, u):
                n = Q * U * it + U * q + u
                channel = at_n(n)
                if u == 0:
                    dve.wait_ge(quad_in[q], 32 * it + 32)
                    wait(dve, yv_out[q], 16 * it)
                dve.wait_ge(back_ready, n + 1)
                v_.scalar_tensor_tensor(out=skipped[u % 2][:, :], in0=vt[q][:, u, ::-1], scalar=skip[:, bass.ds(channel, 1)],
                                        in1=p_back[u % 2][:, 0:TOK], op0=ALU.mult, op1=ALU.add)
                dve.drain()
                v_.tensor_tensor(yv[q][:, u, :], skipped[u % 2][:, :], x0t[q][:, u, :], ALU.mult).then_inc(yv_ready, 1)

            at_n = lambda n: n if isinstance(n, int) else dve.snap(n)
            dve.wait_ge(skip_in, 16)

            def body(it, last=False):
                for q in range(Q):
                    for u in range(U):
                        place = U * q + u + AHEAD
                        if not (last and place >= Q * U):
                            copy_upper(dve, "dve", nc.vector.tensor_copy, it, place)
                        skip_and_gate(it, q, u)
            for place in range(AHEAD):
                copy_upper(dve, "dve", nc.vector.tensor_copy, 0, place)
            body(0)
            with dve.Fori(1, ITERS - 1) as it:
                body(it)
            body(ITERS - 1, last=True)


def project_and_second_ffn(nc, ctx, t):
    sb = lambda name, shape, dt=F32: ctx.enter_context(nc.sbuf_tensor(name, shape, dt))
    names = ("weights2_in proj_ready x3_ready rstd3_ready var3_ready xn3_ready xn3T_ready xT3_done mixed3 rk3_ready tanh_done "
             "k3_done v3_ready y_ready3 setup3 x2b_ready").split()
    s = {n: ctx.enter_context(nc.semaphore(n)) for n in names}
    R = 4
    load_in = [ctx.enter_context(nc.semaphore(f"load{u}")) for u in range(R)]
    stored = [ctx.enter_context(nc.semaphore(f"stored{u}")) for u in range(R)]
    ident = t["ident"]
    w_r, w_k, w_v, mu = t["w_r_sb"], t["w_k_sb"], t["w_v_sb"], t["mu_sb"]
    out_w, out_b = sb("out_w", [128, KT, DIM]), sb("out_b", [128, DIM])
    keep = sb("keep3", [128, TILES + 1])
    yv = [sb(f"yvT{u}", [128, KT, TOK]) for u in range(R)]
    x3 = [sb(f"x3_{u}", [128, DIM]) for u in range(R)]
    mean_var = [sb(f"mean_var3_{u}", [128, 2]) for u in range(R)]
    stats, var_eps, rstd = sb("stats3", [128, 6]), [sb(f"var_eps3_{p}", [128, 1]) for p in range(2)], [sb(f"rstd3_{p}", [128, 1]) for p in range(2)]
    xn = sb("xn3", [128, DIM])
    xT = sb("xT3", [128, KT, TOK + 1])
    dx = sb("dx3", [128, KT, TOK])
    x_r, x_k = [sb(f"x_r3_{p}", [128, KT, TOK]) for p in range(2)], [sb(f"x_k3_{p}", [128, KT, TOK]) for p in range(2)]
    tanh, k_pos, k_sq = [sb(f"tanh3_{p}", [128, DIM]) for p in range(2)], sb("k_pos3", [128, 256]), [sb(f"k_sq3_{p}", [128, KT, TOK]) for p in range(2)]
    gated = sb("gated3", [128, DIM])
    bank = [ctx.enter_context(nc.psum_tensor(f"bank3_{k}", [128, 512], F32)) for k in range(8)]
    p_proj, p_tr, p_rk, p_v = bank[0:2], bank[2:4], bank[4:6], bank[6:8]

    def rounds(eng, body, stages):
        for i in range(R):
            body(i, i, range(min(i, 3) + 1))
        with eng.Fori(1, TILES // R) as g:
            for u in range(R):
                body(g * R + u, u, range(4))
        for i in range(TILES, TILES + 3):
            body(i, i % R, range(i - TILES + 1, 4))

    with nc.Block() as block:
        @block.sync
        def _(sp):
            at = lambda n: n if isinstance(n, int) else sp.snap(n)
            yflat, xflat, oflat = (t["yT_dram"].rearrange("(k p) t n -> p k (t n)", p=128), t["x2_dram"].rearrange("r c -> (r c)"),
                                   t["out"].rearrange("r c -> (r c)"))
            sp.dma_start(out_w[:, :, :], t["out_w"].rearrange("(k p) n -> p k n", p=128)).then_inc(s["weights2_in"], 16)
            sp.dma_start(out_b[:, :], t["out_b"].partition_broadcast(128)).then_inc(s["weights2_in"], 16)

            def body(i, u, stages):
                if 0 in stages:
                    tok_at, block_at, free_y, free_x = at(i * TOK), at(i * (TOK * DIM)), at(i - R + 1), at((i - u) * (16 // R))
                    wait(sp, s["proj_ready"], free_y)
                    sp.dma_start(yv[u][:, :, :], yflat[:, :, bass.ds(tok_at, TOK)]).then_inc(load_in[u], 16)
                    wait(sp, stored[u], free_x)
                    sp.dma_start(x3[u][:, :], xflat[bass.ds(block_at, TOK * DIM)].rearrange("(p c) -> p c", p=TOK)).then_inc(load_in[u], 16)
            rounds(sp, body, 4)

        @block.gpsimd
        def _(pool):
            g_ = nc.gpsimd
            g_.memset(xT[:, :, :], 0.0)
            g_.memset(keep[:, :], 1.0)
            pool.drain()
            g_.memset(keep[:, 0:TILES].rearrange("p (b c) -> p b c", b=BATCH)[:, :, 0], 0.0)
            pool.drain().then_inc(s["setup3"], 1)
            pool.wait_ge(s["weights2_in"], 32)

            def body(i, u, stages):
                if 0 in stages:
                    pool.wait_ge(load_in[u], (i - u) * (32 // R) + 32)
                    g_.tensor_tensor(x3[u][:, :], x3[u][:, :], out_b[:, :], ALU.add).then_inc(s["x2b_ready"], 1)
                    pool.wait_ge(s["var3_ready"], i + 1)
                    wait(pool, s["xn3_ready"], i - 1)
                    g_.tensor_tensor(rstd[u % 2][:, :], var_eps[u % 2][:, :], t["minus_half"][:, 0:1], ALU.pow).then_inc(s["rstd3_ready"], 1)
            rounds(pool, body, 4)

        @block.scalar
        def _(act):
            s_ = nc.scalar
            at = lambda n: n if isinstance(n, int) else act.snap(n)
            oflat = t["out"].rearrange("r c -> (r c)")

            def body(i, u, stages):
                if 1 in stages:
                    j = i - 1
                    act.wait_ge(s["xn3T_ready"], j + 1)
                    wait(act, s["mixed3"], j)
                    s_.copy(xT[:, :, 1:TOK + 1], p_tr[(u - 1) % 2][:, 0:DIM].rearrange("p (k n) -> p k n", k=KT)).then_inc(s["xT3_done"], 1)
                if 2 in stages:
                    j, p = i - 2, u % 2
                    act.wait_ge(s["rk3_ready"], j + 1)
                    wait(act, s["v3_ready"], j - 1)
                    s_.activation(k_pos[:, :], p_rk[p][:, DIM:512], ACT.Relu)
                    act.drain()
                    s_.activation(k_sq[p][:, :, :], k_pos[:, :].rearrange("p (k n) -> p k n", k=KT), ACT.Square).then_inc(s["k3_done"], 1)
                    wait(act, s["y_ready3"], j - 1)
                    s_.activation(tanh[p][:, :], p_rk[p][:, 0:DIM], ACT.Tanh, scale=0.5).then_inc(s["tanh_done"], 1)
                if 3 in stages:
                    j = i - 3
                    block_at, done = at(j * (TOK * DIM)), at(j + 1)
                    act.wait_ge(s["y_ready3"], done)
                    act.dma_start(oflat[bass.ds(block_at, TOK * DIM)].rearrange("(p c) -> p c", p=TOK), x3[(u - 3) % R][:, :]).then_inc(stored[(u - 3) % R], 16)
            rounds(act, body, 4)
            for u in range(R):
                act.wait_ge(stored[u], 16 * TILES // R)

        @block.tensor
        def _(pe):
            mm, tp = nc.tensor.matmul, nc.tensor.transpose
            pe.wait_ge(s["weights2_in"], 32)

            def body(i, u, stages):
                if 1 in stages:
                    j, p = i - 1, (u - 1) % 2
                    pe.wait_ge(s["xn3_ready"], j + 1)
                    wait(pe, s["xT3_done"], j - 1)
                    for k in range(KT):
                        last = tp(p_tr[p][:, k * TOK:(k + 1) * TOK], xn[:, k * 128:(k + 1) * 128], ident[:, :])
                    last.then_inc(s["xn3T_ready"], 1)
                if 3 in stages:
                    j, p = i - 3, (u - 3) % 2
                    pe.wait_ge(s["k3_done"], j + 1)
                    wait(pe, s["y_ready3"], j - 1)
                    for k in range(KT):
                        last = mm(p_v[p][:, 0:DIM], k_sq[p][:, k, :], w_v[:, k, :], start=(k == 0), stop=(k == KT - 1))
                    last.then_inc(s["v3_ready"], 1)
                if 2 in stages:
                    j, p = i - 2, u % 2
                    pe.wait_ge(s["mixed3"], j + 1)
                    wait(pe, s["tanh_done"], j - 1)
                    for e in range(KT):
                        for k in range(KT):
                            mm(p_rk[p][:, DIM + e * TOK:DIM + (e + 1) * TOK], w_k[:, k, e * 128:(e + 1) * 128], x_k[p][:, k, :],
                               start=(k == 0), stop=(k == KT - 1))
                    for k in range(KT):
                        last = mm(p_rk[p][:, 0:DIM], x_r[p][:, k, :], w_r[:, k, :], start=(k == 0), stop=(k == KT - 1))
                    last.then_inc(s["rk3_ready"], 1)
                if 0 in stages:
                    pe.wait_ge(load_in[u], (i - u) * (32 // R) + 32)
                    wait(pe, s["x3_ready"], i - 1)
                    for k in range(KT):
                        last = mm(p_proj[u % 2][:, 0:DIM], yv[u][:, k, :], out_w[:, k, :], start=(k == 0), stop=(k == KT - 1))
                    last.then_inc(s["proj_ready"], 1)
            rounds(pe, body, 4)

        @block.vector
        def _(dve):
            v_ = nc.vector
            dve.wait_ge(s["setup3"], 1)

            def body(i, u, stages):
                if 1 in stages:
                    j, q = i - 1, (u - 1) % R
                    wait(dve, s["xn3T_ready"], j)
                    dve.wait_ge(s["rstd3_ready"], j + 1)
                    v_.tensor_scalar(xn[:, :], x3[q][:, :], mean_var[q][:, 0:1], rstd[q % 2][:, :], ALU.subtract, ALU.mult).then_inc(s["xn3_ready"], 1)
                if 3 in stages:
                    j, q = i - 3, (u - 3) % R
                    dve.wait_ge(s["v3_ready"], j + 1)
                    dve.wait_ge(s["tanh_done"], j + 1)
                    if 0 not in stages:
                        dve.drain()
                    v_.scalar_tensor_tensor(out=gated[:, :], in0=tanh[q % 2][:, :], scalar=1.0, in1=p_v[q % 2][:, 0:DIM], op0=ALU.add, op1=ALU.mult)
                if 0 in stages:
                    dve.wait_ge(s["proj_ready"], i + 1)
                    dve.wait_ge(s["x2b_ready"], i + 1)
                    v_.tensor_tensor(x3[u][:, :], p_proj[u % 2][:, 0:DIM], x3[u][:, :], ALU.add).then_inc(s["x3_ready"], 1)
                dve.drain()
                if 3 in stages:
                    j, q = i - 3, (u - 3) % R
                    v_.scalar_tensor_tensor(out=x3[q][:, :], in0=gated[:, :], scalar=0.5, in1=x3[q][:, :], op0=ALU.mult, op1=ALU.add).then_inc(s["y_ready3"], 1)
                if 0 in stages:
                    v_.bn_stats(stats[:, :], x3[u][:, :])
                    dve.drain()
                    v_.bn_aggr(mean_var[u][:, :], stats[:, :])
                    dve.drain()
                    v_.tensor_scalar(var_eps[u % 2][:, :], mean_var[u][:, 1:2], LN_EPS, None, ALU.add).then_inc(s["var3_ready"], 1)
                if 1 in stages:
                    j, q = i - 1, (u - 1) % R
                    dve.wait_ge(s["xT3_done"], j + 1)
                    wait(dve, s["rk3_ready"], j - 1)
                    v_.tensor_tensor(dx[:, :, :], xT[:, :, 1:TOK + 1], xT[:, :, 0:TOK], ALU.subtract)
                    dve.drain()
                    for k in range(KT):
                        for which, dst in enumerate((x_r[q % 2], x_k[q % 2])):
                            v_.scalar_tensor_tensor(out=dst[:, k, :], in0=dx[:, k, :], scalar=mu[:, which, k:k + 1],
                                                    in1=xT[:, k, 0:TOK], op0=ALU.mult, op1=ALU.add)
                    dve.drain()
                    v_.tensor_scalar(xT[:, :, 0], xT[:, :, TOK], keep[:, bass.ds(i, 1)], None, ALU.mult).then_inc(s["mixed3"], 1)
            rounds(dve, body, 4)


def build(nc, t):
    with ExitStack() as ctx:
        const = lambda name, dt=F32: ctx.enter_context(nc.sbuf_tensor(name, [128, 128], dt))
        for n in ("ident", "upto", "after", "ones", "nxt", "wrap"):
            t[n] = const(n)
        t["mask"], t["ident_b"] = const("mask", BF16), const("ident_b", BF16)
        t["minus_half"] = ctx.enter_context(nc.sbuf_tensor("minus_half", [128, 4], F32))
        t["xnT_dram"] = nc.dram_tensor("xnT_dram", (TILES, 128, KT, TOK), F32, kind="Internal").ap()
        t["params_dram"] = nc.dram_tensor("params_dram", (128, TILES, P_ALL), F32, kind="Internal").ap()
        t["taps_dram"] = nc.dram_tensor("taps_dram", (DIM, TOK - 1 + SEQ), F32, kind="Internal").ap()
        with ExitStack() as early:
            t["scal"] = early.enter_context(nc.sbuf_tensor("scal", [128, TILES, 24], F32))
            with ExitStack() as c:
                normalise_tokens(nc, c, t)
            with ExitStack() as c:
                scan_parameters(nc, c, t)
        with ExitStack() as c:
            long_filter(nc, c, t)
        t["x2_dram"] = nc.dram_tensor("x2_dram", (TILES * TOK, DIM), F32, kind="Internal").ap()
        for n in ("x0T_dram", "vxT_dram", "yT_dram"):
            t[n] = nc.dram_tensor(n, (DIM, TILES, TOK), F32, kind="Internal").ap()
        keepers = lambda name, shape: ctx.enter_context(nc.sbuf_tensor(name, shape, F32))
        for n in ("w_r", "w_k", "w_v"):
            t[n + "_sb"] = keepers(n + "_sb", [128, KT, DIM])
        t["mu_sb"] = keepers("mu_sb", [128, 2, KT])
        with ExitStack() as c:
            mixer_and_first_ffn(nc, c, t)
        with ExitStack() as c:
            long_convolution(nc, c, t)
        with ExitStack() as c:
            project_and_second_ffn(nc, c, t)


_OWN = ("x", "w_scal", "dt_bias", "A_log", "pos", "mlp_w1", "mlp_w2", "mlp_w3", "mlp_wo", "freq_b", "decay",
        "w_u", "w_bc", "w_out", "rms_w", "w_r", "w_k", "w_v", "mu", "in_w", "in_b", "short", "filt_bias", "out_w", "out_b")


def kernel(**inputs):
    import numpy as _np
    import concourse.bacc as _bacc
    from concourse import mybir as _mybir
    from concourse.bass_utils import run_bass_kernel_spmd as _run
    nc = _bacc.Bacc("TRN2", target_bir_lowering=False, num_devices=1)
    a = {k.replace("L0_", "").replace("attn_", ""): _np.asarray(v) for k, v in inputs.items()}
    f32 = _np.float32
    order = (_np.arange(2 * HEADS)[:, None] * STATE
             + _np.concatenate([_np.arange(0, STATE, 2), _np.arange(1, STATE, 2)])[None]).reshape(-1)
    where = _np.linspace(0.0, 1.0, SEQ, dtype=f32)
    turn = (2.0 * _np.pi * _np.linspace(0.0, SEQ - 1.0, SEQ) / SEQ).astype(f32) * f32(1e-4)
    pos = _np.stack([where, _np.cos(turn), -_np.sin(turn)]).astype(f32)
    deltas = _np.linspace(_np.log(0.01) / 1.5, _np.log(0.01) / 0.3, DIM).astype(f32)
    decay = _np.exp(-where[None, :] * _np.abs(deltas)[:, None]).astype(f32)
    arrays = {
        "x": a["a_x"].reshape(TILES * TOK, DIM),
        "w_scal": a["a_sel_proj_w"][2 * HEADS * STATE:].T,
        "dt_bias": a["a_dt_bias"], "A_log": a["a_A_log"],
        "pos": pos, "mlp_w1": a["b_mlp_w1"], "mlp_w2": a["b_mlp_w2"], "mlp_w3": a["b_mlp_w3"], "mlp_wo": a["b_mlp_wo"],
        "freq_b": _np.stack([a["b_freq"][0], a["b_mlp_b1"], a["b_mlp_b2"], a["b_mlp_b3"]], axis=1),
        "decay": decay,
        "w_u": a["a_in_proj_w"].T,
        "w_bc": a["a_sel_proj_w"][order].T,
        "w_out": a["a_out_proj_w"].T, "rms_w": a["a_rms_weight"].reshape(-1, 128).T,
        "w_r": a["ffn_W_r"].T, "w_k": a["ffn_W_k"].T, "w_v": a["ffn_W_v"].T,
        "mu": _np.stack([a["ffn_mu_r"].reshape(KT, 128).T, a["ffn_mu_k"].reshape(KT, 128).T], axis=1),
        "in_w": a["b_in_w"], "in_b": a["b_in_b"].reshape(-1, 128).T,
        "short": _np.concatenate([a["b_short_w"].reshape(6, 128, 3), a["b_short_b"].reshape(6, 128, 1)], axis=2).transpose(1, 0, 2),
        "filt_bias": a["b_filt_bias"], "out_w": a["b_out_w"], "out_b": a["b_out_b"],
    }
    arrays = {n: _np.ascontiguousarray(arrays[n]) for n in _OWN}
    t = {n: nc.dram_tensor("arg_" + n, v.shape, _mybir.dt.from_np(v.dtype), kind="ExternalInput").ap() for n, v in arrays.items()}
    t["out"] = nc.dram_tensor("out", (TILES * TOK, DIM), F32, kind="ExternalOutput").ap()
    build(nc, t)
    r = _run(nc, [{"arg_" + n: v for n, v in arrays.items()}], core_ids=[0])
    return r.results[0]["out"].reshape(BATCH, SEQ, DIM)
```

```python
import numpy as np
import concourse.bass as bass
from concourse import mybir
from contextlib import ExitStack

F32 = mybir.dt.float32
BF16 = mybir.dt.bfloat16
F32R = mybir.dt.float32r
ALU = mybir.AluOpType
ACT = mybir.ActivationFunctionType

BATCH, SEQ, DIM = 8, 2048, 256
HEADS, HEAD_U, STATE = 8, 64, 128
TOK = 128
CHUNKS = SEQ // TOK
TILES = BATCH * CHUNKS
COLS = TILES * HEADS
KT = DIM // 128
GROUP = 4
INNER = 3 * DIM
FILT = 64
LN_EPS, RMS_EPS = 1e-5, 1e-6
P_COS, P_SIN, P_A, P_G, P_RHO, P_W, P_EL, P_ET, P_ALL = 0, 8, 24, 40, 48, 56, 64, 72, 80
P_EARLY = P_G
MASKED = -30000.0
ROUND = 12582912.0
TWO_PI_HI = 6.28125
TWO_PI_LO = float(2.0 * np.pi - 6.28125)
SIN_LIMIT = 3.1415925


def wait(eng, sem, value):
    if isinstance(value, int) and value <= 0:
        return
    eng.wait_ge(sem, value)


def over(ap, n):
    return ap.unsqueeze(len(ap.shape)).broadcast_to(list(ap.shape) + [n])


def normalise_tokens(nc, ctx, t):
    sb = lambda name, shape, dt=F32: ctx.enter_context(nc.sbuf_tensor(name, shape, dt))
    ps = lambda name, shape, dt=F32: ctx.enter_context(nc.psum_tensor(name, shape, dt))
    sem = lambda name: ctx.enter_context(nc.semaphore(name))
    w_scal = sb("w_scal", [128, KT, 24])
    R, GROUPS, LAGS = 4, TILES // 4, 3
    xg = [sb(f"xg{u}", [128, 4, DIM]) for u in range(R)]
    two = lambda name, shape: [sb(f"{name}{p}", shape) for p in range(2)]
    xn, stats, mean_var = two("xn_g", [128, 4, DIM]), two("stats_g", [128, 4, 6]), two("mean_var_g", [128, 4, 2])
    var_eps, rstd, xt = two("var_eps_g", [128, 4]), two("rstd_g", [128, 4]), two("xt_g", [128, 4, KT, TOK])
    p_tr = [[ps(f"p_tr{p}{k}", [128, 4 * TOK]) for k in range(KT)] for p in range(2)]
    p_sc = [ps(f"p_sc{p}", [128, 4, 24]) for p in range(2)]
    x_in = [sem(f"x_in{k}") for k in range(R)]
    w_in, consts = sem("w_in"), sem("consts")
    var_ready, rstd_ready, xn_ready = sem("var_ready"), sem("rstd_ready"), sem("xn_ready")
    transposed, xt_ready, scal_ready, scal_taken = sem("transposed"), sem("xt_ready"), sem("scal_ready"), sem("scal_taken")
    xt_out = [sem(f"xt_out{p}") for p in range(2)]

    def rounds(eng, body):
        def some(g, u):
            def on(lag, step):
                if 0 <= R * g + u - lag < GROUPS:
                    step(R * g + u - lag, g, u - lag)
            return on
        for u in range(R):
            body(some(0, u))
        with eng.Fori(1, GROUPS // R) as g:
            for u in range(R):
                body(lambda lag, step: step(R * g + (u - lag), g, u - lag))
        for u in range(LAGS):
            body(some(GROUPS // R, u))

    with nc.Block() as block:
        @block.sync
        def _(sp):
            sp.dma_start(w_scal[:, :, :], t["w_scal"].rearrange("(k p) n -> p k n", p=128)).then_inc(w_in, 16)

            def load(n, g, v):
                wait(sp, xn_ready, n - R + 1)
                sp.dma_start(xg[v % R][:, :, :], t["x"][bass.ds(n * 4 * TOK, 4 * TOK), :]
                             .rearrange("(q p) c -> p q c", p=128)).then_inc(x_in[v % R], 16)
            rounds(sp, lambda on: on(0, load))

        @block.gpsimd
        def _(pool):
            g_ = nc.gpsimd
            g_.memset(t["ident"][:, :], 0.0)
            g_.memset(t["upto"][:, :], 1.0)
            g_.memset(t["after"][:, :], 1.0)
            g_.memset(t["ones"][:, :], 1.0)
            g_.memset(t["nxt"][:, :], 0.0)
            g_.memset(t["wrap"][:, :], 0.0)
            g_.memset(t["mask"][:, :], MASKED)
            g_.memset(t["minus_half"][:, :], -0.5)
            pool.drain()
            g_.affine_select(out=t["ident"][:, :], in_=t["ident"][:, :], compare_op=ALU.not_equal, fill=1.0,
                             base=0, pattern=[[-1, 128]], channel_multiplier=1)
            g_.affine_select(out=t["upto"][:, :], in_=t["upto"][:, :], compare_op=ALU.is_ge, fill=0.0,
                             base=0, pattern=[[1, 128]], channel_multiplier=-1)
            g_.affine_select(out=t["after"][:, :], in_=t["after"][:, :], compare_op=ALU.is_gt, fill=0.0,
                             base=0, pattern=[[-1, 128]], channel_multiplier=1)
            g_.affine_select(out=t["nxt"][:, :], in_=t["nxt"][:, :], compare_op=ALU.not_equal, fill=1.0,
                             base=-1, pattern=[[-1, 128]], channel_multiplier=1)
            g_.affine_select(out=t["wrap"][:, :], in_=t["wrap"][:, :], compare_op=ALU.not_equal, fill=1.0,
                             base=-127, pattern=[[1, 128]], channel_multiplier=256)
            g_.affine_select(out=t["mask"][:, :], in_=t["mask"][:, :], compare_op=ALU.is_ge, fill=0.0,
                             base=0, pattern=[[-1, 128]], channel_multiplier=1)
            pool.drain()
            g_.tensor_copy(t["ident_b"][:, :], t["ident"][:, :])
            pool.drain().then_inc(consts, 1)

            def token_rstd(n, g, v):
                wait(pool, var_ready, n + 1)
                wait(pool, xn_ready, n - 1)
                g_.tensor_tensor(rstd[v % 2][:, :], var_eps[v % 2][:, :], t["minus_half"][:, 0:4], ALU.pow).then_inc(rstd_ready, 1)
            rounds(pool, lambda on: on(0, token_rstd))

        @block.vector
        def _(dve):
            v_ = nc.vector

            def statistics(n, g, v):
                p = v % 2
                wait(dve, x_in[v % R], 16 * (g + (v // R) + 1))
                for q in range(4):
                    v_.bn_stats(stats[p][:, q, :], xg[v % R][:, q, :])
                dve.drain()
                for q in range(4):
                    v_.bn_aggr(mean_var[p][:, q, :], stats[p][:, q, :])
                dve.drain()
                wait(dve, rstd_ready, n - 1)
                v_.tensor_scalar(var_eps[p][:, :], mean_var[p][:, :, 1], LN_EPS, None, ALU.add).then_inc(var_ready, 1)

            def normalise(n, g, v):
                p = v % 2
                wait(dve, rstd_ready, n + 1)
                wait(dve, transposed, n - 1)
                for q in range(4):
                    last = v_.tensor_scalar(xn[p][:, q, :], xg[v % R][:, q, :], mean_var[p][:, q, 0:1], rstd[p][:, q:q + 1],
                                            ALU.subtract, ALU.mult)
                last.then_inc(xn_ready, 1)

            def take_scalars(n, g, v):
                wait(dve, scal_ready, n + 1)
                v_.tensor_copy(t["scal"][:, bass.ds(n * 4, 4), :], p_sc[v % 2][:, :, :]).then_inc(scal_taken, 1)

            def body(on):
                on(0, statistics)
                on(1, normalise)
                on(3, take_scalars)
            rounds(dve, body)

        @block.tensor
        def _(pe):
            pe.wait_ge(consts, 1)
            pe.wait_ge(w_in, 16)

            def transpose(n, g, v):
                p = v % 2
                wait(pe, xn_ready, n + 1)
                wait(pe, xt_ready, n - 1)
                for k in range(KT):
                    for q in range(4):
                        last = nc.tensor.transpose(p_tr[p][k][:, q * TOK:(q + 1) * TOK],
                                                   xn[p][:, q, k * 128:(k + 1) * 128], t["ident"][:, :])
                last.then_inc(transposed, 1)

            def scalars(n, g, v):
                p = v % 2
                wait(pe, xt_ready, n + 1)
                wait(pe, scal_taken, n - 1)
                for q in range(4):
                    for k in range(KT):
                        last = nc.tensor.matmul(p_sc[p][:, q, :], xt[p][:, q, k, :], w_scal[:, k, :],
                                                start=(k == 0), stop=(k == KT - 1))
                last.then_inc(scal_ready, 1)

            def body(on):
                on(1, transpose)
                on(2, scalars)
            rounds(pe, body)

        @block.scalar
        def _(act):
            def copy_and_store(n, g, v):
                p = v % 2
                wait(act, transposed, n + 1)
                wait(act, scal_ready, n - 1)
                wait(act, xt_out[p], 16 * (R // 2 * g + v // 2))
                for k in range(KT):
                    last = nc.scalar.copy(xt[p][:, :, k, :], p_tr[p][k][:, :].rearrange("p (q t) -> p q t", q=4))
                last.then_inc(xt_ready, 1)
                wait(act, xt_ready, n + 1)
                act.dma_start(t["xnT_dram"][bass.ds(n * 4, 4)].rearrange("q p k t -> p q k t"),
                              xt[p][:, :, :, :]).then_inc(xt_out[p], 16)
            rounds(act, lambda on: on(1, copy_and_store))
            for p in range(2):
                act.wait_ge(xt_out[p], 16 * GROUPS // 2)


def scan_parameters(nc, ctx, t):
    sb = lambda name, shape, dt=F32: ctx.enter_context(nc.sbuf_tensor(name, shape, dt))
    sem = lambda name: ctx.enter_context(nc.semaphore(name))
    params = sb("params_all", [128, TILES, P_ALL])
    arr = {n: sb("sp_" + n, [128, COLS]) for n in ("e1", "e2", "dt", "dth", "gam", "a", "off", "ang", "m", "m2", "r")}
    a_hi = sb("sp_a_hi", [128, COLS], F32R)
    omd = sb("sp_omd", [128, COLS + HEADS])
    dt_bias = sb("dt_bias", [128, HEADS])
    a_neg = sb("a_neg", [128, HEADS])
    pp = [ctx.enter_context(nc.psum_tensor(f"p_sp{k}", [128, COLS])) for k in range(4)]
    small_in, act_done, dve_done, pe_done, out_done = (
        sem("small_in"), sem("sp_act"), sem("sp_dve"), sem("sp_pe"), sem("sp_out"))
    as3 = lambda ap: ap.rearrange("p (t h) -> p t h", h=HEADS)
    col = lambda at: params[:, :, at:at + HEADS]
    with nc.Block() as block:
        @block.sync
        def _(sp):
            sp.dma_start(dt_bias[:, :], t["dt_bias"].partition_broadcast(128)).then_inc(small_in, 16)
            sp.dma_start(a_neg[:, :], t["A_log"].partition_broadcast(128)).then_inc(small_in, 16)
            sp.wait_ge(dve_done, 6)
            sp.dma_start(t["params_dram"], params[:, :, :]).then_inc(out_done, 16)
            sp.wait_ge(out_done, 16)

        @block.vector
        def _(dve):
            v_ = nc.vector
            scal = t["scal"]
            dve.wait_ge(small_in, 32)
            v_.tensor_tensor(as3(arr["dt"][:, :]), scal[:, :, 0:8],
                             dt_bias[:, :].unsqueeze(1).broadcast_to([128, TILES, HEADS]), ALU.add)
            v_.memset(omd[:, COLS:COLS + HEADS], 0.0)
            dve.drain()
            v_.scalar_tensor_tensor(out=arr["m"][:, :], in0=arr["dt"][:, :], scalar=-1.0, in1=arr["dt"][:, :],
                                    op0=ALU.mult, op1=ALU.max).then_inc(dve_done, 1)
            dve.wait_ge(act_done, 1)
            v_.scalar_tensor_tensor(out=arr["dt"][:, :], in0=arr["dt"][:, :], scalar=0.0, in1=arr["e1"][:, :],
                                    op0=ALU.max, op1=ALU.add)
            v_.tensor_scalar(arr["e2"][:, :], arr["e2"][:, :], 1.0, None, ALU.add)
            v_.tensor_scalar(a_neg[:, :], a_neg[:, :], -1.0, None, ALU.mult)
            dve.drain()
            v_.reciprocal(arr["m2"][:, :], arr["e2"][:, :])
            v_.tensor_tensor(as3(arr["dth"][:, :]), as3(arr["dt"][:, :]), scal[:, :, 16:24], ALU.mult)
            v_.tensor_tensor(as3(arr["a"][:, :]), as3(arr["dt"][:, :]),
                             a_neg[:, :].unsqueeze(1).broadcast_to([128, TILES, HEADS]), ALU.mult)
            dve.drain()
            v_.tensor_tensor(arr["gam"][:, :], arr["m2"][:, :], arr["dt"][:, :], ALU.mult)
            v_.tensor_scalar(arr["m2"][:, :], arr["m2"][:, :], -1.0, 1.0, ALU.mult, ALU.add)
            v_.tensor_copy(a_hi[:, :], arr["a"][:, :])
            dve.drain()
            v_.tensor_copy(col(P_A), as3(a_hi[:, :].bitcast(F32)))
            v_.tensor_tensor(col(P_A + HEADS), as3(arr["a"][:, :]), as3(a_hi[:, :].bitcast(F32)), ALU.subtract)
            v_.tensor_tensor(omd[:, 0:COLS], arr["m2"][:, :], arr["dt"][:, :], ALU.mult)
            dve.drain().then_inc(dve_done, 1)
            dve.wait_ge(pe_done, 1)
            off4 = arr["off"][:, :].rearrange("p (b c h) -> p b c h", b=BATCH, c=CHUNKS)
            tot4 = arr["r"][:, :].rearrange("p (b c h) -> p b c h", b=BATCH, c=CHUNKS)
            v_.memset(off4[:, :, 0, :], 0.0)
            v_.tensor_copy(arr["r"][:, :], pp[1][:, :])
            for c in range(1, CHUNKS):
                dve.drain()
                v_.tensor_tensor(off4[:, :, c, :], off4[:, :, c - 1, :], tot4[:, :, c - 1, :], ALU.add)
            dve.drain()
            v_.tensor_tensor(arr["ang"][:, :], arr["off"][:, :], pp[0][:, :], ALU.add)
            v_.tensor_tensor(arr["e1"][:, :], arr["gam"][:, :], pp[2][:, :], ALU.add)
            dve.drain().then_inc(dve_done, 1)
            v_.tensor_scalar(arr["e2"][:, :], arr["e1"][:, :], 1e-30, None, ALU.max)
            v_.tensor_copy(col(P_G), as3(arr["e1"][:, :]))
            dve.drain()
            v_.reciprocal(arr["e1"][:, :], arr["e2"][:, :])
            dve.drain()
            v_.tensor_tensor(col(P_RHO), as3(arr["gam"][:, :]), as3(arr["e1"][:, :]), ALU.mult)
            for shift, r in ((0.0, "r"), (0.25, "m")):
                m = arr["m2"]
                v_.tensor_scalar(m[:, :], arr["ang"][:, :], 1.0 / (2.0 * np.pi), shift, ALU.mult, ALU.add)
                dve.drain()
                v_.tensor_scalar(m[:, :], m[:, :], ROUND, None, ALU.add)
                dve.drain()
                v_.tensor_scalar(m[:, :], m[:, :], ROUND, None, ALU.subtract)
                dve.drain()
                v_.scalar_tensor_tensor(out=arr[r][:, :], in0=m[:, :], scalar=-TWO_PI_HI, in1=arr["ang"][:, :],
                                        op0=ALU.mult, op1=ALU.add)
                dve.drain()
                v_.scalar_tensor_tensor(out=arr[r][:, :], in0=m[:, :], scalar=-TWO_PI_LO, in1=arr[r][:, :],
                                        op0=ALU.mult, op1=ALU.add)
                dve.drain()
                if shift:
                    v_.tensor_scalar(arr[r][:, :], arr[r][:, :], 2.0 * np.pi * shift, None, ALU.add)
                    dve.drain()
                v_.tensor_scalar(arr[r][:, :], arr[r][:, :], SIN_LIMIT, -SIN_LIMIT, ALU.min, ALU.max)
                dve.drain()
            dve.drain().then_inc(dve_done, 1)
            dve.wait_ge(act_done, 2)
            pair = params[:, :, P_SIN:P_SIN + 16].rearrange("p t (h s) -> p t h s", s=2)
            v_.tensor_copy(col(P_COS), as3(arr["gam"][:, :]))
            v_.tensor_copy(pair[:, :, :, 1], as3(arr["off"][:, :]))
            v_.tensor_scalar(pair[:, :, :, 0], as3(arr["off"][:, :]), -1.0, None, ALU.mult)
            dve.drain().then_inc(dve_done, 1)
            dve.wait_ge(act_done, 3)
            by_seq = params[:, :, :].rearrange("p (b c) n -> p b c n", b=BATCH)
            v_.memset(by_seq[:, :, 0, P_EL:P_ALL], 0.0).then_inc(dve_done, 1)

        @block.scalar
        def _(act):
            s_ = nc.scalar
            act.wait_ge(dve_done, 1)
            s_.activation(arr["e1"][:, :], arr["m"][:, :], ACT.Exp, scale=-1.0)
            s_.activation(as3(arr["e2"][:, :]), t["scal"][:, :, 8:16], ACT.Exp, scale=-1.0)
            s_.activation(a_neg[:, :], a_neg[:, :], ACT.Exp)
            act.drain()
            s_.activation(arr["e1"][:, :], arr["e1"][:, :], ACT.Ln, bias=1.0)
            act.drain().then_inc(act_done, 1)
            act.wait_ge(dve_done, 4)
            s_.activation(arr["off"][:, :], arr["r"][:, :], ACT.Sin)
            s_.activation(arr["gam"][:, :], arr["m"][:, :], ACT.Sin)
            act.drain().then_inc(act_done, 1)
            act.wait_ge(pe_done, 2)
            s_.activation(col(P_EL), as3(pp[0][:, :]), ACT.Exp)
            s_.activation(col(P_W), as3(pp[1][:, :]), ACT.Exp)
            s_.activation(col(P_ET), as3(pp[3][:, :]), ACT.Exp)
            act.drain().then_inc(act_done, 1)

        @block.tensor
        def _(pe):
            pe.wait_ge(dve_done, 2)
            for half in range(2):
                c = slice(half * 512, half * 512 + 512)
                c1 = slice(half * 512 + HEADS, half * 512 + 512 + HEADS)
                nc.tensor.matmul(pp[0][:, c], t["upto"][:, :], arr["dth"][:, c], start=True, stop=True)
                nc.tensor.matmul(pp[1][:, c], t["ones"][:, :], arr["dth"][:, c], start=True, stop=True)
                nc.tensor.matmul(pp[2][:, c], t["nxt"][:, :], omd[:, c], start=True, stop=False)
                last = nc.tensor.matmul(pp[2][:, c], t["wrap"][:, :], omd[:, c1], start=False, stop=True)
            last.then_inc(pe_done, 1)
            pe.wait_ge(dve_done, 3)
            for half in range(2):
                c = slice(half * 512, half * 512 + 512)
                nc.tensor.matmul(pp[0][:, c], t["upto"][:, :], arr["a"][:, c], start=True, stop=True)
                nc.tensor.matmul(pp[1][:, c], t["after"][:, :], arr["a"][:, c], start=True, stop=True)
                last = nc.tensor.matmul(pp[3][:, c], t["ones"][:, :], arr["a"][:, c], start=True, stop=True)
            last.then_inc(pe_done, 1)


def long_filter(nc, ctx, t):
    sb = lambda name, shape, dt=F32: ctx.enter_context(nc.sbuf_tensor(name, shape, dt))
    sem = lambda name: ctx.enter_context(nc.semaphore(name))
    HALF = SEQ // 2
    pos = sb("pos", [3, SEQ])
    w1, w2, w3 = sb("mlp_w1", [3, FILT]), sb("mlp_w2", [FILT, FILT]), sb("mlp_w3", [FILT, FILT])
    wo = sb("mlp_wo", [FILT, DIM])
    freq_b = sb("freq_b", [FILT, 4])
    decay = sb("decay", [128, KT, SEQ])
    h, r, m = sb("mlp_h", [FILT, SEQ]), sb("mlp_r", [FILT, SEQ]), sb("mlp_m", [FILT, SEQ])
    taps = sb("taps", [128, KT, TOK - 1 + SEQ])
    ph = ctx.enter_context(nc.psum_tensor("p_mlp", [128, SEQ]))
    f_in, f_pe, f_dve, f_act, f_out = sem("f_in"), sem("f_pe"), sem("f_dve"), sem("f_act"), sem("f_out")
    with nc.Block() as block:
        @block.sync
        def _(sp):
            loads = [(pos[:, :], t["pos"]), (w1[:, :], t["mlp_w1"]), (w2[:, :], t["mlp_w2"]), (w3[:, :], t["mlp_w3"]),
                     (wo[:, :], t["mlp_wo"]), (freq_b[:, :], t["freq_b"]),
                     (decay[:, :, :], t["decay"].rearrange("(k p) n -> p k n", p=128))]
            for dst, src in loads:
                sp.dma_start(dst, src).then_inc(f_in, 16)
            sp.wait_ge(f_dve, 2 * 5)
            sp.dma_start(t["taps_dram"].rearrange("(k p) n -> p k n", p=128), taps[:, :, :]).then_inc(f_out, 16)
            sp.wait_ge(f_out, 16)

        @block.tensor
        def _(pe):
            pe.wait_ge(f_in, 16 * 7)
            for layer, (w, src) in enumerate(((w1, pos), (w2, h), (w3, h))):
                for half in range(2):
                    wait(pe, f_act, 2 * layer + half - 1)
                    for q in range(2):
                        c = slice(half * HALF + q * 512, half * HALF + (q + 1) * 512)
                        last = nc.tensor.matmul(ph[0:FILT, c], w[:, :], src[:, c], start=True, stop=True)
                    last.then_inc(f_pe, 1)
            for k in range(KT):
                for half in range(2):
                    if k == 0:
                        pe.wait_ge(f_act, 5 + half)
                    else:
                        pe.wait_ge(f_dve, 7 + half)
                    for q in range(2):
                        c = slice(half * HALF + q * 512, half * HALF + (q + 1) * 512)
                        last = nc.tensor.matmul(ph[:, c], wo[:, k * 128:(k + 1) * 128], h[:, c], start=True, stop=True)
                    last.then_inc(f_pe, 1)

        @block.vector
        def _(dve):
            v_ = nc.vector
            v_.memset(taps[:, :, 0:TOK - 1], 0.0)
            dve.wait_ge(f_in, 16 * 7)
            for layer in range(3):
                for half in range(2):
                    c = slice(half * HALF, (half + 1) * HALF)
                    dve.wait_ge(f_pe, 2 * layer + half + 1)
                    v_.tensor_scalar(r[:, c], ph[0:FILT, c], freq_b[:, layer + 1:layer + 2], freq_b[:, 0:1], ALU.add, ALU.mult)
                    dve.drain()
                    v_.tensor_scalar(m[:, c], r[:, c], 1.0 / (2.0 * np.pi), None, ALU.mult)
                    dve.drain()
                    v_.tensor_scalar(m[:, c], m[:, c], ROUND, None, ALU.add)
                    dve.drain()
                    v_.tensor_scalar(m[:, c], m[:, c], ROUND, None, ALU.subtract)
                    dve.drain()
                    v_.scalar_tensor_tensor(out=r[:, c], in0=m[:, c], scalar=-TWO_PI_HI, in1=r[:, c], op0=ALU.mult, op1=ALU.add)
                    dve.drain()
                    v_.scalar_tensor_tensor(out=r[:, c], in0=m[:, c], scalar=-TWO_PI_LO, in1=r[:, c], op0=ALU.mult, op1=ALU.add)
                    dve.drain()
                    v_.tensor_scalar(r[:, c], r[:, c], SIN_LIMIT, -SIN_LIMIT, ALU.min, ALU.max)
                    dve.drain().then_inc(f_dve, 1)
            for k in range(KT):
                for half in range(2):
                    c = slice(half * HALF, (half + 1) * HALF)
                    dve.wait_ge(f_pe, 6 + 2 * k + half + 1)
                    v_.tensor_tensor(taps[:, k, TOK - 1 + half * HALF:TOK - 1 + (half + 1) * HALF], decay[:, k, c], ph[:, c], ALU.mult)
                    dve.drain().then_inc(f_dve, 1)

        @block.scalar
        def _(act):
            for step in range(6):
                c = slice(step % 2 * HALF, (step % 2 + 1) * HALF)
                act.wait_ge(f_dve, step + 1)
                nc.scalar.activation(h[:, c], r[:, c], ACT.Sin).then_inc(f_act, 1)


def mixer_and_first_ffn(nc, ctx, t):
    sb = lambda name, shape, dt=F32: ctx.enter_context(nc.sbuf_tensor(name, shape, dt))
    W4 = GROUP * STATE
    H64 = GROUP * HEAD_U
    ident, ident_b, upto, after, mask = t["ident"], t["ident_b"], t["upto"], t["after"], t["mask"]
    w_u, w_bc = [sb(f"w_u{p}", [128, KT, 512], F32R) for p in range(2)], [sb(f"w_bc{p}", [128, KT, 2048], F32R) for p in range(2)]
    after_r = sb("after_r", [128, 128], F32R)
    w_out, rms_w = sb("w_out", [128, 4, DIM]), sb("rms_w", [128, 4])
    in_w, in_b, short = sb("in_w", [128, KT, INNER]), sb("in_b", [128, 6]), sb("short", [128, 6, 4])
    first_tap_b = sb("first_tap_b", [128, 6])
    w_r, w_k, w_v, mu = t["w_r_sb"], t["w_k_sb"], t["w_v_sb"], t["mu_sb"]
    stage = sb("stage", [128, KT, 2560])
    keep = sb("keep", [128, TILES + 1])
    rms_eps = sb("rms_eps", [128, 1])
    xnT_raw = sb("xnT_raw", [128, KT, TOK])
    xnT = [sb(f"xnT{p}", [128, KT, TOK], F32R) for p in range(2)]
    early = sb("par_early", [128, P_EARLY])
    late = sb("par_late", [128, P_ALL - P_EARLY])
    rot1 = [sb(f"rot1_{k}", [128, W4]) for k in range(2)]
    rot2 = [sb(f"rot2_{k}", [128, W4]) for k in range(2)]
    turned = [[sb(f"turned_{g}{k}", [128, W4]) for k in range(2)] for g in range(2)]
    turned_t = [[sb(f"turned_t{g}{k}", [128, W4]) for k in range(2)] for g in range(2)]
    steps = [sb(f"steps{p}", [128, W4], F32R) for p in range(2)]
    decay, own, mix = ([sb(f"{what}{g}", [128, W4]) for g in range(2)] for what in ("decay", "own", "mix"))
    u_g, u_w, state = sb("u_g", [128, 512]), sb("u_w", [128, 512]), sb("state", [128, 512])
    y_from, y = [sb(f"y_from{g}", [128, H64]) for g in range(2)], sb("y", [128, 512])
    y_sq, mean_sq, ms_eps, y_rstd = sb("y_sq", [128, 512]), sb("mean_sq", [128, 1]), sb("ms_eps", [128, 1]), sb("y_rstd", [128, 1])
    yT = sb("yT", [128, 512])
    x_in, x1, x2 = sb("x_in", [128, DIM]), sb("x1", [128, DIM]), sb("x2", [128, DIM])
    xn = [sb(f"xn_{n}", [128, DIM]) for n in "12"]
    stats, mean_var, var_eps, rstd = ([sb(f"{what}_{n}", [128, w]) for n in "12"] for what, w in
                                      (("stats", 6), ("mean_var", 2), ("var_eps", 1), ("rstd", 1)))
    xT = sb("xT", [128, KT, TOK + 1])
    dx, x_r, x_k = sb("dx", [128, KT, TOK]), sb("x_r", [128, KT, TOK]), sb("x_k", [128, KT, TOK])
    tanh_r, k_pos, k_sq, gated = sb("tanh_r", [128, DIM]), sb("k_pos", [128, 256]), sb("k_sq", [128, KT, TOK]), sb("gated", [128, DIM])
    x2T = sb("x2T", [128, KT, TOK])
    up = sb("up", [128, 6, TOK + 2])
    conv = sb("conv", [128, 6, TOK])
    vx = sb("vx", [128, KT, TOK])
    bank = [ctx.enter_context(nc.psum_tensor(f"bank{k}", [128, 512], F32)) for k in range(8)]
    p_bc, p_tr, p_arg, p_gram, p_y, p_post = bank[0:2], bank[2:4], bank[4], bank[5], bank[6], bank[7]
    p_state = p_arg

    names = ("project_b0 project_b1 project_c0 project_c1 rotate_b0 rotate_b1 rotate_c0 rotate_c1 turn_b0 turn_b1 turn_c0 turn_c1 "
             "over_b0 over_b1 over_c0 over_c1 copy_b0 copy_b1 copy_c0 copy_c1 steps0 steps1 logs0 logs1 exp0 exp1 own0 own1 "
             "values gate_values gram0 gram1 mix0 mix1 outputs0 outputs1 take_y0 take_y1 weigh_values new_state fade carry_state "
             "split_hi split_rest y_over copy_yT square_y scan_rstd project_out residual1 rstd1 norm1 xn_over copy_xT shift_mix "
             "receptance_key r_and_k value residual2 rstd2 norm2 x2n_over copy_x2T widen0 widen1 take_up0 take_up1 carry_up short_filter "
             "weights_in setup w_hi w_scaled load_xnT load_early load_late load_x store_x2 store_x0 store_vx").split()
    s = {n: ctx.enter_context(nc.semaphore(n)) for n in names}

    def wait_for(eng, step, i):
        each = 16 if step.startswith(("load", "store")) else 1
        wait(eng, s[step], min(i + 1, TILES) * each if isinstance(i, int) else (i + 1) * each)

    BANK_4 = (("logs0", 0, "exp0"), ("new_state", 1, "carry_state"), ("logs1", 0, "exp1"))
    BANK_5 = (("gram0", 1, "mix0"), ("gram1", 1, "mix1"), ("values", 0, "gate_values"))
    BANK_7 = (("widen1", 4, "take_up1"), ("xn_over", 3, "copy_xT"), ("receptance_key", 3, "r_and_k"), ("y_over", 2, "copy_yT"),
              ("value", 3, "residual2"), ("project_out", 2, "residual1"), ("x2n_over", 3, "copy_x2T"), ("widen0", 3, "take_up0"))

    def bank_read(eng, bank, step, i):
        at = [name for name, _, _ in bank].index(step)
        lag = bank[at][1]
        if isinstance(i, int):
            for n, (name, other, reader) in enumerate(bank):
                if name != step:
                    wait_for(eng, reader, i + lag - other - (1 if n > at else 0))
        else:
            _, other, reader = bank[at - 1]
            wait_for(eng, reader, i + (lag - other - (0 if at else 1)))
    BC = "bc"
    heads = lambda ap: ap.rearrange("p (h n) -> p h n", h=GROUP)
    all_heads = lambda ap: ap.rearrange("p (h n) -> p h n", h=HEADS)
    group_of = lambda ap, g: ap[:, g * GROUP:(g + 1) * GROUP]
    e_col = lambda at: early[:, at:at + HEADS]
    l_col = lambda at: late[:, at - P_EARLY:at - P_EARLY + HEADS]
    halves = lambda ap: ap.rearrange("p (k n) -> p k n", k=KT)
    SPLIT = [(p, q, k) for p, q in ((1, 0), (0, 1), (0, 0)) for k in range(KT)]

    LAGS = 4

    def rounds(eng, body):
        def some(it):
            def on(lag, step, *args):
                if 0 <= it - lag < TILES:
                    step(it - lag, *args)
            return on
        for it in range(LAGS + 1):
            body(some(it))
        with eng.Fori(LAGS + 1, TILES) as it:
            body(lambda lag, step, *args: step(it - lag if lag else it, *args))
        for it in range(TILES, TILES + LAGS):
            body(some(it))

    with nc.Block() as block:
        @block.sync
        def _(sp):
            by_k = lambda name: t[name].rearrange("(k p) n -> p k n", p=128)
            for dst, src in ((stage[:, :, 0:2048], by_k("w_bc")), (stage[:, :, 2048:2560], by_k("w_u")), (w_out[:, :, :], by_k("w_out")),
                             (rms_w[:, :], t["rms_w"]), (in_b[:, :], t["in_b"]), (short[:, :, :], t["short"]), (mu[:, :, :], t["mu"]),
                             (in_w[:, :, :], by_k("in_w")), (w_r[:, :, :], by_k("w_r")), (w_k[:, :, :], by_k("w_k")), (w_v[:, :, :], by_k("w_v"))):
                sp.dma_start(dst, src).then_inc(s["weights_in"], 16)
            at = lambda n: n if isinstance(n, int) else sp.snap(n)
            flat = {n: t[n].rearrange(how) for n, how in (
                ("x", "r c -> (r c)"), ("x2_dram", "r c -> (r c)"), ("xnT_dram", "t p k n -> (t p k n)"),
                ("params_dram", "p t n -> p (t n)"))}
            flat |= {n: t[n].rearrange("(k p) t n -> p k (t n)", p=128) for n in ("x0T_dram", "vxT_dram")}

            def load_xnT(i):
                block_at, this = at(i * (TOK * DIM)), at(i * 1)
                wait(sp, s["split_rest"], this)
                sp.dma_start(xnT_raw[:, :, :], flat["xnT_dram"][bass.ds(block_at, TOK * DIM)]
                             .rearrange("(p k n) -> p k n", p=128, k=KT)).then_inc(s["load_xnT"], 16)

            def load_early(i):
                early_at, this = at(i * P_ALL), at(i * 1)
                for user in ("turn_b0", "turn_c0", "turn_b1", "turn_c1", "steps0", "steps1"):
                    wait(sp, s[user], this)
                sp.dma_start(early[:, :], flat["params_dram"][:, bass.ds(early_at, P_EARLY)]).then_inc(s["load_early"], 16)

            def load_late(i):
                late_at, this = at(i * P_ALL + P_EARLY), at(i * 1)
                wait(sp, s["carry_state"], this)
                wait(sp, s["take_y1"], this)
                sp.dma_start(late[:, :], flat["params_dram"][:, bass.ds(late_at, P_ALL - P_EARLY)]).then_inc(s["load_late"], 16)

            def load_x(j):
                block_at, this = at(j * (TOK * DIM)), at(j * 1)
                wait(sp, s["residual1"], this)
                sp.dma_start(x_in[:, :], flat["x"][bass.ds(block_at, TOK * DIM)].rearrange("(p c) -> p c", p=TOK)).then_inc(s["load_x"], 16)

            def store_x2(j):
                block_at, nxt = at(j * (TOK * DIM)), at(j + 1)
                wait(sp, s["residual2"], nxt)
                sp.dma_start(flat["x2_dram"][bass.ds(block_at, TOK * DIM)].rearrange("(p c) -> p c", p=TOK), x2[:, :]).then_inc(s["store_x2"], 16)

            def store_conv(j):
                tok_at, nxt = at(j * TOK), at(j + 1)
                wait(sp, s["short_filter"], nxt)
                sp.dma_start(flat["x0T_dram"][:, :, bass.ds(tok_at, TOK)], conv[:, 0:KT, :]).then_inc(s["store_x0"], 16)
                sp.dma_start(flat["vxT_dram"][:, :, bass.ds(tok_at, TOK)], vx[:, :, :]).then_inc(s["store_vx"], 16)

            def body(on):
                on(0, load_xnT)
                on(1, load_late)
                on(0, load_early)
                on(4, store_conv)
                on(2, load_x)
                on(3, store_x2)
            rounds(sp, body)
            for step in ("store_x2", "store_x0", "store_vx"):
                wait_for(sp, step, TILES - 1)

        @block.tensor
        def _(pe):
            mm, tp = nc.tensor.matmul, nc.tensor.transpose
            pe.wait_ge(s["setup"], 1)
            pe.wait_ge(s["w_scaled"], 2)

            def project_bc(i, g, c):
                wait_for(pe, "split_rest", i)
                wait_for(pe, f"rotate_{BC[c]}{1 - g}", i - 1 + g)
                for n, (p, q, k) in enumerate(SPLIT):
                    last = mm(p_bc[c][:, :], xnT[p][:, k, :], w_bc[q][:, k, c * 1024 + g * W4:c * 1024 + (g + 1) * W4],
                              start=(n == 0), stop=(n == len(SPLIT) - 1))
                last.then_inc(s[f"project_{BC[c]}{g}"], 1)

            def decay_logs(i, g):
                wait_for(pe, f"steps{g}", i)
                bank_read(pe, BANK_4, f"logs{g}", i)
                mm(p_arg[:, :], after_r[:, :], steps[0][:, :], start=True, stop=False)
                mm(p_arg[:, :], after_r[:, :], steps[1][:, :], start=False, stop=False)
                mm(p_arg[:, :], ident_b[:, :], mask[:, :].unsqueeze(1).broadcast_to([128, GROUP, TOK]),
                   start=False, stop=True).then_inc(s[f"logs{g}"], 1)

            def project_u(i):
                wait_for(pe, "split_rest", i)
                bank_read(pe, BANK_5, "values", i)
                for n, (p, q, k) in enumerate(SPLIT):
                    last = mm(p_gram[:, :], xnT[p][:, k, :], w_u[q][:, k, :], start=(n == 0), stop=(n == len(SPLIT) - 1))
                last.then_inc(s["values"], 1)

            def turn_over(i, g, c):
                wait_for(pe, f"turn_{BC[c]}{g}", i)
                wait_for(pe, f"copy_{BC[c]}{1 - g}", i - 1 + g)
                for h in range(GROUP):
                    last = tp(p_tr[c][:, h * TOK:(h + 1) * TOK], turned[g][c][:, h * STATE:(h + 1) * STATE], ident[:, :])
                last.then_inc(s[f"over_{BC[c]}{g}"], 1)

            def gram(i, g):
                wait_for(pe, f"copy_b{g}", i)
                wait_for(pe, f"copy_c{g}", i)
                bank_read(pe, BANK_5, f"gram{g}", i)
                for h in range(GROUP):
                    c = slice(h * TOK, (h + 1) * TOK)
                    last = mm(p_gram[:, c], turned_t[g][0][:, c], turned_t[g][1][:, c], start=True, stop=True)
                last.then_inc(s[f"gram{g}"], 1)

            def outputs(i, g):
                wait_for(pe, f"mix{g}", i)
                wait_for(pe, f"take_y{1 - g}", i - 1 + g)
                wait_for(pe, "carry_state", i - 1)
                for h in range(GROUP):
                    v, r = slice((g * GROUP + h) * HEAD_U, (g * GROUP + h + 1) * HEAD_U), slice(h * TOK, (h + 1) * TOK)
                    mm(p_y[:, h * HEAD_U:(h + 1) * HEAD_U], mix[g][:, r], u_g[:, v], start=True, stop=True)
                    last = mm(p_y[:, H64 + h * HEAD_U:H64 + (h + 1) * HEAD_U], turned_t[g][1][:, r], state[:, v],
                              start=True, stop=True)
                last.then_inc(s[f"outputs{g}"], 1)

            def new_state(i):
                wait_for(pe, "weigh_values", i)
                bank_read(pe, BANK_4, "new_state", i)
                for h in range(HEADS):
                    v = slice(h * HEAD_U, (h + 1) * HEAD_U)
                    last = mm(p_state[:, v], turned[h // GROUP][0][:, (h % GROUP) * STATE:(h % GROUP + 1) * STATE], u_w[:, v],
                              start=True, stop=True)
                last.then_inc(s["new_state"], 1)

            def y_over(j):
                wait_for(pe, "take_y1", j)
                bank_read(pe, BANK_7, "y_over", j)
                for k in range(4):
                    last = tp(p_post[:, k * TOK:(k + 1) * TOK], y[:, k * 128:(k + 1) * 128], ident[:, :])
                last.then_inc(s["y_over"], 1)

            def x2n_over(j):
                wait_for(pe, "norm2", j)
                bank_read(pe, BANK_7, "x2n_over", j)
                for k in range(KT):
                    last = tp(p_post[:, k * TOK:(k + 1) * TOK], xn[1][:, k * 128:(k + 1) * 128], ident[:, :])
                last.then_inc(s["x2n_over"], 1)

            def widen(j, part):
                wait_for(pe, "copy_x2T", j)
                bank_read(pe, BANK_7, f"widen{part}", j)
                for e in range(4 * part, min(4 * part + 4, 6)):
                    for k in range(KT):
                        last = mm(p_post[:, (e % 4) * TOK:(e % 4 + 1) * TOK], in_w[:, k, e * 128:(e + 1) * 128], x2T[:, k, :],
                                  start=(k == 0), stop=(k == KT - 1))
                last.then_inc(s[f"widen{part}"], 1)

            def project_out(j):
                wait_for(pe, "copy_yT", j)
                bank_read(pe, BANK_7, "project_out", j)
                for k in range(4):
                    last = mm(p_post[:, 0:DIM], yT[:, k * TOK:(k + 1) * TOK], w_out[:, k, :], start=(k == 0), stop=(k == 3))
                last.then_inc(s["project_out"], 1)

            def xn_over(j):
                wait_for(pe, "norm1", j)
                bank_read(pe, BANK_7, "xn_over", j)
                for k in range(KT):
                    last = tp(p_post[:, k * TOK:(k + 1) * TOK], xn[0][:, k * 128:(k + 1) * 128], ident[:, :])
                last.then_inc(s["xn_over"], 1)

            def receptance_key(j):
                wait_for(pe, "shift_mix", j)
                bank_read(pe, BANK_7, "receptance_key", j)
                for e in range(KT):
                    for k in range(KT):
                        mm(p_post[:, DIM + e * TOK:DIM + (e + 1) * TOK], w_k[:, k, e * 128:(e + 1) * 128], x_k[:, k, :],
                           start=(k == 0), stop=(k == KT - 1))
                for k in range(KT):
                    last = mm(p_post[:, 0:DIM], x_r[:, k, :], w_r[:, k, :], start=(k == 0), stop=(k == KT - 1))
                last.then_inc(s["receptance_key"], 1)

            def value(j):
                wait_for(pe, "r_and_k", j)
                bank_read(pe, BANK_7, "value", j)
                for k in range(KT):
                    last = mm(p_post[:, 0:DIM], k_sq[:, k, :], w_v[:, k, :], start=(k == 0), stop=(k == KT - 1))
                last.then_inc(s["value"], 1)

            def body(on):
                on(0, project_bc, 0, 1)
                on(0, project_bc, 0, 0)
                on(4, widen, 1)
                on(1, gram, 0)
                on(1, turn_over, 1, 1)
                on(1, turn_over, 1, 0)
                on(3, xn_over)
                on(0, project_bc, 1, 1)
                on(0, decay_logs, 0)
                on(1, gram, 1)
                on(3, receptance_key)
                on(1, outputs, 0)
                on(2, y_over)
                on(0, project_bc, 1, 0)
                on(3, value)
                on(1, new_state)
                on(0, turn_over, 0, 1)
                on(2, project_out)
                on(1, outputs, 1)
                on(0, turn_over, 0, 0)
                on(3, x2n_over)
                on(0, project_u)
                on(3, widen, 0)
                on(0, decay_logs, 1)
            rounds(pe, body)

        @block.scalar
        def _(act):
            s_ = nc.scalar

            def split_xnT(i):
                wait_for(act, "load_xnT", i)
                for user in ("project_b0", "project_c0", "project_b1", "project_c1", "values"):
                    wait_for(act, user, i - 1)
                s_.copy(xnT[0][:, :, :], xnT_raw[:, :, :]).then_inc(s["split_hi"], 1)

            def exponentials(i, g):
                wait_for(act, f"logs{g}", i)
                wait_for(act, f"mix{g}", i - 1)
                s_.activation(decay[g][:, :], p_arg[:, :], ACT.Exp).then_inc(s[f"exp{g}"], 1)

            def copy_turned(i, g, c):
                wait_for(act, f"over_{BC[c]}{g}", i)
                wait_for(act, f"gram{g}", i - 1)
                if c == 1:
                    wait_for(act, f"outputs{g}", i - 1)
                s_.copy(turned_t[g][c][:, :], p_tr[c][:, :]).then_inc(s[f"copy_{BC[c]}{g}"], 1)

            def square_y(j):
                wait_for(act, "take_y1", j)
                wait_for(act, "scan_rstd", j - 1)
                s_.activation(y_sq[:, :], y[:, :], ACT.Square, scale=float((HEADS * HEAD_U) ** -0.5),
                              accum_out=mean_sq[:, :]).then_inc(s["square_y"], 1)

            def copy_yT(j):
                wait_for(act, "y_over", j)
                wait_for(act, "project_out", j - 1)
                s_.copy(yT[:, :], p_post[:, :]).then_inc(s["copy_yT"], 1)

            def copy_x2T(j):
                wait_for(act, "x2n_over", j)
                wait_for(act, "widen1", j - 1)
                s_.copy(x2T[:, :, :], halves(p_post[:, 0:DIM])).then_inc(s["copy_x2T"], 1)

            def take_up(j, part):
                wait_for(act, f"widen{part}", j)
                if part == 0:
                    wait_for(act, "carry_up", j)
                    wait_for(act, "store_x0", j - 1)
                for e in range(4 * part, min(4 * part + 4, 6)):
                    column = p_post[:, (e % 4) * TOK:(e % 4 + 1) * TOK]
                    s_.activation(conv[:, e, :], column, ACT.Identity, scale=short[:, e, 2:3], bias=first_tap_b[:, e:e + 1])
                    last = s_.activation(up[:, e, 2:TOK + 2], column, ACT.Identity, bias=in_b[:, e:e + 1])
                last.then_inc(s[f"take_up{part}"], 1)

            def copy_xT(j):
                wait_for(act, "xn_over", j)
                s_.copy(xT[:, :, 1:TOK + 1], halves(p_post[:, 0:DIM])).then_inc(s["copy_xT"], 1)

            def r_and_k(j):
                wait_for(act, "receptance_key", j)
                wait_for(act, "value", j - 1)
                wait_for(act, "residual2", j - 1)
                s_.activation(k_pos[:, :], p_post[:, DIM:512], ACT.Relu)
                act.drain()
                s_.activation(k_sq[:, :, :], halves(k_pos[:, :]), ACT.Square)
                s_.activation(tanh_r[:, :], p_post[:, 0:DIM], ACT.Tanh, scale=0.5).then_inc(s["r_and_k"], 1)

            act.wait_ge(s["weights_in"], 16 * 11)
            s_.copy(w_bc[0][:, :, :], stage[:, :, 0:2048])
            s_.copy(w_u[0][:, :, :], stage[:, :, 2048:2560])
            act.drain().then_inc(s["w_hi"], 1)

            def body(on):
                on(0, split_xnT)
                on(4, take_up, 0)
                on(4, take_up, 1)
                on(1, exponentials, 1)
                on(3, copy_xT)
                on(1, copy_turned, 1, 0)
                on(1, copy_turned, 1, 1)
                on(2, square_y)
                on(3, r_and_k)
                on(0, exponentials, 0)
                on(2, copy_yT)
                on(0, copy_turned, 0, 1)
                on(3, copy_x2T)
                on(0, copy_turned, 0, 0)
            rounds(act, body)

        @block.gpsimd
        def _(pool):
            g_ = nc.gpsimd
            g_.memset(state[:, :], 0.0)
            g_.memset(xT[:, :, :], 0.0)
            g_.memset(up[:, :, :], 0.0)
            g_.memset(keep[:, :], 1.0)
            g_.memset(rms_eps[:, :], RMS_EPS)
            pool.drain()
            g_.memset(keep[:, 0:TILES].rearrange("p (b c) -> p b c", b=BATCH)[:, :, 0], 0.0)
            pool.drain().then_inc(s["setup"], 1)
            pool.wait_ge(s["weights_in"], 16 * 11)
            for k in range(4):
                g_.tensor_scalar(w_out[:, k, :], w_out[:, k, :], rms_w[:, k:k + 1], None, ALU.mult)
            g_.tensor_copy(after_r[:, :], after[:, :])
            g_.tensor_tensor(first_tap_b[:, :], short[:, :, 2], in_b[:, :], ALU.mult)
            pool.drain()
            g_.tensor_tensor(first_tap_b[:, :], first_tap_b[:, :], short[:, :, 3], ALU.add)
            pool.drain().then_inc(s["w_scaled"], 1)

            def split_xnT(i):
                wait_for(pool, "split_hi", i)
                g_.tensor_tensor(xnT[1][:, :, :], xnT_raw[:, :, :], xnT[0][:, :, :].bitcast(F32), ALU.subtract).then_inc(s["split_rest"], 1)

            def masked_steps(i, g):
                wait_for(pool, "load_early", i)
                wait_for(pool, f"logs{1 - g}", i - 1 + g)
                for p in range(2):
                    last = g_.tensor_tensor(heads(steps[p][:, :]), upto[:, :].unsqueeze(1).broadcast_to([128, GROUP, TOK]),
                                            over(group_of(e_col(P_A + p * HEADS), g), TOK), ALU.mult)
                last.then_inc(s[f"steps{g}"], 1)

            def add_turned(i, g, c):
                wait_for(pool, f"rotate_{BC[c]}{g}", i)
                wait_for(pool, f"over_{BC[c]}{g}", i - 1)
                if c == 0:
                    wait_for(pool, "new_state", i - 1)
                g_.tensor_tensor(turned[g][c][:, :], rot1[c][:, :], rot2[c][:, :], ALU.add).then_inc(s[f"turn_{BC[c]}{g}"], 1)

            def own_diagonal(i, g):
                wait_for(pool, "load_late", i)
                g_.tensor_tensor(heads(own[g][:, :]), ident[:, :].unsqueeze(1).broadcast_to([128, GROUP, TOK]),
                                 over(group_of(l_col(P_RHO), g), TOK), ALU.mult)

            def add_own(i, g):
                pool.drain()
                wait_for(pool, f"exp{g}", i)
                g_.tensor_tensor(decay[g][:, :], decay[g][:, :], own[g][:, :], ALU.add).then_inc(s[f"own{g}"], 1)

            def decay_values(i):
                wait_for(pool, "gate_values", i)
                wait_for(pool, "new_state", i - 1)
                g_.tensor_tensor(all_heads(u_w[:, :]), all_heads(u_g[:, :]), over(l_col(P_W), HEAD_U), ALU.mult).then_inc(s["weigh_values"], 1)

            def fade_state(i):
                wait_for(pool, "outputs1", i)
                g_.tensor_tensor(all_heads(state[:, :]), all_heads(state[:, :]), over(l_col(P_ET), HEAD_U), ALU.mult).then_inc(s["fade"], 1)

            def scan_rstd(j):
                wait_for(pool, "square_y", j)
                wait_for(pool, "residual1", j - 1)
                g_.tensor_tensor(ms_eps[:, :], mean_sq[:, :], rms_eps[:, :], ALU.add)
                pool.drain()
                g_.tensor_tensor(y_rstd[:, :], ms_eps[:, :], t["minus_half"][:, 0:1], ALU.pow).then_inc(s["scan_rstd"], 1)

            def layer_rstd(j, n):
                wait_for(pool, f"residual{n}", j)
                g_.tensor_tensor(rstd[n - 1][:, :], var_eps[n - 1][:, :], t["minus_half"][:, 0:1], ALU.pow).then_inc(s[f"rstd{n}"], 1)

            def body(on):
                on(0, split_xnT)
                on(1, own_diagonal, 0)
                on(1, add_own, 0)
                on(0, masked_steps, 0)
                on(1, own_diagonal, 1)
                on(0, add_turned, 0, 1)
                on(1, decay_values)
                on(2, scan_rstd)
                on(0, masked_steps, 1)
                on(1, add_own, 1)
                on(3, layer_rstd, 2)
                on(0, add_turned, 0, 0)
                on(0, add_turned, 1, 1)
                on(1, fade_state)
                on(2, layer_rstd, 1)
                on(0, add_turned, 1, 0)
            rounds(pool, body)

        @block.vector
        def _(dve):
            v_ = nc.vector

            def rotate(i, g, c):
                cos = over(group_of(e_col(P_COS), g), STATE)
                sin = early[:, P_SIN + 2 * g * GROUP:P_SIN + 2 * (g + 1) * GROUP]
                parts = lambda ap: ap.rearrange("p (h s n) -> p h s n", h=GROUP, s=2)
                wait_for(dve, "load_early", i)
                wait_for(dve, f"project_{BC[c]}{g}", i)
                wait_for(dve, f"turn_{BC[c]}{1 - g}", i - 1 + g)
                v_.tensor_tensor(heads(rot1[c][:, :]), heads(p_bc[c][:, :]), cos, ALU.mult)
                v_.tensor_tensor(parts(rot2[c][:, :]), parts(p_bc[c][:, :])[:, :, ::-1, :],
                                 over(sin.rearrange("p (h s) -> p h s", s=2), STATE // 2), ALU.mult).then_inc(s[f"rotate_{BC[c]}{g}"], 1)

            def gate_values(i):
                wait_for(dve, "values", i)
                wait_for(dve, "load_late", i)
                wait_for(dve, "weigh_values", i - 1)
                wait_for(dve, "outputs1", i - 1)
                v_.tensor_tensor(all_heads(u_g[:, :]), all_heads(p_gram[:, :]), over(l_col(P_G), HEAD_U), ALU.mult).then_inc(s["gate_values"], 1)

            def weigh_gram(i, g):
                wait_for(dve, f"gram{g}", i)
                wait_for(dve, f"own{g}", i)
                wait_for(dve, f"outputs{g}", i - 1)
                v_.tensor_tensor(mix[g][:, :], p_gram[:, :], decay[g][:, :], ALU.mult).then_inc(s[f"mix{g}"], 1)

            def take_y(i, g):
                wait_for(dve, f"outputs{g}", i)
                if g == 0:
                    wait_for(dve, "y_over", i - 1)
                    wait_for(dve, "square_y", i - 1)
                v_.tensor_tensor(heads(y_from[g][:, :]), heads(p_y[:, H64:]), over(group_of(l_col(P_EL), g), HEAD_U), ALU.mult)
                dve.drain()
                v_.tensor_tensor(y[:, g * H64:(g + 1) * H64], p_y[:, 0:H64], y_from[g][:, :], ALU.add).then_inc(s[f"take_y{g}"], 1)

            def carry_state(i):
                wait_for(dve, "fade", i)
                wait_for(dve, "new_state", i)
                v_.tensor_tensor(state[:, :], p_state[:, :], state[:, :], ALU.add).then_inc(s["carry_state"], 1)

            def norm(src, n):
                v_.bn_stats(stats[n - 1][:, :], src)
                dve.drain()
                v_.bn_aggr(mean_var[n - 1][:, :], stats[n - 1][:, :])
                dve.drain()
                v_.tensor_scalar(var_eps[n - 1][:, :], mean_var[n - 1][:, 1:2], LN_EPS, None, ALU.add).then_inc(s[f"residual{n}"], 1)

            def normalised(j, src, n):
                wait_for(dve, f"rstd{n}", j)
                wait_for(dve, "xn_over" if n == 1 else "x2n_over", j - 1)
                v_.tensor_scalar(xn[n - 1][:, :], src, mean_var[n - 1][:, 0:1], rstd[n - 1][:, :],
                                 ALU.subtract, ALU.mult).then_inc(s[f"norm{n}"], 1)

            def residual1(j):
                wait_for(dve, "project_out", j)
                wait_for(dve, "scan_rstd", j)
                wait_for(dve, "load_x", j)
                v_.scalar_tensor_tensor(out=x1[:, :], in0=p_post[:, 0:DIM], scalar=y_rstd[:, :], in1=x_in[:, :],
                                        op0=ALU.mult, op1=ALU.add)
                v_.tensor_scalar(xT[:, :, 0], xT[:, :, TOK], keep[:, bass.ds(j, 1)], None, ALU.mult)
                dve.drain()
                norm(x1[:, :], 1)

            def shift_mix(j):
                wait_for(dve, "copy_xT", j)
                wait_for(dve, "receptance_key", j - 1)
                v_.tensor_tensor(dx[:, :, :], xT[:, :, 1:TOK + 1], xT[:, :, 0:TOK], ALU.subtract)
                dve.drain()
                for k in range(KT):
                    for which, dst in enumerate((x_r, x_k)):
                        last = v_.scalar_tensor_tensor(out=dst[:, k, :], in0=dx[:, k, :], scalar=mu[:, which, k:k + 1],
                                                       in1=xT[:, k, 0:TOK], op0=ALU.mult, op1=ALU.add)
                last.then_inc(s["shift_mix"], 1)

            def residual2(j):
                wait_for(dve, "value", j)
                wait_for(dve, "r_and_k", j)
                v_.scalar_tensor_tensor(out=gated[:, :], in0=tanh_r[:, :], scalar=1.0, in1=p_post[:, 0:DIM], op0=ALU.add, op1=ALU.mult)
                dve.drain()
                wait_for(dve, "store_x2", j - 1)
                v_.scalar_tensor_tensor(out=x2[:, :], in0=gated[:, :], scalar=0.5, in1=x1[:, :], op0=ALU.mult, op1=ALU.add)
                dve.drain()
                norm(x2[:, :], 2)

            def short_filter(j):
                wait_for(dve, "take_up0", j)
                wait_for(dve, "take_up1", j)
                wait_for(dve, "store_vx", j - 1)
                for tap in (1, 0):
                    for e in range(6):
                        v_.scalar_tensor_tensor(out=conv[:, e, :], in0=up[:, e, tap:TOK + tap], scalar=short[:, e, tap:tap + 1],
                                                in1=conv[:, e, :], op0=ALU.mult, op1=ALU.add)
                    dve.drain()
                v_.tensor_tensor(vx[:, :, ::-1], conv[:, 4:6, :], conv[:, 2:4, :], ALU.mult).then_inc(s["short_filter"], 1)

            def carry_up(j):
                v_.tensor_scalar(up[:, :, 0:2], up[:, :, TOK:TOK + 2], keep[:, bass.ds(j, 1)], None, ALU.mult).then_inc(s["carry_up"], 1)

            dve.wait_ge(s["weights_in"], 16 * 11)
            dve.wait_ge(s["setup"], 1)
            dve.wait_ge(s["w_hi"], 1)
            v_.tensor_tensor(w_bc[1][:, :, :], stage[:, :, 0:2048], w_bc[0][:, :, :].bitcast(F32), ALU.subtract)
            v_.tensor_tensor(w_u[1][:, :, :], stage[:, :, 2048:2560], w_u[0][:, :, :].bitcast(F32), ALU.subtract)
            dve.drain().then_inc(s["w_scaled"], 1)

            def body(on):
                on(1, gate_values)
                on(0, rotate, 0, 1)
                on(0, rotate, 0, 0)
                on(1, weigh_gram, 0)
                on(3, shift_mix)
                on(4, short_filter)
                on(1, take_y, 0)
                on(0, rotate, 1, 1)
                on(3, residual2)
                on(1, weigh_gram, 1)
                on(3, carry_up)
                on(3, lambda j: normalised(j, x2[:, :], 2))
                on(2, residual1)
                on(0, rotate, 1, 0)
                on(1, carry_state)
                on(1, take_y, 1)
                on(2, lambda j: normalised(j, x1[:, :], 1))
            rounds(dve, body)


def long_convolution(nc, ctx, t):
    sb = lambda name, shape, dt=F32: ctx.enter_context(nc.sbuf_tensor(name, shape, dt))
    sem = lambda name: ctx.enter_context(nc.semaphore(name))
    U, Q, SLOTS = 4, 4, 8
    ident = t["ident"]
    skip = sb("skip", [128, DIM])
    HALF, AHEAD = TOK // 2, 2
    toep = [sb(f"toep{u}", [128, SEQ + HALF]) for u in range(SLOTS)]
    PARTS = {"dve": (0, 1152), "act": (1152, SEQ)}
    vt = [sb(f"vt{p}", [128, U, TOK]) for p in range(Q)]
    x0t = [sb(f"x0t{p}", [128, U, TOK]) for p in range(Q)]
    sig = [sb(f"sig{p}", [128, TILES]) for p in range(2)]
    skipped = [sb(f"skipped{p}", [128, TOK]) for p in range(2)]
    ys = [sb(f"ys{p}", [128, TILES]) for p in range(2)]
    yv = [sb(f"yv{p}", [128, U, TOK]) for p in range(Q)]
    pst = lambda name: ctx.enter_context(nc.psum_tensor(name, [128, 512], F32))
    p_sig, p_y, p_back = [pst(f"p_sig{p}") for p in range(2)], [pst(f"p_yc{p}") for p in range(2)], [pst(f"p_back{p}") for p in range(2)]
    skip_in = sem("skip_in")
    toep_in = [sem(f"toep_in{u}") for u in range(SLOTS)]
    quad_in, yv_out = [sem(f"quad_in{p}") for p in range(Q)], [sem(f"yv_out{p}") for p in range(Q)]
    sig_over, sig_ready, conv_ready, ys_ready, back_ready, yv_ready = (
        sem("sig_over"), sem("sig_ready"), sem("conv_ready"), sem("ys_ready"), sem("back_ready"), sem("yv_ready"))
    upper_by = {eng: sem(f"upper_by_{eng}") for eng in PARTS}

    def copy_upper(eng, name, copy, it, place):
        slot, (a, b) = place % SLOTS, PARTS[name]
        eng.wait_ge(toep_in[slot], 16 * (Q * U // SLOTS * it + place // SLOTS) + 16)
        copy(toep[slot][HALF:, a:b], toep[slot][0:HALF, a + HALF:b + HALF]).then_inc(upper_by[name], 1)

    by_seq = lambda ap: ap.rearrange("p (b c) -> p b c", b=BATCH)
    ROW = TOK - 1 + SEQ
    ITERS = DIM // (Q * U)
    taps = t["taps_dram"].rearrange("d n -> (d n)")

    with nc.Block() as block:
        @block.sync
        def _(sp):
            at = lambda n: n if isinstance(n, int) else sp.snap(n)
            sp.dma_start(skip[:, :], t["filt_bias"].partition_broadcast(128)).then_inc(skip_in, 16)

            def quad(it, q):
                n0 = Q * U * it + U * q
                offs = [at((n0 + u) * ROW) for u in range(U)]
                frees = [at(n0 + u - SLOTS + 1) for u in range(U)]
                for u in range(U):
                    wait(sp, conv_ready, frees[u])
                    src = taps[bass.ds(offs[u], ROW)]
                    rows = bass.AP(src.tensor, src.offset, [[1, HALF], [1, SEQ + HALF]])
                    slot = (U * q + u) % SLOTS
                    sp.dma_start(toep[slot][0:HALF, :], rows).then_inc(toep_in[slot], 16)
            for q in range(Q):
                quad(0, q)
            with sp.Fori(1, ITERS) as it:
                for q in range(Q):
                    quad(it, q)

        @block.scalar
        def _(act):
            at = lambda n: n if isinstance(n, int) else act.snap(n)
            flat = {n: t[n].rearrange("c t n -> (c t n)") for n in ("vxT_dram", "x0T_dram", "yT_dram")}
            QUAD = U * TILES * TOK
            rows = lambda name, off: flat[name][bass.ds(off, QUAD)].rearrange("(u t n) -> t u n", u=U, t=TILES)

            def fetch(off, q, frees):
                wait(act, yv_ready, frees)
                act.dma_start(vt[q][:, :, :], rows("vxT_dram", off)).then_inc(quad_in[q], 16)
                act.dma_start(x0t[q][:, :, :], rows("x0T_dram", off)).then_inc(quad_in[q], 16)

            def store(off, q, done):
                wait(act, yv_ready, done)
                act.dma_start(rows("yT_dram", off), yv[q][:, :, :]).then_inc(yv_out[q], 16)

            def copy_signal(n, p):
                act.wait_ge(sig_over, n + 1)
                wait(act, conv_ready, n - 1)
                nc.scalar.copy(sig[p][:, :], p_sig[p][:, 0:TILES]).then_inc(sig_ready, 1)

            def copy_sums(n, p):
                wait(act, conv_ready, n + 1)
                wait(act, back_ready, n - 1)
                nc.scalar.copy(ys[p][:, :], p_y[p][:, 0:TILES]).then_inc(ys_ready, 1)

            def body(it, first=False, last=False):
                for q in range(Q):
                    for u in range(U):
                        n = Q * U * it + U * q + u
                        copy_signal(n, u % 2)
                        place = U * q + u + AHEAD
                        if not (last and place >= Q * U):
                            copy_upper(act, "act", nc.scalar.copy, it, place)
                        if not (first and q == 0 and u == 0):
                            copy_sums(n - 1, (u - 1) % 2)
                        if u == 2 and not (first and q == 0):
                            off, off_next, done = at((Q * it + q - 1) * QUAD), at((Q * it + q + Q - 1) * QUAD), at((Q * it + q) * U)
                            slot = (q - 1) % Q
                            store(off, slot, done)
                            if not (last and q > 0):
                                fetch(off_next, slot, done)
            for q in range(Q):
                fetch(q * QUAD, q, 0)
            for place in range(AHEAD):
                copy_upper(act, "act", nc.scalar.copy, 0, place)
            body(0, first=True)
            with act.Fori(1, ITERS - 1) as it:
                body(it)
            body(ITERS - 1, last=True)
            copy_sums(DIM - 1, 1)
            store((Q * ITERS - 1) * QUAD, Q - 1, DIM)
            for p in range(Q):
                act.wait_ge(yv_out[p], 16 * ITERS)

        @block.tensor
        def _(pe):
            mm, tp = nc.tensor.matmul, nc.tensor.transpose

            def signal_over(it, q, u):
                n = Q * U * it + U * q + u
                if u == 0:
                    pe.wait_ge(quad_in[q], 32 * it + 32)
                wait(pe, sig_ready, n - 1)
                tp(p_sig[u % 2][:, 0:TILES], vt[q][:, u, :], ident[:, :]).then_inc(sig_over, 1)

            def convolve(it, q, u):
                n = Q * U * it + U * q + u
                for by in upper_by.values():
                    pe.wait_ge(by, n + 1)
                pe.wait_ge(sig_ready, n + 1)
                wait(pe, ys_ready, n - 1)
                p = u % 2
                for lag in range(CHUNKS):
                    last = mm(by_seq(p_y[p][:, 0:TILES])[:, :, lag:], toep[(U * q + u) % SLOTS][:, lag * TOK:(lag + 1) * TOK],
                              by_seq(sig[p][:, :])[:, :, 0:CHUNKS - lag], start=(lag == 0), stop=(lag == CHUNKS - 1))
                last.then_inc(conv_ready, 1)

            def back_over(it, q, u):
                n = Q * U * it + U * q + u
                pe.wait_ge(ys_ready, n + 1)
                wait(pe, yv_ready, n - 1)
                tp(p_back[u % 2][:, 0:TOK], ys[u % 2][:, :], ident[:, :]).then_inc(back_ready, 1)

            def body(it, first=False):
                for q in range(Q):
                    for u in range(U):
                        nxt = (it, q, u + 1) if u + 1 < U else (it, q + 1, 0) if q + 1 < Q else (it + 1, 0, 0)
                        prev = (it, q, u - 1) if u else (it, q - 1, U - 1) if q else (it - 1, Q - 1, U - 1)
                        if not (first == "last" and q == Q - 1 and u == U - 1):
                            signal_over(*nxt)
                        convolve(it, q, u)
                        if not (first is True and q == 0 and u == 0):
                            back_over(*prev)
            signal_over(0, 0, 0)
            body(0, first=True)
            with pe.Fori(1, ITERS - 1) as it:
                body(it)
            body(ITERS - 1, first="last")
            back_over(ITERS - 1, Q - 1, U - 1)

        @block.vector
        def _(dve):
            v_ = nc.vector

            def skip_and_gate(it, q, u):
                n = Q * U * it + U * q + u
                channel = at_n(n)
                if u == 0:
                    dve.wait_ge(quad_in[q], 32 * it + 32)
                    wait(dve, yv_out[q], 16 * it)
                dve.wait_ge(back_ready, n + 1)
                v_.scalar_tensor_tensor(out=skipped[u % 2][:, :], in0=vt[q][:, u, ::-1], scalar=skip[:, bass.ds(channel, 1)],
                                        in1=p_back[u % 2][:, 0:TOK], op0=ALU.mult, op1=ALU.add)
                dve.drain()
                v_.tensor_tensor(yv[q][:, u, :], skipped[u % 2][:, :], x0t[q][:, u, :], ALU.mult).then_inc(yv_ready, 1)

            at_n = lambda n: n if isinstance(n, int) else dve.snap(n)
            dve.wait_ge(skip_in, 16)

            def body(it, last=False):
                for q in range(Q):
                    for u in range(U):
                        place = U * q + u + AHEAD
                        if not (last and place >= Q * U):
                            copy_upper(dve, "dve", nc.vector.tensor_copy, it, place)
                        skip_and_gate(it, q, u)
            for place in range(AHEAD):
                copy_upper(dve, "dve", nc.vector.tensor_copy, 0, place)
            body(0)
            with dve.Fori(1, ITERS - 1) as it:
                body(it)
            body(ITERS - 1, last=True)


def project_and_second_ffn(nc, ctx, t):
    sb = lambda name, shape, dt=F32: ctx.enter_context(nc.sbuf_tensor(name, shape, dt))
    two = lambda name, shape: [sb(f"{name}_{p}", shape) for p in range(2)]
    names = ("weights2_in setup2 bias2 project2 add2 rstd2nd norm2nd xn2nd_over copy2nd_xT first_column difference mix2nd "
             "receptance_key2 r_and_k2 value2 output2").split()
    s = {n: ctx.enter_context(nc.semaphore(n)) for n in names}
    R, SLOTS = 8, 4
    load_in = [ctx.enter_context(nc.semaphore(f"load{u}")) for u in range(SLOTS)]
    stored = [ctx.enter_context(nc.semaphore(f"stored{u}")) for u in range(SLOTS)]
    ident = t["ident"]
    w_r, w_k, w_v, mu = t["w_r_sb"], t["w_k_sb"], t["w_v_sb"], t["mu_sb"]
    out_w, out_b = sb("out_w", [128, KT, DIM]), sb("out_b", [128, DIM])
    keep = sb("keep3", [128, TILES])
    yv = [sb(f"yvT{u}", [128, KT, TOK]) for u in range(SLOTS)]
    x3 = [sb(f"x3_{u}", [128, DIM]) for u in range(R)]
    out = [sb(f"out3_{u}", [128, DIM]) for u in range(SLOTS)]
    stats, mean_var, var_eps, rstd = sb("stats3", [128, 6]), two("mean_var3", [128, 2]), two("var_eps3", [128, 1]), two("rstd3", [128, 1])
    xn, xT, dx = two("xn3", [128, DIM]), two("xT3", [128, KT, TOK + 1]), two("dx3", [128, KT, TOK])
    x_r, x_k, tanh_r, k_sq = two("x_r3", [128, KT, TOK]), two("x_k3", [128, KT, TOK]), two("tanh3", [128, DIM]), two("k_sq3", [128, KT, TOK])
    k_pos, gated = two("k_pos3", [128, 256]), two("gated3", [128, DIM])
    bank = [ctx.enter_context(nc.psum_tensor(f"bank3_{k}", [128, 512], F32)) for k in range(8)]
    p_proj, p_tr, p_rk, p_v = bank[0:2], bank[2:4], bank[4:6], bank[6:8]

    def wait_for(eng, step, i):
        wait(eng, s[step], i + 1)

    def in_slot(sem, each, g, v, back=0):
        return sem[v % SLOTS], each * (R // SLOTS * g + (v - back) // SLOTS + 1)

    LAGS = 6

    def rounds(eng, body):
        def some(g, u):
            def on(lag, step):
                if 0 <= R * g + u - lag < TILES:
                    step(g, u - lag)
            return on
        for u in range(R):
            body(some(0, u))
        with eng.Fori(1, TILES // R) as g:
            for u in range(R):
                body(lambda lag, step: step(g, u - lag))
        for u in range(LAGS):
            body(some(TILES // R, u))

    with nc.Block() as block:
        @block.sync
        def _(sp):
            at = lambda n: n if isinstance(n, int) else sp.snap(n)
            yflat, xflat, oflat = (t["yT_dram"].rearrange("(k p) t n -> p k (t n)", p=128), t["x2_dram"].rearrange("r c -> (r c)"),
                                   t["out"].rearrange("r c -> (r c)"))
            sp.dma_start(out_w[:, :, :], t["out_w"].rearrange("(k p) n -> p k n", p=128)).then_inc(s["weights2_in"], 16)
            sp.dma_start(out_b[:, :], t["out_b"].partition_broadcast(128)).then_inc(s["weights2_in"], 16)

            def load(g, v):
                i = R * g + v
                tok_at, block_at, slot_free = at(i * TOK), at(i * (TOK * DIM)), at(i - SLOTS + 1)
                wait(sp, s["project2"], slot_free)
                wait(sp, s["bias2"], slot_free)
                sp.dma_start(yv[v % SLOTS][:, :, :], yflat[:, :, bass.ds(tok_at, TOK)]).then_inc(load_in[v % SLOTS], 16)
                sp.dma_start(x3[v % R][:, :], xflat[bass.ds(block_at, TOK * DIM)].rearrange("(p c) -> p c", p=TOK)).then_inc(load_in[v % SLOTS], 16)

            def store(g, v):
                i = R * g + v
                block_at, done = at(i * (TOK * DIM)), at(i + 1)
                wait(sp, s["output2"], done)
                sp.dma_start(oflat[bass.ds(block_at, TOK * DIM)].rearrange("(p c) -> p c", p=TOK), out[v % SLOTS][:, :]).then_inc(stored[v % SLOTS], 16)

            def body(on):
                on(0, load)
                on(6, store)
            rounds(sp, body)
            for u in range(SLOTS):
                sp.wait_ge(stored[u], 16 * TILES // SLOTS)

        @block.gpsimd
        def _(pool):
            g_ = nc.gpsimd
            g_.memset(xT[0][:, :, :], 0.0)
            g_.memset(xT[1][:, :, :], 0.0)
            g_.memset(keep[:, :], 1.0)
            pool.drain()
            g_.memset(keep[:, :].rearrange("p (b c) -> p b c", b=BATCH)[:, :, 0], 0.0)
            pool.drain().then_inc(s["setup2"], 1)
            pool.wait_ge(s["weights2_in"], 32)

            def add_bias(g, v):
                wait(pool, *in_slot(load_in, 32, g, v))
                g_.tensor_tensor(x3[v % R][:, :], x3[v % R][:, :], out_b[:, :], ALU.add).then_inc(s["bias2"], 1)

            def layer_rstd(g, v):
                i, p = R * g + v, v % 2
                wait_for(pool, "add2", i)
                wait_for(pool, "norm2nd", i - 2)
                g_.tensor_tensor(rstd[p][:, :], var_eps[p][:, :], t["minus_half"][:, 0:1], ALU.pow).then_inc(s["rstd2nd"], 1)

            def first_column(g, v):
                i, p = R * g + v, v % 2
                wait_for(pool, "copy2nd_xT", i - 1)
                wait_for(pool, "mix2nd", i - 2)
                before = keep[:, bass.ds(i, 1)].broadcast_to([128, KT])
                g_.tensor_tensor(xT[p][:, :, 0], xT[1 - p][:, :, TOK], before, ALU.mult).then_inc(s["first_column"], 1)

            def difference(g, v):
                i, p = R * g + v, v % 2
                pool.drain()
                wait_for(pool, "copy2nd_xT", i)
                wait_for(pool, "mix2nd", i - 2)
                g_.tensor_tensor(dx[p][:, :, :], xT[p][:, :, 1:TOK + 1], xT[p][:, :, 0:TOK], ALU.subtract).then_inc(s["difference"], 1)

            def body(on):
                on(0, add_bias)
                on(2, difference)
                on(0, layer_rstd)
                on(1, first_column)
            rounds(pool, body)

        @block.scalar
        def _(act):
            s_ = nc.scalar

            def copy_xT(g, v):
                i, p = R * g + v, v % 2
                wait_for(act, "xn2nd_over", i)
                wait_for(act, "mix2nd", i - 2)
                wait_for(act, "difference", i - 2)
                wait_for(act, "first_column", i - 1)
                s_.copy(xT[p][:, :, 1:TOK + 1], p_tr[p][:, 0:DIM].rearrange("p (k n) -> p k n", k=KT)).then_inc(s["copy2nd_xT"], 1)

            def r_and_k(g, v):
                i, p = R * g + v, v % 2
                wait_for(act, "receptance_key2", i)
                wait_for(act, "value2", i - 2)
                wait_for(act, "output2", i - 2)
                s_.activation(k_pos[p][:, :], p_rk[p][:, DIM:512], ACT.Relu)
                act.drain()
                s_.activation(k_sq[p][:, :, :], k_pos[p][:, :].rearrange("p (k n) -> p k n", k=KT), ACT.Square)
                s_.activation(tanh_r[p][:, :], p_rk[p][:, 0:DIM], ACT.Tanh, scale=0.5).then_inc(s["r_and_k2"], 1)

            def body(on):
                on(3, r_and_k)
                on(1, copy_xT)
            rounds(act, body)

        @block.tensor
        def _(pe):
            mm, tp = nc.tensor.matmul, nc.tensor.transpose
            pe.wait_ge(s["weights2_in"], 32)

            def project(g, v):
                i, p = R * g + v, v % 2
                wait(pe, *in_slot(load_in, 32, g, v))
                wait_for(pe, "add2", i - 2)
                for k in range(KT):
                    last = mm(p_proj[p][:, 0:DIM], yv[v % SLOTS][:, k, :], out_w[:, k, :], start=(k == 0), stop=(k == KT - 1))
                last.then_inc(s["project2"], 1)

            def xn_over(g, v):
                i, p = R * g + v, v % 2
                wait_for(pe, "norm2nd", i)
                wait_for(pe, "copy2nd_xT", i - 2)
                for k in range(KT):
                    last = tp(p_tr[p][:, k * TOK:(k + 1) * TOK], xn[p][:, k * 128:(k + 1) * 128], ident[:, :])
                last.then_inc(s["xn2nd_over"], 1)

            def receptance_key(g, v):
                i, p = R * g + v, v % 2
                wait_for(pe, "mix2nd", i)
                wait_for(pe, "r_and_k2", i - 2)
                for e in range(KT):
                    for k in range(KT):
                        mm(p_rk[p][:, DIM + e * TOK:DIM + (e + 1) * TOK], w_k[:, k, e * 128:(e + 1) * 128], x_k[p][:, k, :],
                           start=(k == 0), stop=(k == KT - 1))
                for k in range(KT):
                    last = mm(p_rk[p][:, 0:DIM], x_r[p][:, k, :], w_r[:, k, :], start=(k == 0), stop=(k == KT - 1))
                last.then_inc(s["receptance_key2"], 1)

            def value(g, v):
                i, p = R * g + v, v % 2
                wait_for(pe, "r_and_k2", i)
                wait_for(pe, "output2", i - 2)
                for k in range(KT):
                    last = mm(p_v[p][:, 0:DIM], k_sq[p][:, k, :], w_v[:, k, :], start=(k == 0), stop=(k == KT - 1))
                last.then_inc(s["value2"], 1)

            def body(on):
                on(0, project)
                on(3, receptance_key)
                on(4, value)
                on(1, xn_over)
            rounds(pe, body)

        @block.vector
        def _(dve):
            v_ = nc.vector
            dve.wait_ge(s["setup2"], 1)

            def add_and_stats(g, v):
                i, p = R * g + v, v % 2
                wait_for(dve, "project2", i)
                wait_for(dve, "bias2", i)
                v_.tensor_tensor(x3[v % R][:, :], p_proj[p][:, 0:DIM], x3[v % R][:, :], ALU.add)
                dve.drain()
                v_.bn_stats(stats[:, :], x3[v % R][:, :])
                dve.drain()
                v_.bn_aggr(mean_var[p][:, :], stats[:, :])
                dve.drain()
                wait_for(dve, "rstd2nd", i - 2)
                v_.tensor_scalar(var_eps[p][:, :], mean_var[p][:, 1:2], LN_EPS, None, ALU.add).then_inc(s["add2"], 1)

            def normalise(g, v):
                i, p = R * g + v, v % 2
                wait_for(dve, "rstd2nd", i)
                wait_for(dve, "xn2nd_over", i - 2)
                v_.tensor_scalar(xn[p][:, :], x3[v % R][:, :], mean_var[p][:, 0:1], rstd[p][:, :], ALU.subtract, ALU.mult).then_inc(s["norm2nd"], 1)

            def shift_mix(g, v):
                i, p = R * g + v, v % 2
                wait_for(dve, "difference", i)
                wait_for(dve, "receptance_key2", i - 2)
                for k in range(KT):
                    for which, dst in enumerate((x_r[p], x_k[p])):
                        last = v_.scalar_tensor_tensor(out=dst[:, k, :], in0=dx[p][:, k, :], scalar=mu[:, which, k:k + 1],
                                                       in1=xT[p][:, k, 0:TOK], op0=ALU.mult, op1=ALU.add)
                last.then_inc(s["mix2nd"], 1)

            def output(g, v):
                i, p = R * g + v, v % 2
                wait_for(dve, "value2", i)
                wait_for(dve, "r_and_k2", i)
                v_.scalar_tensor_tensor(out=gated[p][:, :], in0=tanh_r[p][:, :], scalar=1.0, in1=p_v[p][:, 0:DIM], op0=ALU.add, op1=ALU.mult)
                dve.drain()
                wait(dve, *in_slot(stored, 16, g, v, SLOTS))
                v_.scalar_tensor_tensor(out=out[v % SLOTS][:, :], in0=gated[p][:, :], scalar=0.5, in1=x3[v % R][:, :], op0=ALU.mult, op1=ALU.add).then_inc(s["output2"], 1)

            def body(on):
                on(0, add_and_stats)
                on(2, shift_mix)
                on(4, output)
                on(0, normalise)
            rounds(dve, body)


def build(nc, t):
    with ExitStack() as ctx:
        const = lambda name, dt=F32: ctx.enter_context(nc.sbuf_tensor(name, [128, 128], dt))
        for n in ("ident", "upto", "after", "ones", "nxt", "wrap"):
            t[n] = const(n)
        t["mask"], t["ident_b"] = const("mask", BF16), const("ident_b", BF16)
        t["minus_half"] = ctx.enter_context(nc.sbuf_tensor("minus_half", [128, 4], F32))
        t["xnT_dram"] = nc.dram_tensor("xnT_dram", (TILES, 128, KT, TOK), F32, kind="Internal").ap()
        t["params_dram"] = nc.dram_tensor("params_dram", (128, TILES, P_ALL), F32, kind="Internal").ap()
        t["taps_dram"] = nc.dram_tensor("taps_dram", (DIM, TOK - 1 + SEQ), F32, kind="Internal").ap()
        with ExitStack() as early:
            t["scal"] = early.enter_context(nc.sbuf_tensor("scal", [128, TILES, 24], F32))
            with ExitStack() as c:
                normalise_tokens(nc, c, t)
            with ExitStack() as c:
                scan_parameters(nc, c, t)
        with ExitStack() as c:
            long_filter(nc, c, t)
        t["x2_dram"] = nc.dram_tensor("x2_dram", (TILES * TOK, DIM), F32, kind="Internal").ap()
        for n in ("x0T_dram", "vxT_dram", "yT_dram"):
            t[n] = nc.dram_tensor(n, (DIM, TILES, TOK), F32, kind="Internal").ap()
        keepers = lambda name, shape: ctx.enter_context(nc.sbuf_tensor(name, shape, F32))
        for n in ("w_r", "w_k", "w_v"):
            t[n + "_sb"] = keepers(n + "_sb", [128, KT, DIM])
        t["mu_sb"] = keepers("mu_sb", [128, 2, KT])
        with ExitStack() as c:
            mixer_and_first_ffn(nc, c, t)
        with ExitStack() as c:
            long_convolution(nc, c, t)
        with ExitStack() as c:
            project_and_second_ffn(nc, c, t)


_OWN = ("x", "w_scal", "dt_bias", "A_log", "pos", "mlp_w1", "mlp_w2", "mlp_w3", "mlp_wo", "freq_b", "decay",
        "w_u", "w_bc", "w_out", "rms_w", "w_r", "w_k", "w_v", "mu", "in_w", "in_b", "short", "filt_bias", "out_w", "out_b")


def kernel(**inputs):
    import numpy as _np
    import concourse.bacc as _bacc
    from concourse import mybir as _mybir
    from concourse.bass_utils import run_bass_kernel_spmd as _run
    nc = _bacc.Bacc("TRN2", target_bir_lowering=False, num_devices=1)
    a = {k.replace("L0_", "").replace("attn_", ""): _np.asarray(v) for k, v in inputs.items()}
    f32 = _np.float32
    order = (_np.arange(2 * HEADS)[:, None] * STATE
             + _np.concatenate([_np.arange(0, STATE, 2), _np.arange(1, STATE, 2)])[None]).reshape(-1)
    where = _np.linspace(0.0, 1.0, SEQ, dtype=f32)
    turn = (2.0 * _np.pi * _np.linspace(0.0, SEQ - 1.0, SEQ) / SEQ).astype(f32) * f32(1e-4)
    pos = _np.stack([where, _np.cos(turn), -_np.sin(turn)]).astype(f32)
    deltas = _np.linspace(_np.log(0.01) / 1.5, _np.log(0.01) / 0.3, DIM).astype(f32)
    decay = _np.exp(-where[None, :] * _np.abs(deltas)[:, None]).astype(f32)
    arrays = {
        "x": a["a_x"].reshape(TILES * TOK, DIM),
        "w_scal": a["a_sel_proj_w"][2 * HEADS * STATE:].T,
        "dt_bias": a["a_dt_bias"], "A_log": a["a_A_log"],
        "pos": pos, "mlp_w1": a["b_mlp_w1"], "mlp_w2": a["b_mlp_w2"], "mlp_w3": a["b_mlp_w3"], "mlp_wo": a["b_mlp_wo"],
        "freq_b": _np.stack([a["b_freq"][0], a["b_mlp_b1"], a["b_mlp_b2"], a["b_mlp_b3"]], axis=1),
        "decay": decay,
        "w_u": a["a_in_proj_w"].T,
        "w_bc": a["a_sel_proj_w"][order].T,
        "w_out": a["a_out_proj_w"].T, "rms_w": a["a_rms_weight"].reshape(-1, 128).T,
        "w_r": a["ffn_W_r"].T, "w_k": a["ffn_W_k"].T, "w_v": a["ffn_W_v"].T,
        "mu": _np.stack([a["ffn_mu_r"].reshape(KT, 128).T, a["ffn_mu_k"].reshape(KT, 128).T], axis=1),
        "in_w": a["b_in_w"], "in_b": a["b_in_b"].reshape(-1, 128).T,
        "short": _np.concatenate([a["b_short_w"].reshape(6, 128, 3), a["b_short_b"].reshape(6, 128, 1)], axis=2).transpose(1, 0, 2),
        "filt_bias": a["b_filt_bias"], "out_w": a["b_out_w"], "out_b": a["b_out_b"],
    }
    arrays = {n: _np.ascontiguousarray(arrays[n]) for n in _OWN}
    t = {n: nc.dram_tensor("arg_" + n, v.shape, _mybir.dt.from_np(v.dtype), kind="ExternalInput").ap() for n, v in arrays.items()}
    t["out"] = nc.dram_tensor("out", (TILES * TOK, DIM), F32, kind="ExternalOutput").ap()
    build(nc, t)
    r = _run(nc, [{"arg_" + n: v for n, v in arrays.items()}], core_ids=[0])
    return r.results[0]["out"].reshape(BATCH, SEQ, DIM)
```
